# Optimizing a Trainium2 kernel written in Bass

```python
import numpy as np
import jax
import jax.numpy as jnp

def _softmax(x, axis=-1):
    return jax.nn.softmax(x, axis=axis)

def _gelu(x):
    return jax.nn.gelu(x, approximate=True)

def _silu(x):
    return jax.nn.silu(x)

def _sigmoid(x):
    return jax.nn.sigmoid(x)

def _layernorm(x, axis=-1, eps=1e-05):
    m = jnp.mean(x, axis=axis, keepdims=True)
    v = jnp.var(x, axis=axis, keepdims=True)
    return (x - m) / jnp.sqrt(v + eps)

def _scatter_add(tgt, idx, src, axis=0):
    return tgt.at[idx].add(src)

def _segment_sum(src, seg, n):
    return jax.ops.segment_sum(src, seg, n)
kernel_name = 'mk_decoder_postln_d1_seqx_r8_7bc3a0'

def setup_inputs(seed: int=0):
    np.random.seed(seed)
    _w = jnp.asarray

    def _rec_inputs():
        import jax
        import jax.numpy as jnp
        _rk = jax.random.key(seed)
        x = -0.0003929 + 0.9999 * jax.random.normal(jax.random.fold_in(_rk, 1), (16, 64, 512), jnp.float32)
        _lenS = 64 - jax.random.randint(jax.random.fold_in(_rk, 7), (16,), 0, max(1, 64 // 4) + 1, jnp.int32)
        _lenS2 = 64 - jax.random.randint(jax.random.fold_in(_rk, 8), (16,), 0, max(1, 64 // 4) + 1, jnp.int32)
        _ctx_4096P = jax.random.normal(jax.random.fold_in(_rk, 11), (16, 16, 512), jnp.float32)
        _ctx_4096c = jax.random.dirichlet(jax.random.fold_in(_rk, 511), 0.3 * jnp.ones((16,), jnp.float32), (16, 64))
        _ctx_4096t = jnp.einsum('bsk,bkd->bsd', _ctx_4096c, _ctx_4096P)
        _ctx_4096t = _ctx_4096t * jax.lax.rsqrt(jnp.mean(jnp.square(_ctx_4096t)) + 1e-12) * 0.953939
        ctx_4096 = 2.81802e-05 + 1.00001 * (_ctx_4096t + 0.3 * jax.random.normal(jax.random.fold_in(_rk, 611), (16, 64, 512), jnp.float32))
        return (x, ctx_4096)
    x, ctx_4096 = _rec_inputs()

    def _L0_attn_setup():
        import jax, jax.numpy as jnp
        import numpy as np
        H = 512
        D_IN = 1024
        N = 16
        K = 4
        R = 32
        EPS = 1e-06

        def rms_forward(x, eps=EPS):
            xf = x.astype(jnp.float32)
            var = jnp.mean(xf * xf, axis=-1, keepdims=True)
            return (xf * jax.lax.rsqrt(var + eps)).astype(x.dtype)
        key = jax.random.key(seed)
        ks = jax.random.split(key, 10)
        s = 0.02
        hidden_states = jax.random.normal(ks[0], (2, 128, H), dtype=jnp.float32)
        W_in = jax.random.normal(ks[1], (2 * D_IN, H), dtype=jnp.float32) * s
        conv_w = jax.random.normal(ks[2], (D_IN, K), dtype=jnp.float32) * 0.2
        conv_b = jax.random.normal(ks[3], (D_IN,), dtype=jnp.float32) * 0.02
        W_x = jax.random.normal(ks[4], (R + 2 * N, D_IN), dtype=jnp.float32) * s
        W_dt = jax.random.normal(ks[5], (D_IN, R), dtype=jnp.float32) * s
        b_dt = jax.random.normal(ks[6], (D_IN,), dtype=jnp.float32) * 0.02
        A_log = jnp.log(jnp.broadcast_to(jnp.arange(1, N + 1, dtype=jnp.float32)[None, :], (D_IN, N)))
        D = jnp.ones((D_IN,), dtype=jnp.float32)
        W_out = jax.random.normal(ks[7], (H, D_IN), dtype=jnp.float32) * s
        return {'hidden_states': hidden_states, 'W_in': W_in, 'conv_w': conv_w, 'conv_b': conv_b, 'W_x': W_x, 'W_dt': W_dt, 'b_dt': b_dt, 'A_log': A_log, 'D': D, 'W_out': W_out}
    _L0_attn_all = _L0_attn_setup()
    _L0_attn_in = {k: v for k, v in _L0_attn_all.items() if k in ('W_in', 'conv_w', 'conv_b', 'W_x', 'W_dt', 'b_dt', 'A_log', 'D', 'W_out')}
    del _L0_attn_all

    def _L0_xattn_setup():
        import jax, jax.numpy as jnp
        import numpy as np
        DIM = 64
        HEADS = 8
        DIM_HEAD = 64
        HIDDEN = HEADS * DIM_HEAD
        SCALE = DIM_HEAD ** (-0.5)
        key = jax.random.key(seed)
        ks = jax.random.split(key, 9)
        b, n = (8, 512)
        std = 1.0 / np.sqrt(DIM)
        return {'q': jax.random.normal(ks[0], (b, DIM, n), jnp.float32), 'k': jax.random.normal(ks[1], (b, DIM, n), jnp.float32), 'v': jax.random.normal(ks[2], (b, DIM, n), jnp.float32), 'Wq': jax.random.normal(ks[3], (HIDDEN, DIM), jnp.float32) * std, 'Wk': jax.random.normal(ks[4], (HIDDEN, DIM), jnp.float32) * std, 'Wv': jax.random.normal(ks[5], (HIDDEN, DIM), jnp.float32) * std, 'Wo': jax.random.normal(ks[6], (DIM, HIDDEN), jnp.float32) * (1.0 / np.sqrt(HIDDEN)), 'bo': jax.random.normal(ks[7], (DIM,), jnp.float32) * 0.01, 'g': jnp.ones((1, DIM, 1), jnp.float32)}
    _L0_xattn_all = _L0_xattn_setup()
    _L0_xattn_in = {k: v for k, v in _L0_xattn_all.items() if k in ('Wq', 'Wk', 'Wv', 'Wo', 'bo', 'g')}
    del _L0_xattn_all

    def _L0_ffn_setup():
        import jax, jax.numpy as jnp
        import numpy as np
        H, FF = (512, 1792)
        B, S = (4, 256)
        key = jax.random.key(seed)
        ks = jax.random.split(key, 7)
        x = jax.random.normal(ks[0], (B, S, H), dtype=jnp.float32)
        gate_t = jax.random.randint(ks[1], (FF, H), -1, 2, dtype=jnp.int32)
        up_t = jax.random.randint(ks[2], (FF, H), -1, 2, dtype=jnp.int32)
        down_t = jax.random.randint(ks[3], (H, FF), -1, 2, dtype=jnp.int32)
        gate_s = jax.random.uniform(ks[4], (FF,), jnp.float32, 0.01, 0.1)
        up_s = jax.random.uniform(ks[5], (FF,), jnp.float32, 0.01, 0.1)
        down_s = jax.random.uniform(ks[6], (H,), jnp.float32, 0.01, 0.1)
        return {'x': x, 'gate_t': gate_t, 'up_t': up_t, 'down_t': down_t, 'gate_s': gate_s, 'up_s': up_s, 'down_s': down_s}
    _L0_ffn_all = _L0_ffn_setup()
    _L0_ffn_in = {k: v for k, v in _L0_ffn_all.items() if k in ('gate_t', 'up_t', 'down_t', 'gate_s', 'up_s', 'down_s')}
    del _L0_ffn_all
    return {'x': x, 'ctx_4096': ctx_4096, 'L0_attn_W_in': _L0_attn_in['W_in'], 'L0_attn_conv_w': _L0_attn_in['conv_w'], 'L0_attn_conv_b': _L0_attn_in['conv_b'], 'L0_attn_W_x': _L0_attn_in['W_x'], 'L0_attn_W_dt': _L0_attn_in['W_dt'], 'L0_attn_b_dt': _L0_attn_in['b_dt'], 'L0_attn_A_log': _L0_attn_in['A_log'], 'L0_attn_D': _L0_attn_in['D'], 'L0_attn_W_out': _L0_attn_in['W_out'], 'L0_xattn_Wq': _L0_xattn_in['Wq'], 'L0_xattn_Wk': _L0_xattn_in['Wk'], 'L0_xattn_Wv': _L0_xattn_in['Wv'], 'L0_xattn_Wo': _L0_xattn_in['Wo'], 'L0_xattn_bo': _L0_xattn_in['bo'], 'L0_xattn_g': _L0_xattn_in['g'], 'L0_ffn_gate_t': _L0_ffn_in['gate_t'], 'L0_ffn_up_t': _L0_ffn_in['up_t'], 'L0_ffn_down_t': _L0_ffn_in['down_t'], 'L0_ffn_gate_s': _L0_ffn_in['gate_s'], 'L0_ffn_up_s': _L0_ffn_in['up_s'], 'L0_ffn_down_s': _L0_ffn_in['down_s']}

def reference(x, ctx_4096, L0_attn_W_in, L0_attn_conv_w, L0_attn_conv_b, L0_attn_W_x, L0_attn_W_dt, L0_attn_b_dt, L0_attn_A_log, L0_attn_D, L0_attn_W_out, L0_xattn_Wq, L0_xattn_Wk, L0_xattn_Wv, L0_xattn_Wo, L0_xattn_bo, L0_xattn_g, L0_ffn_gate_t, L0_ffn_up_t, L0_ffn_down_t, L0_ffn_gate_s, L0_ffn_up_s, L0_ffn_down_s):
    import jax
    import jax.numpy as jnp

    def _L0_attn_ref(hidden_states, W_in, conv_w, conv_b, W_x, W_dt, b_dt, A_log, D, W_out):
        import jax, jax.numpy as jnp
        import numpy as np
        H = 512
        D_IN = 1024
        N = 16
        K = 4
        R = 32
        EPS = 1e-06

        def rms_forward(x, eps=EPS):
            xf = x.astype(jnp.float32)
            var = jnp.mean(xf * xf, axis=-1, keepdims=True)
            return (xf * jax.lax.rsqrt(var + eps)).astype(x.dtype)
        b, L, _ = hidden_states.shape
        proj = hidden_states @ W_in.T
        x, gate = (proj[..., :D_IN], proj[..., D_IN:])
        xpad = jnp.pad(x, ((0, 0), (K - 1, 0), (0, 0)))
        xc = conv_b
        for j in range(K):
            xc = xc + conv_w[:, j] * xpad[:, j:j + L, :]
        x = jax.nn.silu(xc)
        ssm = x @ W_x.T
        ts, Bm, Cm = (ssm[..., :R], ssm[..., R:R + N], ssm[..., R + N:])
        ts = rms_forward(ts)
        Bm = rms_forward(Bm)
        Cm = rms_forward(Cm)
        dt = jax.nn.softplus(ts @ W_dt.T + b_dt)
        A = -jnp.exp(A_log.astype(jnp.float32))

        def step(state, inp):
            dt_t, B_t, C_t, u_t = inp
            dA = jnp.exp(dt_t[..., None] * A)
            state = state * dA + (dt_t * u_t)[..., None] * B_t[:, None, :]
            y = jnp.einsum('bdn,bn->bd', state, C_t)
            return (state, y)
        init = jnp.zeros((b, D_IN, N), dtype=jnp.float32)
        xs = (dt.transpose(1, 0, 2), Bm.transpose(1, 0, 2), Cm.transpose(1, 0, 2), x.transpose(1, 0, 2))
        _, ys = jax.lax.scan(step, init, xs)
        y = ys.transpose(1, 0, 2) + x * D
        y = y * jax.nn.silu(gate)
        return y @ W_out.T

    def _L0_xattn_ref(q, k, v, Wq, Wk, Wv, Wo, bo, g):
        import jax, jax.numpy as jnp
        import numpy as np
        DIM = 64
        HEADS = 8
        DIM_HEAD = 64
        HIDDEN = HEADS * DIM_HEAD
        SCALE = DIM_HEAD ** (-0.5)
        b = q.shape[0]
        qh = jnp.einsum('bcn,oc->bon', q, Wq).reshape(b, HEADS, DIM_HEAD, -1)
        kh = jnp.einsum('bcn,oc->bon', k, Wk).reshape(b, HEADS, DIM_HEAD, -1)
        vh = jnp.einsum('bcn,oc->bon', v, Wv).reshape(b, HEADS, DIM_HEAD, -1)
        qh = jax.nn.softmax(qh, axis=-2) * SCALE
        kh = jax.nn.softmax(kh, axis=-1)
        context = jnp.einsum('bhdn,bhen->bhde', kh, vh)
        out = jnp.einsum('bhde,bhdn->bhen', context, qh)
        out = out.reshape(b, HIDDEN, -1)
        out = jnp.einsum('bcn,oc->bon', out, Wo) + bo[None, :, None]
        norm = jnp.maximum(jnp.sqrt(jnp.sum(out * out, axis=1, keepdims=True)), 1e-12)
        return out / norm * g * np.sqrt(DIM)

    def _L0_ffn_ref(x, gate_t, up_t, down_t, gate_s, up_s, down_s):
        import jax, jax.numpy as jnp
        import numpy as np
        H, FF = (512, 1792)
        B, S = (4, 256)
        Bb, Ss, Hh = x.shape
        x_flat = x.reshape(Bb * Ss, Hh)
        gate_w = gate_t.astype(jnp.float32) * gate_s[:, None]
        up_w = up_t.astype(jnp.float32) * up_s[:, None]
        down_w = down_t.astype(jnp.float32) * down_s[:, None]
        gate_out = x_flat @ gate_w.T
        up_out = x_flat @ up_w.T
        hidden = jax.nn.silu(gate_out) * up_out
        out_flat = hidden @ down_w.T
        return out_flat.reshape(Bb, Ss, -1)
    x = _layernorm(x + _L0_attn_ref(x, L0_attn_W_in, L0_attn_conv_w, L0_attn_conv_b, L0_attn_W_x, L0_attn_W_dt, L0_attn_b_dt, L0_attn_A_log, L0_attn_D, L0_attn_W_out), axis=-1)
    x = _layernorm(x + _L0_xattn_ref(x, ctx_4096, ctx_4096, L0_xattn_Wq, L0_xattn_Wk, L0_xattn_Wv, L0_xattn_Wo, L0_xattn_bo, L0_xattn_g), axis=-1)
    x = _layernorm(x + _L0_ffn_ref(x, L0_ffn_gate_t, L0_ffn_up_t, L0_ffn_down_t, L0_ffn_gate_s, L0_ffn_up_s, L0_ffn_down_s), axis=-1)
    return x

_drawn_inputs = setup_inputs


def setup_inputs(seed=0):
    import zlib

    import numpy as np

    out = dict(_drawn_inputs(seed))
    spreads = {'L0_attn_D': (1.0, 0.6), 'L0_xattn_g': (1.0, 0.2)}
    factors = {'L0_attn_conv_b': 5.89,
     'L0_attn_W_dt': 8.0,
     'L0_attn_b_dt': 46.818,
     'L0_attn_A_log': 16.596}
    for name, (base, spread) in spreads.items():
        noise = np.random.default_rng([zlib.crc32(name.encode()), seed]).standard_normal(out[name].shape)
        drawn = base * np.exp(spread * noise) if base else spread * noise
        out[name] = jnp.asarray(drawn.astype(out[name].dtype))
    for name, factor in factors.items():
        out[name] = (out[name] * factor).astype(out[name].dtype)
    return out
```

```python
from contextlib import ExitStack

import numpy as np

import concourse.bass as bass
from concourse import mybir

F32 = mybir.dt.float32
F32R = mybir.dt.float32r
I32 = mybir.dt.int32
ALU = mybir.AluOpType
ACT = mybir.ActivationFunctionType
AX_X = mybir.AxisListType.X

P = 128
B, L, H = 16, 64, 512
PAIRS = B // 2
KC = H // P
DI, NS, RK = 1024, 16, 32
DC = DI // P
TAPS = 4
HEADS, DH = 8, 64
GN = 4
NG = NS // GN
GC = 4
NGC = DC // GC
ITEMS = NG * NGC
SCANS = ITEMS * GC
STEPS = SCANS + GC
FF = 1792
FC = FF // P
HALF = 512
TOK = B * L
TC = TOK // P
HALVES = TOK // HALF
WR = 2
LN_EPS, RMS_EPS = 1e-5, 1e-6
NORM_SCALE = 2.0 ** 20

FRONT = 16
RING = 8
ATT_B = 25
ATT = 2 * ATT_B + 1
ATT_FREE = (ATT_B + 1, ATT_B)


PRIMED = 1


def bank_of(n):
    return n % 2, n // 2


def decoder_kernel(nc, x_tok, x_t, ctx, ctx_t, w_in, conv_w, conv_b, w_x, w_dt, b_dt, a_log, d_skip, w_out,
                   wq, wk, wv, wo, bo, gain, gate_w, up_w, down_w, gate_s, up_s, down_s, out):
    x2_dram = nc.dram_tensor("x2_scratch", [PAIRS, P, H], F32).ap()
    with ExitStack() as whole:
        def sem(name):
            return whole.enter_context(nc.semaphore(name))

        def sb(name, shape, dt=F32, scope=whole):
            return scope.enter_context(nc.sbuf_tensor(name, shape, dt))

        front = [whole.enter_context(nc.psum_tensor(f"front{i}", [P, 512], F32)) for i in range(2)]
        drive = [whole.enter_context(nc.psum_tensor(f"drive{i}", [P, 512], F32)) for i in range(2)]
        turned = [whole.enter_context(nc.psum_tensor(f"turned{i}", [P, 512], F32)) for i in range(2)]
        att = [whole.enter_context(nc.psum_tensor(f"att{i}", [P, 512], F32)) for i in range(2)]

        ident = sb("ident", [P, P])
        eps_ln, eps_rms = sb("eps_ln", [P, 1]), sb("eps_rms", [P, 1])
        gs_sb, us_sb = sb("gs_sb", [P, FC]), sb("us_sb", [P, FC])

        loop_mem = whole.enter_context(ExitStack())

        def lb(name, shape, dt=F32):
            return sb(name, shape, dt, loop_mem)

        blocks = lb("blocks", [P, P])
        ones_r = lb("ones_r", [P, P], F32R)
        two_eyes = lb("two_eyes", [P, L])
        pick = lb("pick", [P, KC, P], F32R)
        cw, cb = lb("cw", [P, DC, TAPS]), lb("cb", [P, DC])
        bdt, dsk = lb("bdt", [P, DC]), lb("dsk", [P, DC])
        neg_a = lb("neg_a", [P, DC, NS])
        bo_sb, g8 = lb("bo_sb", [P, 1]), lb("g8", [P, 1])
        win = lb("win", [P, KC, 2 * DI])
        wx = lb("wx", [P, DC, 64])
        wdt = lb("wdt", [P, DI])
        wout = lb("wout", [P, DC, H])
        wq_hi, wq_lo = lb("wq_hi", [P, H], F32R), lb("wq_lo", [P, H], F32R)
        wk_hi, wk_lo = lb("wk_hi", [P, H], F32R), lb("wk_lo", [P, H], F32R)
        ucat = lb("ucat", [P, KC, P + 1])

        xt, xtok = lb("xt", [P, KC, P]), lb("xtok", [P, H])
        xs, sg = lb("xs", [P, DC, P]), lb("sg", [P, DC, P])
        ssm, ssm2 = lb("ssm", [P, P]), lb("ssm2", [P, 2, 2, L])
        tr, sq3 = lb("tr", [P, 3, 64]), lb("sq3", [P, 3, 64])
        rms = lb("rms", [P, 4])
        tsn, c_col = lb("tsn", [P, RK]), lb("c_col", [P, NS])
        b_nrm = lb("b_nrm", [P, 2, NS])
        b_hi, b_lo = lb("b_hi", [P, 2, NS]), lb("b_lo", [P, 2, NS])
        diag_hi, diag_lo = lb("diag_hi", [P, 2, NS, L], F32R), lb("diag_lo", [P, 2, NS, L], F32R)
        tst = lb("tst", [P, P])
        dt = lb("dt", [P, DC, P])
        du = lb("du", [P, DC, P])
        du_t = lb("du_t", [P, 2, DC, P], F32R)
        decay = lb("decay", [P, RING, GN, 2, L])
        state = lb("state", [P, RING, GN, P])
        acc = lb("acc", [P, DI])
        r1, x1 = lb("r1", [P, H]), lb("x1", [P, H])
        bn, mv, rstd = lb("bn", [P, 6]), lb("mv", [P, 2]), lb("rstd", [P, 1])
        du_hl = state[:, 0:4, :, :].rearrange("p r g t -> p (r g t)").rearrange(
            "p (c b s l) -> p c b s l", c=DC, b=2, s=2)
        y = du

        c2, cs = lb("c2", [P, H]), lb("cs", [P, H], F32R)
        ctx1 = lb("ctx1", [P, KC, 65])
        km, nkm = lb("km", [P, KC]), lb("nkm", [P, KC])
        kdiag = lb("kdiag", [P, KC, P], F32R)
        ek, eq = lb("ek", [P, KC, H]), lb("eq", [P, KC, H])
        gt = lb("gt", [P, H])
        rz = lb("rz", [P, 4])
        mt = [lb(f"mt{j}", [P, KC, P]) for j in range(2)]
        s_hl = [lb(f"s_hl{j}", [P, H], F32R) for j in range(2)]
        s_tmp = lb("s_tmp", [P, H], F32R)
        qm = lb("qm", [P, KC, HEADS])
        qrow = lb("qrow", [P, H], F32R)
        rq, u2, rn = lb("rq", [P, 2, H]), lb("u2", [P, H]), lb("rn", [P, H])
        bn2, mv2, rstd2 = lb("bn2", [P, 6]), lb("mv2", [P, 2]), lb("rstd2", [P, 1])
        x2 = lb("x2", [P, H])
        wq_raw, wk_raw = rn, u2
        wv_raw = ek[:, 0, 0:KC * 64].rearrange("p (c j) -> p c j", c=KC)
        wo_raw = ek[:, 1, :].rearrange("p (c j) -> p c j", c=KC)
        pick_raw = eq[:, 0, :].rearrange("p (c j) -> p c j", c=KC)
        ones_raw = eq[:, 1, 0:P]
        loop_mem.close()

        hid_mem = whole.enter_context(ExitStack())
        hid_hi = sb("hid_hi", [P, FC, TOK], F32R, hid_mem)
        hid_lo = sb("hid_lo", [P, FC, TOK], F32R, hid_mem)
        dw_raw = sb("dw_raw", [P, FC, H], I32, hid_mem)
        ds_sb = sb("ds_sb", [P, H], F32, hid_mem)
        up_mem = whole.enter_context(ExitStack())
        x2t_hi = sb("x2t_hi", [P, KC, TOK], F32R, up_mem)
        x2t_lo = sb("x2t_lo", [P, KC, TOK], F32R, up_mem)
        gu_raw = sb("gu_raw", [P, WR, 2, KC, P], I32, up_mem)
        gu = sb("gu", [P, WR, 2, KC, P], F32R, up_mem)
        gate = sb("gate", [P, 2, HALF], F32, up_mem)
        hid = sb("hid", [P, 2, HALF], F32, up_mem)
        x2_in = [gate[:, 0, :], gate[:, 1, :], hid[:, 0, :], hid[:, 1, :]]
        up_mem.close()
        down_mem = whole.enter_context(ExitStack())
        dw = sb("dw", [P, FC, H], F32R, down_mem)
        x2_res = sb("x2_res", [P, 2, H], F32, down_mem)
        r3 = sb("r3", [P, 2, H], F32, down_mem)
        y3 = sb("y3", [P, 2, H], F32, down_mem)
        bn3, mv3, rstd3 = sb("bn3", [P, 2, 6], F32, down_mem), sb("mv3", [P, 2, 2], F32, down_mem), sb("rstd3", [P, 2, 1], F32, down_mem)
        down_mem.close()

        par_in, win_in, wout_in = sem("par_in"), sem("win_in"), sem("wout_in")
        xt_in, xtok_in, ctx_in, ctx1_in = sem("xt_in"), sem("xtok_in"), sem("ctx_in"), sem("ctx1_in")
        const_step, const_done, setup_act, setup_vec, setup_pe = (
            sem("const_step"), sem("const_done"), sem("setup_act"), sem("setup_vec"), sem("setup_pe"))
        front_full, drive_full = sem("front_full"), sem("drive_full")
        turned_full, att_full = sem("turned_full"), sem("att_full")
        front_free = [sem("front_free0"), sem("front_free1")]
        att_free = [sem("att_free0"), sem("att_free1")]
        taps_done, conv_step, xs_done = sem("taps_done"), sem("conv_step"), sem("xs_done")
        sq3_done, rms_step = sem("sq3_done"), sem("rms_step")
        diag_done = sem("diag_done")
        log_step, dt_done, du_done, du_hi = sem("log_step"), sem("dt_done"), sem("du_done"), sem("du_hi")
        du_lo = sem("du_lo")
        decay_done, scan_done, mix_done = sem("decay_done"), sem("scan_done"), sem("mix_done")
        y_done, ln1_step, x1_done = sem("y_done"), sem("ln1_step"), sem("x1_done")
        cs_hi, cs_lo = sem("cs_hi"), sem("cs_lo")
        km_done, kdiag_done = sem("km_done"), sem("kdiag_done")
        rz_step = sem("rz_step")
        s_hi, s_lo, s_in = sem("s_hi"), sem("s_lo"), sem("s_in")
        rms_root, ln1_root, ln2_root, ln3_root = sem("rms_root"), sem("ln1_root"), sem("ln2_root"), sem("ln3_root")
        norm_step, rq_done = sem("norm_step"), sem("rq_done")
        eq_done = sem("eq_done")
        usq_done, ln2_step, x2_done, x2_out = sem("usq_done"), sem("ln2_step"), sem("x2_done"), sem("x2_out")
        x2_stored = sem("x2_stored")
        f_in = [sem(f"f_in{k}") for k in range(4)]
        f_full, f_hi, f_lo = sem("f_full"), sem("f_hi"), sem("f_lo")
        gu_in = [sem(f"gu_in{k}") for k in range(WR)]
        gu_done, gate_full, up_full, gate_done, hid_done = (
            sem("gu_done"), sem("gate_full"), sem("up_full"), sem("gate_done"), sem("hid_done"))
        hid_hi_done, hid_lo_done, dw_in, dw_done = sem("hid_hi_done"), sem("hid_lo_done"), sem("dw_in"), sem("dw_done")
        res_in = [sem("res_in0"), sem("res_in1")]
        down_full, ln3_step, y3_done = sem("down_full"), sem("ln3_step"), sem("y3_done")
        out_done = [sem("out_done0"), sem("out_done1")]

        block = whole.enter_context(nc.Block())
        N_PAR = 26

        @block.sync
        def _(sp):
            def load(dst, src, to=par_in):
                sp.dma_start(dst, src).then_inc(to, 16)

            for k in range(KC):
                load(win[:, k, :], w_in[k], win_in)
            load(cw[:, :, :], conv_w)
            load(cb[:, :], conv_b)
            load(bdt[:, :], b_dt)
            load(dsk[:, :], d_skip)
            load(neg_a[:, :, :], a_log)
            load(wx[:, :, :], w_x)
            load(wq_raw[0:64, :], wq)
            load(wq_raw[64:P, :], wq)
            load(wk_raw[0:64, :], wk)
            load(wk_raw[64:P, :], wk)
            load(wv_raw, wv)
            sp.wait_ge(const_done, 1)
            load(wdt[0:RK, :], w_dt)
            for c in range(KC):
                for j in range(2):
                    load(wo_raw[64 * j:64 * j + 64, c, 64 * j:64 * j + 64], wo[64 * j:64 * j + 64, c, :])
            load(bo_sb[0:64, :], bo)
            load(bo_sb[64:P, :], bo)
            load(g8[0:64, :], gain)
            load(g8[64:P, :], gain)
            load(gs_sb[:, :], gate_s)
            load(us_sb[:, :], up_s)
            load(wout[:, :, :], w_out, wout_in)

            def load_tokens(i):
                sp.wait_ge(xs_done, PRIMED + 2 * i)
                load(xt[:, :, :], x_t[i], xt_in)

            def load_residual(i):
                sp.wait_ge(front_free[1], PRIMED + 8 * i)
                load(xtok[:, :], x_tok[i], xtok_in)

            def load_context(p, j):
                sp.wait_ge(cs_lo, PRIMED + 2 * p + j)
                load(c2[0:64, :], ctx[2 * p + j], ctx_in)
                load(c2[64:P, :], ctx[2 * p + j], ctx_in)
                sp.wait_ge(rz_step, PRIMED + 4 * p + 2 * j)
                load(ctx1[:, :, 0:64], ctx_t[2 * p + j], ctx1_in)

            def move_parts(p):
                sp.wait_ge(s_lo, p + 1)
                load(s_hl[0][64:P, :].bitcast(F32), s_tmp[0:64, :].bitcast(F32), s_in)
                load(s_hl[1][0:64, :].bitcast(F32), s_tmp[64:P, :].bitcast(F32), s_in)

            load_tokens(0)
            load_residual(0)
            with sp.Fori(1, PAIRS) as i:
                load_tokens(i)
                load_context(i - 1, 0)
                load_residual(i)
                move_parts(i - 1)
                load_context(i - 1, 1)
            load_context(PAIRS - 1, 0)
            move_parts(PAIRS - 1)
            load_context(PAIRS - 1, 1)

            sp.wait_ge(x2_out, 16 * PAIRS)
            sp.wait_ge(att_full, PRIMED + ATT * PAIRS)
            for t in range(TC):
                if t >= 4:
                    sp.wait_ge(f_lo, t - 3)
                load(x2_in[t % 4], x2_dram[t], f_in[t % 4])
            for f in range(FC):
                if f == 0:
                    load(ds_sb[:, :], down_s.partition_broadcast(P), dw_in)
                if f >= WR:
                    sp.wait_ge(gu_done, f - WR + 1)
                load(gu_raw[:, f % WR, 0, :, :], gate_w[f], gu_in[f % WR])
                load(gu_raw[:, f % WR, 1, :, :], up_w[f], gu_in[f % WR])
                load(dw_raw[:, f, :], down_w[f], dw_in)
            for t in range(TC):
                if t < 2:
                    sp.wait_ge(up_full, HALVES * FC)
                    sp.wait_ge(hid_lo_done, HALVES * FC)
                else:
                    sp.wait_ge(ln3_step, 4 * (t - 2) + 2)
                load(x2_res[:, t % 2, :], x2_dram[t], res_in[t % 2])

        @block.gpsimd
        def _(pool):
            for counter in (xs_done, *front_free, cs_lo, rz_step, drive_full, scan_done, mix_done, diag_done, y_done,
                            turned_full, eq_done, x2_done, decay_done, kdiag_done, att_full, *att_free, x2_stored):
                pool.sem_inc(counter, PRIMED)
            pool.memset(ident[:, :], 0.0)
            pool.memset(eps_ln[:, :], LN_EPS)
            pool.memset(eps_rms[:, :], RMS_EPS)
            pool.memset(two_eyes[:, :], 0.0)
            pool.memset(pick_raw, 0.0)
            pool.memset(ones_raw, 1.0)
            pool.memset(ek[:, 1, :], 0.0)
            pool.memset(blocks[:, :], 0.0)
            pool.memset(wdt[:, :], 0.0).then_inc(const_step, 1)
            pool.wait_ge(const_step, 1)
            pool.affine_select(out=ident[:, :], in_=ident[:, :], compare_op=ALU.not_equal, fill=1.0, base=0,
                               pattern=[[-1, P]], channel_multiplier=1)
            pool.affine_select(out=pick_raw, in_=pick_raw, compare_op=ALU.not_equal, fill=-1.0, base=0,
                               pattern=[[-2, KC], [-1, 2], [0, 64]], channel_multiplier=1)
            pool.affine_select(out=two_eyes[:, :], in_=two_eyes[:, :], compare_op=ALU.not_equal, fill=1.0, base=0,
                               pattern=[[-1, L]], channel_multiplier=1).then_inc(const_step, 1)
            pool.wait_ge(const_step, 2)
            pool.affine_select(out=two_eyes[:, :], in_=two_eyes[:, :], compare_op=ALU.not_equal, fill=1.0, base=-L,
                               pattern=[[-1, L]], channel_multiplier=1)
            pool.memset(blocks[0:64, 0:64], 1.0)
            pool.memset(tst[:, :], 0.0)
            pool.memset(ssm[:, :], 0.0)
            pool.memset(ssm2[:, :, :, :], 0.0)
            pool.memset(decay[:, :, :, :, :].rearrange("p r n b l -> p (r n b l)"), 0.0)
            pool.memset(qrow[:, :].bitcast(F32), 0.0)
            pool.memset(mt[0][:, :, :], 0.0)
            pool.memset(mt[1][:, :, :], 0.0)
            pool.memset(ctx1[:, :, 64:65], 1.0)
            pool.memset(ucat[:, :, :], 0.0).then_inc(const_step, 1)
            pool.wait_ge(const_step, 3)
            pool.memset(blocks[64:P, 64:P], 1.0)
            pool.memset(ucat[64:65, :, P:P + 1], 1.0).then_inc(const_done, 1)
            pool.wait_ge(const_done, 1)

            def diagonals(i):
                pool.wait_ge(rms_step, 6 * i + 6)
                pool.wait_ge(drive_full, PRIMED + SCANS * i)
                for g in range(NG):
                    for b in range(2):
                        for part, diag in ((b_hi, diag_hi), (b_lo, diag_lo)):
                            pool.tensor_tensor(
                                diag[:, b, g * GN:(g + 1) * GN, :],
                                two_eyes[:, :].unsqueeze(1).to_broadcast([P, GN, L]),
                                part[:, b, g * GN:(g + 1) * GN].unsqueeze(2).to_broadcast([P, GN, L]),
                                ALU.mult).then_inc(diag_done, 1)

            def maxima(p, j):
                pool.wait_ge(km_done, 2 * p + j + 1)
                pool.wait_ge(rz_step, PRIMED + 4 * p + 2 * j)
                pool.tensor_tensor(
                    kdiag[:, :, :], ident[:, :].unsqueeze(1).to_broadcast([P, KC, P]),
                    nkm[:, :].unsqueeze(2).to_broadcast([P, KC, P]), ALU.mult).then_inc(kdiag_done, 1)

            def store_x2(p):
                pool.wait_ge(x2_done, PRIMED + p + 1)
                pool.dma_start(x2_dram[p], x2[:, :]).then_inc(x2_out, 16)
                pool.wait_ge(x2_out, 16 * p + 16)
                pool.sem_inc(x2_stored, 1)

            diagonals(0)
            with pool.Fori(1, PAIRS) as i:
                maxima(i - 1, 0)
                diagonals(i)
                maxima(i - 1, 1)
                store_x2(i - 1)
            maxima(PAIRS - 1, 0)
            maxima(PAIRS - 1, 1)
            store_x2(PAIRS - 1)

            for f in range(FC):
                for h in range(HALVES):
                    n = f * HALVES + h
                    pool.wait_ge(hid_hi_done, n + 1)
                    pool.tensor_tensor(hid_lo[:, f, h * HALF:(h + 1) * HALF], hid[:, n % 2, :],
                                       hid_hi[:, f, h * HALF:(h + 1) * HALF].bitcast(F32),
                                       ALU.subtract).then_inc(hid_lo_done, 1)
            for t in range(TC):
                pool.wait_ge(y3_done, t + 1)
                pool.dma_start(out[t], y3[:, t % 2, :]).then_inc(out_done[t % 2], 16)
            for k in range(2):
                pool.wait_ge(out_done[k], 16 * TC // 2)

        @block.scalar
        def _(act):
            act.preload_act_table_set("natural_log_exp_and_others")
            act.wait_ge(par_in, 16 * N_PAR)
            act.wait_ge(const_done, 1)
            act.activation(neg_a[:, :, :], neg_a[:, :, :], ACT.Exp).then_inc(setup_act, 1)
            act.activation(wq_hi[:, :], wq_raw[:, :], ACT.Copy).then_inc(setup_act, 1)
            act.activation(wk_hi[:, :], wk_raw[:, :], ACT.Copy).then_inc(setup_act, 1)
            act.activation(pick[:, :, :], pick_raw, ACT.Copy).then_inc(setup_act, 1)
            act.activation(ones_r[:, :], ones_raw, ACT.Copy).then_inc(setup_act, 1)
            act.wait_ge(setup_pe, 1)
            act.activation(ucat[0:64, :, 0:P], att[0][0:64, :].rearrange("p (c j) -> p c j", c=KC),
                           ACT.Copy).then_inc(setup_act, 1)
            act.wait_ge(setup_vec, 1)

            def inverse_root(to, var, eps, step, before):
                act.activation(to, var, ACT.Ln, bias=eps).then_inc(step, 1)
                act.wait_ge(step, before + 1)
                act.activation(to, to, ACT.Exp, scale=-0.5).then_inc(step, 1)

            def project_and_convolve(i):
                for h in range(2):
                    act.wait_ge(front_full, FRONT * i + h + 1)
                    act.wait_ge(y_done, PRIMED + 2 * i)
                    for c in range(4):
                        d = 4 * h + c
                        tap = act.activation(xs[:, d, :], front[h][:, c * P:(c + 1) * P], ACT.Identity,
                                             bias=cb[:, d:d + 1], scale=cw[:, d, TAPS - 1:TAPS])
                    tap.then_inc(taps_done, 1)
                for h in range(2):
                    act.wait_ge(front_full, FRONT * i + h + 3)
                    act.activation(sg[:, 4 * h:4 * h + 4, :], front[h][:, :].rearrange("p (c t) -> p c t", c=4),
                                   ACT.Silu).then_inc(front_free[h], 1)
                for h in range(2):
                    act.wait_ge(front_free[h], PRIMED + 8 * i + 1)
                    act.activation(xs[:, 4 * h:4 * h + 4, :], xs[:, 4 * h:4 * h + 4, :], ACT.Silu).then_inc(xs_done, 1)
                act.preload_act_table_set("natural_log_exp_and_others")

            def ssm_by_channel(i):
                act.wait_ge(front_full, FRONT * i + 5)
                act.activation(ssm[0:64, :], front[0][0:64, 0:P], ACT.Copy)
                act.activation(ssm2[0:64, :, :, :], front[0][0:64, 0:P].rearrange("k (b l) -> k b l", b=2).unsqueeze(2)
                               .to_broadcast([64, 2, 2, L]), ACT.Copy).then_inc(front_free[0], 1)

            def ssm_by_token(i):
                act.wait_ge(front_full, FRONT * i + 6)
                act.activation(tr[:, :, :], front[1][:, 0:3 * P].rearrange("p (s k) -> p s k", s=3)[:, :, 0:64],
                               ACT.Copy).then_inc(front_free[1], 1)
                act.wait_ge(front_free[1], PRIMED + 8 * i + 3)
                act.activation(sq3[:, :, :], tr[:, :, :], ACT.Square).then_inc(sq3_done, 1)
                act.wait_ge(rms_step, 6 * i + 2)
                inverse_root(rms[:, :], rms[:, :], eps_rms[:, :], rms_root, 2 * i)

            def dt_input(i):
                act.wait_ge(front_full, FRONT * i + 7)
                act.activation(tst[0:RK, :], front[0][0:RK, 0:P], ACT.Copy).then_inc(front_free[0], 1)

            def softplus(i):
                act.wait_ge(front_free[0], PRIMED + 8 * i + 5)
                act.wait_ge(front_free[1], PRIMED + 8 * i + 4)
                act.activation(du[:, :, :], dt[:, :, :], ACT.Abs).then_inc(log_step, 1)
                act.wait_ge(log_step, 3 * i + 1)
                act.activation(du[:, :, :], du[:, :, :], ACT.Exp, scale=-1.0).then_inc(log_step, 1)
                act.wait_ge(log_step, 3 * i + 2)
                act.activation(du[:, :, :], du[:, :, :], ACT.Ln, bias=1.0).then_inc(log_step, 1)

            def du_parts(i):
                act.wait_ge(du_done, i + 1)
                act.wait_ge(turned_full, PRIMED + SCANS * i)
                act.activation(du_hl[:, :, :, 0, :].bitcast(F32R), du[:, :, :].rearrange("p c (b l) -> p c b l", b=2),
                               ACT.Copy).then_inc(du_hi, 1)

            def du_by_token(i):
                for k in range(4):
                    act.wait_ge(front_full, FRONT * i + 10 + k)
                    act.wait_ge(drive_full, PRIMED + SCANS * i)
                    act.activation(du_t[:, :, 2 * k:2 * k + 2, :],
                                   front[(9 + k) % 2][:, :].rearrange("p (b c d) -> p b c d", b=2, c=2),
                                   ACT.Copy).then_inc(front_free[(9 + k) % 2], 1)

            def decays(i, u):
                g, d = u // DC, u % DC
                act.wait_ge(scan_done, PRIMED + SCANS * i + max(u - RING + 1, 0))
                for n in range(GN):
                    ins = act.activation(
                        decay[:, u % RING, n, :, 1:L],
                        dt[:, d, :].rearrange("p (b l) -> p b l", b=2)[:, :, 1:L],
                        ACT.Exp, scale=neg_a[:, d, g * GN + n:g * GN + n + 1])
                ins.then_inc(decay_done, 1)

            def split_x1(p):
                act.wait_ge(x1_done, p + 1)
                act.activation(s_hl[0][0:64, :], x1[0:64, :], ACT.Copy)
                act.activation(s_tmp[64:P, :], x1[64:P, :], ACT.Copy).then_inc(s_hi, 1)

            def split_context(p, j):
                act.wait_ge(ctx_in, 64 * p + 32 * j + 32)
                act.wait_ge(att_full, PRIMED + ATT * p + 8 * j)
                act.activation(cs[:, :], c2[:, :], ACT.Copy).then_inc(cs_hi, 1)

            def exp_keys(p, j, c):
                act.wait_ge(att_full, PRIMED + ATT * p + ATT_B * j + 5 + c)
                bank, _ = bank_of(ATT_B * j + 4 + c)
                act.activation(ek[:, c, :], att[bank][:, :], ACT.Exp).then_inc(att_free[bank], 1)

            def keys_times_context(p, j):
                act.wait_ge(att_full, PRIMED + ATT * p + ATT_B * j + 9)
                bank, _ = bank_of(ATT_B * j + 8)
                act.activation(gt[0:65, :], att[bank][0:65, :], ACT.Copy).then_inc(att_free[bank], 1)

            def query_maxima(p, j):
                act.wait_ge(att_full, PRIMED + ATT * p + ATT_B * j + 16)
                bank, _ = bank_of(ATT_B * j + 15)
                act.activation(qrow[0:HEADS, :], att[bank][0:HEADS, :], ACT.Copy).then_inc(att_free[bank], 1)

            def exp_queries(p, j, c):
                act.wait_ge(att_full, PRIMED + ATT * p + ATT_B * j + 17 + c)
                bank, _ = bank_of(ATT_B * j + 16 + c)
                act.activation(eq[:, c, :], att[bank][:, :], ACT.Exp).then_inc(att_free[bank], 1)

            def inverse_sums(p, j, c):
                act.wait_ge(att_full, PRIMED + ATT * p + ATT_B * j + 21 + c)
                bank, k = bank_of(ATT_B * j + 20 + c)
                act.wait_ge(eq_done, PRIMED + 8 * p + 4 * j + max(c - 1, 0))
                act.activation(rq[:, c % 2, :], att[bank][:, :], ACT.Ln).then_inc(att_free[bank], 1)
                act.wait_ge(att_free[bank], PRIMED + ATT_FREE[bank] * p + k + 1)
                act.activation(rq[:, c % 2, :], rq[:, c % 2, :], ACT.Exp, scale=-1.0).then_inc(rq_done, 1)

            def attention_out(p, j):
                act.wait_ge(att_full, PRIMED + ATT * p + ATT_B * j + 25)
                bank, _ = bank_of(ATT_B * j + 24)
                act.wait_ge(x2_done, PRIMED + p)
                act.activation(u2[64 * j:64 * j + 64, :], att[bank][64 * j:64 * j + 64, :], ACT.Identity,
                               bias=bo_sb[64 * j:64 * j + 64, :]).then_inc(att_free[bank], 1)

            def norm_of_out(p):
                act.wait_ge(att_free[1], PRIMED + 25 * p + 25)
                act.activation(rn[:, :], u2[:, :], ACT.Square).then_inc(usq_done, 1)

            def inverse_norm(p):
                act.wait_ge(att_free[0], PRIMED + 26 * p + 26)
                act.activation(rn[:, :], rn[:, :], ACT.Ln, scale=NORM_SCALE).then_inc(norm_step, 1)
                act.wait_ge(norm_step, 2 * p + 1)
                act.activation(rn[:, :], rn[:, :], ACT.Exp, scale=-0.5).then_inc(norm_step, 1)

            def root_ln2(p):
                act.wait_ge(ln2_step, 4 * p + 4)
                inverse_root(rstd2[:, :], mv2[:, 1:2], eps_ln[:, :], ln2_root, 2 * p)

            def root_ln1(i):
                act.wait_ge(ln1_step, 2 * i + 2)
                inverse_root(rstd[:, :], mv[:, 1:2], eps_ln[:, :], ln1_root, 2 * i)

            def attention_beside(p, s):
                c = s % KC
                if s < 4:
                    inverse_sums(p, 0, c)
                elif s == 4:
                    split_context(p, 1)
                elif s == 7:
                    attention_out(p, 0)
                elif s in range(12, 16):
                    exp_keys(p, 1, c)
                elif s == 19:
                    keys_times_context(p, 1)
                elif s == 25:
                    query_maxima(p, 1)
                elif s in range(26, 30):
                    exp_queries(p, 1, s - 26)
                elif s in range(30, 34):
                    inverse_sums(p, 1, s - 30)
                elif s == 35:
                    attention_out(p, 1)

            def turn(i, p):
                mamba, attention = i is not None, p is not None
                if attention:
                    split_x1(p)
                    split_context(p, 0)
                if mamba:
                    project_and_convolve(i)
                    ssm_by_channel(i)
                if attention:
                    for c in range(KC):
                        exp_keys(p, 0, c)
                if mamba:
                    ssm_by_token(i)
                if attention:
                    keys_times_context(p, 0)
                if mamba:
                    dt_input(i)
                    softplus(i)
                if attention:
                    query_maxima(p, 0)
                if mamba:
                    du_parts(i)
                if attention:
                    for c in range(KC):
                        exp_queries(p, 0, c)
                if mamba:
                    du_by_token(i)
                for s in range(STEPS + GC):
                    if mamba and s < SCANS:
                        decays(i, s)
                    if attention and s >= GC:
                        attention_beside(p, s - GC)
                if attention:
                    norm_of_out(p)
                    inverse_norm(p)
                    root_ln2(p)
                if mamba:
                    root_ln1(i)

            turn(0, None)
            with act.Fori(1, PAIRS) as i:
                turn(i, i - 1)
            turn(None, PAIRS - 1)

            for t in range(TC):
                act.wait_ge(f_full, t + 1)
                act.activation(x2t_hi[:, :, t * P:(t + 1) * P],
                               front[t % 2][:, :].rearrange("p (c t) -> p c t", c=KC), ACT.Copy).then_inc(f_hi, 1)

            def convert(f):
                act.wait_ge(gu_in[f % WR], 32 * (f // WR) + 32)
                if f >= WR:
                    act.wait_ge(up_full, HALVES * (f - WR + 1))
                act.activation(gu[:, f % WR, :, :, :].rearrange("p s c k -> p (s c k)"),
                               gu_raw[:, f % WR, :, :, :].rearrange("p s c k -> p (s c k)"),
                               ACT.Copy).then_inc(gu_done, 1)

            convert(0)
            for f in range(FC):
                if f + 1 < FC:
                    convert(f + 1)
                for h in range(HALVES):
                    n = f * HALVES + h
                    act.wait_ge(gate_full, n + 1)
                    if n >= 2:
                        act.wait_ge(hid_done, n - 1)
                    act.activation(gate[:, n % 2, :], drive[n % 2][:, :], ACT.Silu,
                                   scale=gs_sb[:, f:f + 1]).then_inc(gate_done, 1)
                    act.wait_ge(hid_done, n + 1)
                    act.activation(hid_hi[:, f, h * HALF:(h + 1) * HALF], hid[:, n % 2, :],
                                   ACT.Copy).then_inc(hid_hi_done, 1)
            act.preload_act_table_set("natural_log_exp_and_others")
            for t in range(TC):
                act.wait_ge(ln3_step, 4 * t + 4)
                inverse_root(rstd3[:, t % 2, :], mv3[:, t % 2, 1:2], eps_ln[:, :], ln3_root, 2 * t)

        @block.vector
        def _(dve):
            dve.wait_ge(par_in, 16 * N_PAR)
            dve.wait_ge(setup_act, 3)
            dve.tensor_tensor(wq_lo[:, :], wq_raw[:, :], wq_hi[:, :].bitcast(F32), ALU.subtract)
            dve.tensor_tensor(wk_lo[:, :], wk_raw[:, :], wk_hi[:, :].bitcast(F32), ALU.subtract)
            dve.tensor_scalar(g8[:, :], g8[:, :], float(np.sqrt(DH) * np.sqrt(NORM_SCALE)), None, ALU.mult)
            dve.tensor_scalar(neg_a[:, :, :], neg_a[:, :, :], -1.0, None, ALU.mult).then_inc(setup_vec, 1)

            def convolve(i):
                for h in range(2):
                    dve.wait_ge(taps_done, 2 * i + h + 1)
                    for s in range(1, TAPS):
                        if s > 1:
                            dve.wait_ge(conv_step, 4 * i + 2 * h + s - 1)
                        for c in range(4):
                            d = 4 * h + c
                            new = xs[:, d, :].rearrange("p (b l) -> p b l", b=2)[:, :, s:L]
                            src = front[h][:, c * P:(c + 1) * P].rearrange("p (b l) -> p b l", b=2)[:, :, 0:L - s]
                            tap = dve.scalar_tensor_tensor(out=new, in0=src, scalar=cw[:, d, TAPS - 1 - s:TAPS - s],
                                                           in1=new, op0=ALU.mult, op1=ALU.add)
                        tap.then_inc(conv_step if s < TAPS - 1 else front_free[h], 1)

            def ssm_norms(i):
                dve.wait_ge(sq3_done, i + 1)
                dve.tensor_reduce(rms[:, 0:1], sq3[:, 0, 0:RK], AX_X, ALU.add)
                dve.tensor_reduce(rms[:, 1:2], sq3[:, 0, RK + NS:64], AX_X, ALU.add)
                dve.tensor_reduce(rms[:, 2:4], sq3[:, 1:3, RK:RK + NS], AX_X, ALU.add).then_inc(rms_step, 1)
                dve.wait_ge(rms_step, 6 * i + 1)
                dve.tensor_scalar(rms[:, 0:1], rms[:, 0:1], 1.0 / RK, None, ALU.mult)
                dve.tensor_scalar(rms[:, 1:4], rms[:, 1:4], 1.0 / NS, None, ALU.mult).then_inc(rms_step, 1)
                dve.wait_ge(rms_root, 2 * i + 2)
                dve.tensor_scalar(tsn[:, :], tr[:, 0, 0:RK], rms[:, 0:1], None, ALU.mult).then_inc(rms_step, 1)
                dve.tensor_scalar(c_col[:, :], tr[:, 0, RK + NS:64], rms[:, 1:2], None, ALU.mult)
                for b in range(2):
                    ins = dve.tensor_scalar(b_nrm[:, b, :], tr[:, 1 + b, RK:RK + NS], rms[:, 2 + b:3 + b], None, ALU.mult)
                ins.then_inc(rms_step, 1)
                dve.wait_ge(rms_step, 6 * i + 4)
                dve.wait_ge(diag_done, PRIMED + 16 * i)
                dve.tensor_copy(b_hi[:, :, :].bitcast(F32R), b_nrm[:, :, :]).then_inc(rms_step, 1)
                dve.wait_ge(rms_step, 6 * i + 5)
                dve.tensor_tensor(b_lo[:, :, :], b_nrm[:, :, :], b_hi[:, :, :], ALU.subtract).then_inc(rms_step, 1)

            def dt_before_softplus(i):
                for h in range(2):
                    bank = (7 + h) % 2
                    dve.wait_ge(front_full, FRONT * i + 8 + h)
                    dve.wait_ge(decay_done, PRIMED + SCANS * i)
                    dve.tensor_tensor(dt[:, 4 * h:4 * h + 4, :], front[bank][:, :].rearrange("p (c t) -> p c t", c=4),
                                      bdt[:, 4 * h:4 * h + 4].unsqueeze(2).to_broadcast([P, 4, P]),
                                      ALU.add).then_inc(front_free[bank], 1)

            def dt_and_du(i):
                dve.wait_ge(log_step, 3 * i + 3)
                dve.scalar_tensor_tensor(out=dt[:, :, :].rearrange("p c t -> p (c t)"),
                                         in0=dt[:, :, :].rearrange("p c t -> p (c t)"), scalar=0.0,
                                         in1=du[:, :, :].rearrange("p c t -> p (c t)"),
                                         op0=ALU.max, op1=ALU.add).then_inc(dt_done, 1)
                dve.wait_ge(dt_done, i + 1)
                dve.wait_ge(xs_done, PRIMED + 2 * i + 2)
                dve.tensor_tensor(du[:, :, :], dt[:, :, :], xs[:, :, :], ALU.mult).then_inc(du_done, 1)

            def du_low_part(i):
                dve.wait_ge(du_hi, i + 1)
                dve.tensor_tensor(du_hl[:, :, :, 1, :], du[:, :, :].rearrange("p c (b l) -> p c b l", b=2),
                                  du_hl[:, :, :, 0, :], ALU.subtract).then_inc(du_lo, 1)

            def scan(i, u):
                dve.wait_ge(decay_done, PRIMED + SCANS * i + u + 1)
                dve.wait_ge(drive_full, PRIMED + SCANS * i + u + 1)
                dve.wait_ge(turned_full, PRIMED + SCANS * i + max(GN * (u // GC - 1), 0))
                dve.tensor_tensor_scan(
                    state[:, u % RING, :, :].rearrange("p n t -> p (n t)"),
                    decay[:, u % RING, :, :, :].rearrange("p n b l -> p (n b l)"),
                    drive[u % 2][:, :], 0.0, ALU.mult, ALU.add).then_inc(scan_done, 1)

            def mix(i, v):
                item, c = v // GN, v % GN
                n, part = (item // NGC) * GN + c, item % NGC
                to = acc[:, part * 512:(part + 1) * 512]
                dve.wait_ge(turned_full, PRIMED + SCANS * i + v + 1)
                dve.wait_ge(mix_done, PRIMED + SCANS * i + v)
                if n == 0:
                    ins = dve.tensor_scalar(to, turned[v % 2][:, :], c_col[:, n:n + 1], None, ALU.mult)
                else:
                    ins = dve.scalar_tensor_tensor(out=to, in0=turned[v % 2][:, :], scalar=c_col[:, n:n + 1],
                                                   in1=to, op0=ALU.mult, op1=ALU.add)
                ins.then_inc(mix_done, 1)

            def gated_sum(i):
                for h in range(2):
                    bank, k = bank_of(13 + h)
                    dve.wait_ge(front_full, FRONT * i + 14 + h)
                    for c in range(4):
                        d = 4 * h + c
                        ins = dve.scalar_tensor_tensor(out=y[:, d, :], in0=xs[:, d, :], scalar=dsk[:, d:d + 1],
                                                       in1=front[bank][:, c * P:(c + 1) * P], op0=ALU.mult, op1=ALU.add)
                    ins.then_inc(front_free[bank], 1)
                    dve.wait_ge(front_free[bank], PRIMED + 8 * i + k + 1)
                    dve.tensor_tensor(y[:, 4 * h:4 * h + 4, :], y[:, 4 * h:4 * h + 4, :], sg[:, 4 * h:4 * h + 4, :],
                                      ALU.mult).then_inc(y_done, 1)

            def layernorm_x1(i):
                dve.wait_ge(front_full, FRONT * i + 16)
                dve.wait_ge(xtok_in, 16 * i + 16)
                dve.tensor_tensor(r1[:, :], front[1][:, :], xtok[:, :], ALU.add).then_inc(front_free[1], 1)
                dve.wait_ge(front_free[1], PRIMED + 8 * i + 8)
                dve.bn_stats(bn[:, :], r1[:, :]).then_inc(ln1_step, 1)
                dve.drain()
                dve.bn_aggr(mv[:, :], bn[:, :]).then_inc(ln1_step, 1)
                dve.wait_ge(ln1_root, 2 * i + 2)
                dve.tensor_scalar(x1[:, :], r1[:, :], mv[:, 0:1], rstd[:, 0:1], ALU.subtract, ALU.mult).then_inc(x1_done, 1)

            def context_low_part(p, j):
                dve.wait_ge(cs_hi, 2 * p + j + 1)
                dve.tensor_tensor(cs[64:P, :], c2[64:P, :], cs[64:P, :].bitcast(F32), ALU.subtract).then_inc(cs_lo, 1)

            def x1_low_part(p):
                dve.wait_ge(s_hi, p + 1)
                dve.tensor_tensor(s_tmp[0:64, :], x1[0:64, :], s_hl[0][0:64, :].bitcast(F32), ALU.subtract)
                dve.tensor_tensor(s_hl[1][64:P, :], x1[64:P, :], s_tmp[64:P, :].bitcast(F32),
                                  ALU.subtract).then_inc(s_lo, 1)

            def key_maxima(p, j, c):
                dve.wait_ge(att_full, PRIMED + ATT * p + ATT_B * j + 1 + c)
                bank, k = bank_of(ATT_B * j + c)
                dve.tensor_reduce(km[:, c:c + 1], att[bank][:, :], AX_X, ALU.max).then_inc(att_free[bank], 1)
                if c == KC - 1:
                    dve.wait_ge(att_free[bank], PRIMED + ATT_FREE[bank] * p + k + 1)
                    dve.wait_ge(kdiag_done, PRIMED + 2 * p + j)
                    dve.tensor_scalar(nkm[:, :], km[:, :], -1.0, None, ALU.mult).then_inc(km_done, 1)

            def context_matrix(p, j, k):
                bank, _ = bank_of(ATT_B * j + 9 + k)
                both = att[bank][:, 0:2 * (P + 1)].rearrange("p (c x) -> p c x", c=2)
                dve.wait_ge(att_full, PRIMED + ATT * p + ATT_B * j + 10 + k)
                dve.reciprocal(rz[:, 2 * k:2 * k + 2], both[:, :, P:P + 1].squeeze(2)).then_inc(rz_step, 1)
                dve.wait_ge(rz_step, PRIMED + 4 * p + 2 * j + k + 1)
                for r in (0, 64):
                    ins = dve.scalar_tensor_tensor(
                        out=mt[j][r:r + 64, 2 * k:2 * k + 2, 64 * j:64 * j + 64], in0=both[r:r + 64, :, r:r + 64],
                        scalar=DH ** -0.5, in1=rz[r:r + 64, 2 * k:2 * k + 2].unsqueeze(2).to_broadcast([64, 2, 64]),
                        op0=ALU.mult, op1=ALU.mult)
                ins.then_inc(att_free[bank], 1)

            def query_maxima(p, j, c):
                dve.wait_ge(att_full, PRIMED + ATT * p + ATT_B * j + 12 + c)
                bank, _ = bank_of(ATT_B * j + 11 + c)
                dve.tensor_reduce(qm[:, c, :], att[bank][:, :].rearrange("p (h d) -> p h d", h=HEADS),
                                  AX_X, ALU.max).then_inc(att_free[bank], 1)

            def softmax_queries(p, j, c):
                dve.wait_ge(rq_done, 8 * p + 4 * j + c + 1)
                dve.tensor_tensor(eq[:, c, :], eq[:, c, :], rq[:, c % 2, :], ALU.mult).then_inc(eq_done, 1)

            def bound_norm(p):
                dve.wait_ge(att_full, PRIMED + ATT * p + ATT)
                dve.tensor_scalar(rn[:, :], att[0][:, :], 1e-24, None, ALU.max).then_inc(att_free[0], 1)

            def layernorm_x2(p):
                dve.wait_ge(norm_step, 2 * p + 2)
                dve.scalar_tensor_tensor(out=u2[:, :], in0=u2[:, :], scalar=g8[:, 0:1], in1=rn[:, :],
                                         op0=ALU.mult, op1=ALU.mult).then_inc(ln2_step, 1)
                dve.wait_ge(ln2_step, 4 * p + 1)
                dve.tensor_tensor(u2[:, :], u2[:, :], x1[:, :], ALU.add).then_inc(ln2_step, 1)
                dve.wait_ge(ln2_step, 4 * p + 2)
                dve.bn_stats(bn2[:, :], u2[:, :]).then_inc(ln2_step, 1)
                dve.drain()
                dve.bn_aggr(mv2[:, :], bn2[:, :]).then_inc(ln2_step, 1)
                dve.wait_ge(ln2_root, 2 * p + 2)
                dve.wait_ge(x2_stored, PRIMED + p)
                dve.tensor_scalar(x2[:, :], u2[:, :], mv2[:, 0:1], rstd2[:, 0:1],
                                  ALU.subtract, ALU.mult).then_inc(x2_done, 1)

            def attention_beside(p, s):
                c = s % KC
                if s < 4:
                    softmax_queries(p, 0, c)
                elif s == 4:
                    context_low_part(p, 1)
                elif s in range(8, 12):
                    key_maxima(p, 1, c)
                elif s == 20:
                    context_matrix(p, 1, 0)
                    context_matrix(p, 1, 1)
                elif s in range(21, 25):
                    query_maxima(p, 1, s - 21)
                elif s in range(30, 34):
                    softmax_queries(p, 1, s - 30)

            def turn(i, p):
                mamba, attention = i is not None, p is not None
                if attention:
                    x1_low_part(p)
                    context_low_part(p, 0)
                if mamba:
                    convolve(i)
                if attention:
                    for c in range(KC):
                        key_maxima(p, 0, c)
                if mamba:
                    ssm_norms(i)
                if attention:
                    context_matrix(p, 0, 0)
                    context_matrix(p, 0, 1)
                if mamba:
                    dt_before_softplus(i)
                if attention:
                    for c in range(KC):
                        query_maxima(p, 0, c)
                if mamba:
                    dt_and_du(i)
                    du_low_part(i)
                for s in range(STEPS):
                    if mamba and s < SCANS:
                        scan(i, s)
                    if mamba and s >= GC:
                        mix(i, s - GC)
                    if attention and s > 0:
                        attention_beside(p, s - 1)
                if mamba:
                    gated_sum(i)
                if attention:
                    bound_norm(p)
                    layernorm_x2(p)
                if mamba:
                    layernorm_x1(i)

            turn(0, None)
            with dve.Fori(1, PAIRS) as i:
                turn(i, i - 1)
            turn(None, PAIRS - 1)

            for t in range(TC):
                dve.wait_ge(f_hi, t + 1)
                dve.tensor_tensor(x2t_lo[:, :, t * P:(t + 1) * P], front[t % 2][:, :].rearrange("p (c t) -> p c t", c=KC),
                                  x2t_hi[:, :, t * P:(t + 1) * P].bitcast(F32), ALU.subtract).then_inc(f_lo, 1)
            for n in range(FC * HALVES):
                f = n // HALVES
                dve.wait_ge(gate_done, n + 1)
                dve.wait_ge(up_full, n + 1)
                if n >= 2:
                    dve.wait_ge(hid_lo_done, n - 1)
                dve.scalar_tensor_tensor(out=hid[:, n % 2, :], in0=turned[n % 2][:, :], scalar=us_sb[:, f:f + 1],
                                         in1=gate[:, n % 2, :], op0=ALU.mult, op1=ALU.mult).then_inc(hid_done, 1)
            dve.wait_ge(dw_in, 16 * (FC + 1))
            for f in range(FC):
                dve.tensor_copy(dw[:, f, :], dw_raw[:, f, :]).then_inc(dw_done, 1)
            for t in range(TC):
                k = t % 2
                dve.wait_ge(down_full, t + 1)
                dve.tensor_tensor(r3[:, k, :], att[k][:, :], ds_sb[:, :], ALU.mult).then_inc(ln3_step, 1)
                dve.wait_ge(ln3_step, 4 * t + 1)
                dve.wait_ge(res_in[k], 16 * (t // 2 + 1))
                dve.tensor_tensor(r3[:, k, :], r3[:, k, :], x2_res[:, k, :], ALU.add).then_inc(ln3_step, 1)
                dve.wait_ge(ln3_step, 4 * t + 2)
                dve.bn_stats(bn3[:, k, :], r3[:, k, :]).then_inc(ln3_step, 1)
                dve.wait_ge(ln3_step, 4 * t + 3)
                dve.bn_aggr(mv3[:, k, :], bn3[:, k, :]).then_inc(ln3_step, 1)
                dve.wait_ge(ln3_root, 2 * t + 2)
                if t >= 2:
                    dve.wait_ge(out_done[k], 16 * (t // 2))
                dve.tensor_scalar(y3[:, k, :], r3[:, k, :], mv3[:, k, 0:1], rstd3[:, k, 0:1],
                                  ALU.subtract, ALU.mult).then_inc(y3_done, 1)

        @block.tensor
        def _(pe):
            pe.wait_ge(par_in, 16 * N_PAR)
            pe.wait_ge(const_done, 1)
            for c in range(KC):
                mm = pe.matmul(att[0][0:64, c * P:(c + 1) * P], wv_raw[:, c, :], wo_raw[:, c, :], start=True, stop=True)
            mm.then_inc(setup_pe, 1)
            pe.wait_ge(win_in, 16 * KC)
            pe.wait_ge(setup_act, 6)
            pe.wait_ge(setup_vec, 1)
            pe.wait_ge(wout_in, 16)

            def fill_front(i, n):
                bank, k = bank_of(n)
                pe.wait_ge(front_free[bank], PRIMED + 8 * i + k)
                return front[bank]

            def fill(p, j, n):
                bank, k = bank_of(ATT_B * j + n)
                pe.wait_ge(att_free[bank], PRIMED + ATT_FREE[bank] * p + k)
                return att[bank]

            def drained(p, j, n):
                bank, k = bank_of(ATT_B * j + n)
                pe.wait_ge(att_free[bank], PRIMED + ATT_FREE[bank] * p + k + 1)

            def project(i):
                pe.wait_ge(xt_in, 16 * i + 16)
                for h in range(4):
                    to = fill_front(i, h)
                    for c in range(4):
                        for k in range(KC):
                            mm = pe.matmul(to[:, c * P:(c + 1) * P], win[:, k, (4 * h + c) * P:(4 * h + c + 1) * P],
                                           xt[:, k, :], start=(k == 0), stop=(k == KC - 1))
                    mm.then_inc(front_full, 1)

            def ssm_by_channel(i):
                to = fill_front(i, 4)
                pe.wait_ge(xs_done, PRIMED + 2 * i + 2)
                for d in range(DC):
                    mm = pe.matmul(to[0:64, 0:P], wx[:, d, :], xs[:, d, :], start=(d == 0), stop=(d == DC - 1))
                mm.then_inc(front_full, 1)

            def ssm_by_token(i):
                to = fill_front(i, 5)
                pe.wait_ge(front_free[0], PRIMED + 8 * i + 3)
                pe.transpose(to[:, 0:P], ssm[:, :], ident[:, :])
                for b in range(2):
                    mm = pe.transpose(to[:, P * (b + 1):P * (b + 2)],
                                      ssm2[:, b, :, :].rearrange("k s l -> k (s l)"), ident[:, :])
                mm.then_inc(front_full, 1)

            def dt_input(i):
                to = fill_front(i, 6)
                pe.wait_ge(rms_step, 6 * i + 3)
                pe.transpose(to[0:RK, 0:P], tsn[:, :], ident[:, :]).then_inc(front_full, 1)

            def dt_projection(i):
                for h in range(2):
                    to = fill_front(i, 7 + h)
                    pe.wait_ge(front_free[0], PRIMED + 8 * i + 4)
                    for c in range(4):
                        d = 4 * h + c
                        mm = pe.matmul(to[:, c * P:(c + 1) * P], wdt[:, d * P:(d + 1) * P], tst[:, :], start=True, stop=True)
                    mm.then_inc(front_full, 1)

            def du_by_token(i):
                pe.wait_ge(du_lo, i + 1)
                for k in range(4):
                    to = fill_front(i, 9 + k)
                    for b in range(2):
                        for c in range(2):
                            mm = pe.transpose(to[:, (2 * b + c) * P:(2 * b + c + 1) * P],
                                              du_hl[:, 2 * k + c, b, :, :].rearrange("p s l -> p (s l)"), ident[:, :])
                    mm.then_inc(front_full, 1)
                pe.wait_ge(front_free[1], PRIMED + 8 * i + 6)
                pe.wait_ge(front_free[0], PRIMED + 8 * i + 7)

            def drives(i, u):
                g, d = u // DC, u % DC
                pe.wait_ge(scan_done, PRIMED + SCANS * i + max(u - 1, 0))
                pe.wait_ge(diag_done, PRIMED + 16 * i + 4 * (g + 1))
                to = drive[u % 2][:, :].rearrange("p (n b l) -> p n b l", n=GN, b=2)
                for b in range(2):
                    pe.matmul(to[:, :, b, :], du_t[:, b, d, :], diag_hi[:, b, g * GN:(g + 1) * GN, :],
                              start=True, stop=False)
                    mm = pe.matmul(to[:, :, b, :], du_t[:, b, d, :], diag_lo[:, b, g * GN:(g + 1) * GN, :],
                                   start=False, stop=True)
                mm.then_inc(drive_full, 1)

            def states_by_token(i, v):
                item, c = v // GN, v % GN
                pe.wait_ge(scan_done, PRIMED + SCANS * i + GC * (item + 1))
                pe.wait_ge(mix_done, PRIMED + SCANS * i + max(v - 1, 0))
                for k in range(GC):
                    mm = pe.transpose(turned[v % 2][:, k * P:(k + 1) * P],
                                      state[:, (GC * item + k) % RING, c, :], ident[:, :])
                mm.then_inc(turned_full, 1)

            def sums_by_channel(i):
                pe.wait_ge(mix_done, PRIMED + SCANS * i + SCANS)
                for h in range(2):
                    to = fill_front(i, 13 + h)
                    for c in range(4):
                        d = 4 * h + c
                        mm = pe.transpose(to[:, c * P:(c + 1) * P], acc[:, d * P:(d + 1) * P], ident[:, :])
                    mm.then_inc(front_full, 1)

            def project_out(i):
                to = fill_front(i, 15)
                pe.wait_ge(y_done, PRIMED + 2 * i + 2)
                for d in range(DC):
                    mm = pe.matmul(to[:, :], y[:, d, :], wout[:, d, :], start=(d == 0), stop=(d == DC - 1))
                mm.then_inc(front_full, 1)

            def keys_by_channel(p, j, c):
                to = fill(p, j, c)
                pe.wait_ge(cs_lo, PRIMED + 2 * p + j + 1)
                pe.matmul(to[:, :], wk_hi[:, c * P:(c + 1) * P], cs[:, :], start=True, stop=True).then_inc(att_full, 1)

            def keys_by_position(p, j, c):
                to = fill(p, j, 4 + c)
                pe.matmul(to[:, :], cs[:, c * P:(c + 1) * P], wk_hi[:, :], start=True, stop=False)
                pe.matmul(to[:, :], cs[:, c * P:(c + 1) * P], wk_lo[:, :], start=False, stop=False)
                pe.wait_ge(kdiag_done, PRIMED + 2 * p + j + 1)
                pe.matmul(to[:, :], ones_r[:, :], kdiag[:, :, :].rearrange("p c k -> p (c k)"),
                          start=False, stop=True).then_inc(att_full, 1)

            def keys_times_context(p, j, c):
                if c == 0:
                    fill(p, j, 8)
                    drained(p, j, 7)
                    pe.wait_ge(ctx1_in, 32 * p + 16 * j + 16)
                bank, _ = bank_of(ATT_B * j + 8)
                mm = pe.matmul(att[bank][0:65, :], ctx1[:, c, :], ek[:, c, :], start=(c == 0), stop=(c == KC - 1))
                if c == KC - 1:
                    mm.then_inc(att_full, 1)

            def context_matrix(p, j, k):
                drained(p, j, 8)
                to = fill(p, j, 9 + k)
                for c in range(2):
                    h = 2 * k + c
                    mm = pe.matmul(to[:, c * (P + 1):(c + 1) * (P + 1)], gt[0:65, h * P:(h + 1) * P],
                                   ucat[0:65, h, :], start=True, stop=True)
                mm.then_inc(att_full, 1)

            def queries_by_position(p, j, c):
                to = fill(p, j, 11 + c)
                pe.wait_ge(s_in, 32 * p + 32)
                pe.matmul(to[:, :], s_hl[j][:, c * P:(c + 1) * P], wq_hi[:, :],
                          start=True, stop=True).then_inc(att_full, 1)

            def query_maxima(p, j):
                to = fill(p, j, 15)
                drained(p, j, 14)
                for c in range(KC):
                    mm = pe.transpose(to[0:HEADS, c * P:(c + 1) * P], qm[:, c, :], ident[:, :])
                mm.then_inc(att_full, 1)

            def queries_by_channel(p, j, c):
                to = fill(p, j, 16 + c)
                drained(p, j, 15)
                pe.matmul(to[:, :], wq_hi[:, c * P:(c + 1) * P], s_hl[j][:, :], start=True, stop=False)
                pe.matmul(to[:, :], wq_lo[:, c * P:(c + 1) * P], s_hl[j][:, :], start=False, stop=False)
                pe.matmul(to[:, :], pick[:, c, :], qrow[:, :], start=False, stop=True).then_inc(att_full, 1)

            def query_sums(p, j, c):
                to = fill(p, j, 20 + c)
                drained(p, j, 16 + c)
                pe.matmul(to[:, :], blocks[:, :], eq[:, c, :], start=True, stop=True).then_inc(att_full, 1)

            def attention_out(p, j, c):
                if c == 0:
                    fill(p, j, 24)
                bank, _ = bank_of(ATT_B * j + 24)
                pe.wait_ge(eq_done, PRIMED + 8 * p + 4 * j + c + 1)
                mm = pe.matmul(att[bank][:, :], mt[j][:, c, :], eq[:, c, :], start=(c == 0), stop=(c == KC - 1))
                if c == KC - 1:
                    mm.then_inc(att_full, 1)

            def norm_of_out(p):
                pe.wait_ge(usq_done, p + 1)
                pe.wait_ge(att_free[0], PRIMED + 26 * p + 25)
                pe.matmul(att[0][:, :], blocks[:, :], rn[:, :], start=True, stop=True).then_inc(att_full, 1)

            def attention_beside(p, s):
                c = s % KC
                if s < 4:
                    query_sums(p, 0, c)
                elif s < 8:
                    attention_out(p, 0, c)
                elif s < 12:
                    keys_by_channel(p, 1, c)
                elif s < 16:
                    keys_by_position(p, 1, c)
                elif s < 20:
                    keys_times_context(p, 1, c)
                elif s == 20:
                    context_matrix(p, 1, 0)
                    context_matrix(p, 1, 1)
                elif s < 25:
                    queries_by_position(p, 1, s - 21)
                elif s == 25:
                    query_maxima(p, 1)
                elif s < 30:
                    queries_by_channel(p, 1, s - 26)
                elif s < 34:
                    query_sums(p, 1, s - 30)
                else:
                    attention_out(p, 1, 2 * (s - 34))
                    attention_out(p, 1, 2 * (s - 34) + 1)

            def turn(i, p):
                mamba, attention = i is not None, p is not None
                if mamba:
                    project(i)
                if attention:
                    for c in range(KC):
                        keys_by_channel(p, 0, c)
                if mamba:
                    ssm_by_channel(i)
                if attention:
                    for c in range(KC):
                        keys_by_position(p, 0, c)
                if mamba:
                    ssm_by_token(i)
                if attention:
                    for c in range(KC):
                        keys_times_context(p, 0, c)
                if mamba:
                    dt_input(i)
                if attention:
                    context_matrix(p, 0, 0)
                    context_matrix(p, 0, 1)
                if mamba:
                    dt_projection(i)
                if attention:
                    for c in range(KC):
                        queries_by_position(p, 0, c)
                    query_maxima(p, 0)
                    for c in range(KC):
                        queries_by_channel(p, 0, c)
                if mamba:
                    du_by_token(i)
                for s in range(STEPS):
                    if mamba and s < SCANS:
                        drives(i, s)
                    if mamba and s >= GC:
                        states_by_token(i, s - GC)
                    if attention:
                        attention_beside(p, s)
                if mamba:
                    sums_by_channel(i)
                if attention:
                    norm_of_out(p)
                if mamba:
                    project_out(i)

            turn(0, None)
            with pe.Fori(1, PAIRS) as i:
                turn(i, i - 1)
            turn(None, PAIRS - 1)

            for t in range(TC):
                pe.wait_ge(f_in[t % 4], 16 * (t // 4 + 1))
                if t >= 2:
                    pe.wait_ge(f_lo, t - 1)
                for c in range(KC):
                    mm = pe.transpose(front[t % 2][:, c * P:(c + 1) * P], x2_in[t % 4][:, c * P:(c + 1) * P], ident[:, :])
                mm.then_inc(f_full, 1)
            pe.wait_ge(f_lo, TC)
            for f in range(FC):
                pe.wait_ge(gu_done, f + 1)
                for h in range(HALVES):
                    n = f * HALVES + h
                    for s, banks, free, full in ((0, drive, gate_done, gate_full), (1, turned, hid_done, up_full)):
                        if n >= 2:
                            pe.wait_ge(free, n - 1)
                        for k in range(KC):
                            for part in (x2t_hi, x2t_lo):
                                mm = pe.matmul(banks[n % 2][:, :], gu[:, f % WR, s, k, :],
                                               part[:, k, h * HALF:(h + 1) * HALF],
                                               start=(k == 0 and part is x2t_hi), stop=(k == KC - 1 and part is x2t_lo))
                        mm.then_inc(full, 1)
            pe.wait_ge(hid_hi_done, FC * HALVES)
            pe.wait_ge(hid_lo_done, FC * HALVES)
            for t in range(TC):
                if t >= 2:
                    pe.wait_ge(ln3_step, 4 * (t - 2) + 1)
                for f in range(FC):
                    if t == 0:
                        pe.wait_ge(dw_done, f + 1)
                    for part in (hid_hi, hid_lo):
                        mm = pe.matmul(att[t % 2][:, :], part[:, f, t * P:(t + 1) * P], dw[:, f, :],
                                       start=(f == 0 and part is hid_hi), stop=(f == FC - 1 and part is hid_lo))
                mm.then_inc(down_full, 1)


def lay_out(a):
    c = np.ascontiguousarray
    x, ctx = a["x"].reshape(TOK, H), a["ctx_4096"]

    def by_part(w):
        return c(w.reshape(-1, P, w.shape[1]).transpose(1, 0, 2))

    def col(v):
        return c(v.reshape(-1, P).T)

    def blocks_t(w):
        return c(w.reshape(FC, P, KC, P).transpose(0, 3, 2, 1))

    return {
        "x_tok": c(x.reshape(PAIRS, P, H)),
        "x_t": c(x.reshape(PAIRS, P, KC, P).transpose(0, 3, 2, 1)),
        "ctx": c(ctx),
        "ctx_t": c(ctx.reshape(B, L, KC, P).transpose(0, 3, 2, 1)),
        "w_in": c(a["L0_attn_W_in"].T.reshape(KC, P, 2 * DI)),
        "conv_w": by_part(a["L0_attn_conv_w"]),
        "conv_b": col(a["L0_attn_conv_b"]),
        "w_x": by_part(a["L0_attn_W_x"].T),
        "w_dt": c(a["L0_attn_W_dt"].T),
        "b_dt": col(a["L0_attn_b_dt"]),
        "a_log": by_part(a["L0_attn_A_log"]),
        "d_skip": col(a["L0_attn_D"]),
        "w_out": by_part(a["L0_attn_W_out"].T),
        "wq": c(a["L0_xattn_Wq"].T),
        "wk": c(a["L0_xattn_Wk"].T),
        "wv": by_part(a["L0_xattn_Wv"]),
        "wo": by_part(a["L0_xattn_Wo"].T),
        "bo": c(a["L0_xattn_bo"].reshape(64, 1)),
        "gain": c(a["L0_xattn_g"].reshape(64, 1)),
        "gate_w": blocks_t(a["L0_ffn_gate_t"]),
        "up_w": blocks_t(a["L0_ffn_up_t"]),
        "down_w": c(a["L0_ffn_down_t"].T.reshape(FC, P, H)),
        "gate_s": col(a["L0_ffn_gate_s"]),
        "up_s": col(a["L0_ffn_up_s"]),
        "down_s": c(a["L0_ffn_down_s"]),
    }


def kernel(**inputs):
    import concourse.bacc as bacc
    from concourse.bass_utils import run_bass_kernel_spmd

    arrays = lay_out({k: np.asarray(v) for k, v in inputs.items()})
    nc = bacc.Bacc("TRN2", target_bir_lowering=False, num_devices=1)
    args = [nc.dram_tensor(f"in_{k}", v.shape, mybir.dt.from_np(v.dtype), kind="ExternalInput").ap()
            for k, v in arrays.items()]
    out = nc.dram_tensor("out", (TC, P, H), F32, kind="ExternalOutput").ap()
    decoder_kernel(nc, *args, out)
    r = run_bass_kernel_spmd(nc, [{f"in_{k}": v for k, v in arrays.items()}], core_ids=[0])
    return r.results[0]["out"].reshape(B, L, H)
```

```python
from contextlib import ExitStack

import numpy as np

import concourse.bass as bass
from concourse import mybir

F32 = mybir.dt.float32
F32R = mybir.dt.float32r
I32 = mybir.dt.int32
ALU = mybir.AluOpType
ACT = mybir.ActivationFunctionType
AX_X = mybir.AxisListType.X

P = 128
B, L, H = 16, 64, 512
PAIRS = B // 2
KC = H // P
DI, NS, RK = 1024, 16, 32
DC = DI // P
TAPS = 4
HEADS, DH = 8, 64
GN = 4
NG = NS // GN
GC = 4
NGC = DC // GC
ITEMS = NG * NGC
SCANS = ITEMS * GC
STEPS = SCANS + GC
FF = 1792
FC = FF // P
HALF = 512
TOK = B * L
TC = TOK // P
HALVES = TOK // HALF
WR = 2
LN_EPS, RMS_EPS = 1e-5, 1e-6
NORM_SCALE = 2.0 ** 20

RING = 8
DRING = 4
LEAD = 3
AHEAD = 2
PRIMED = 1




def begins(i):
    return not isinstance(i, int) or i < PAIRS - 1


def scans(i):
    return not isinstance(i, int) or 0 <= i < PAIRS


def ends(i):
    return not isinstance(i, int) or i > 0


F_SUM, F_CONV0, F_OUT, F_CONV1, F_GATE, F_SSM, F_TOKEN, F_DT_IN, F_DT, F_DU, F_ALL = 0, 2, 3, 4, 5, 7, 8, 9, 10, 12, 16
A_KEY, A_POS, A_CTX, A_MAT, A_KEYS = 0, 4, 8, 9, 11
A_QPOS, A_QMAX, A_QCH, A_SUM, A_OUT, A_QUERIES = 0, 4, 5, 9, 13, 14
A_NORM = 2 * A_KEYS + 2 * A_QUERIES
A_ALL = A_NORM + 1


def key_use(j, n):
    return A_KEYS * j + n


def query_use(j, n):
    return 2 * A_KEYS + A_QUERIES * j + n


def front_uses(t):
    tail = (F_SUM, F_SUM + 1, F_OUT)
    return [n for n in range(F_ALL) if (ends(t) if n in tail else begins(t))]


def att_uses(t):
    return [n for n in range(A_ALL) if (ends(t) if n >= 2 * A_KEYS else scans(t))]


def place(uses, i, n):
    t, bank = (i if isinstance(i, int) else 1), n % 2
    before = [m for s in range(-1, t) for m in uses(s)] + [m for m in uses(t) if m < n]
    own = [m for m in before if m % 2 == bank]
    if isinstance(i, int):
        return bank, len(before), len(own)
    return bank, len(uses(1)) * (i - 1) + len(before), sum(m % 2 == bank for m in uses(1)) * (i - 1) + len(own)


def decoder_kernel(nc, x_tok, x_t, ctx, ctx_t, w_in, conv_w, conv_b, w_x, w_dt, b_dt, a_log, d_skip, w_out,
                   wq, wk, wv, wo, bo, gain, gate_w, up_w, down_w, gate_s, up_s, down_s, out):
    x2_dram = nc.dram_tensor("x2_scratch", [PAIRS, P, H], F32).ap()
    with ExitStack() as whole:
        def sem(name):
            return whole.enter_context(nc.semaphore(name))

        def sb(name, shape, dt=F32, scope=whole):
            return scope.enter_context(nc.sbuf_tensor(name, shape, dt))

        front = [whole.enter_context(nc.psum_tensor(f"front{i}", [P, 512], F32)) for i in range(2)]
        drive = [whole.enter_context(nc.psum_tensor(f"drive{i}", [P, 512], F32)) for i in range(2)]
        turned = [whole.enter_context(nc.psum_tensor(f"turned{i}", [P, 512], F32)) for i in range(2)]
        att = [whole.enter_context(nc.psum_tensor(f"att{i}", [P, 512], F32)) for i in range(2)]

        ident = sb("ident", [P, P])
        eps_ln, eps_rms = sb("eps_ln", [P, 1]), sb("eps_rms", [P, 1])
        gs_sb, us_sb = sb("gs_sb", [P, FC]), sb("us_sb", [P, FC])

        loop_mem = whole.enter_context(ExitStack())

        def lb(name, shape, dt=F32):
            return sb(name, shape, dt, loop_mem)

        blocks = lb("blocks", [P, P])
        ones_r = lb("ones_r", [P, P], F32R)
        two_eyes = lb("two_eyes", [P, L])
        pick = lb("pick", [P, KC, P], F32R)
        cw, cb = lb("cw", [P, DC, TAPS]), lb("cb", [P, DC])
        bdt, dsk = lb("bdt", [P, DC]), lb("dsk", [P, DC])
        neg_a = lb("neg_a", [P, DC, NS])
        bo_sb, g8 = lb("bo_sb", [P, 1]), lb("g8", [P, 1])
        win = lb("win", [P, KC, 2 * DI])
        wx = lb("wx", [P, DC, 64])
        wdt = lb("wdt", [P, DI])
        wout = lb("wout", [P, DC, H])
        wq_hi, wq_lo = lb("wq_hi", [P, H], F32R), lb("wq_lo", [P, H], F32R)
        wk_hi, wk_lo = lb("wk_hi", [P, H], F32R), lb("wk_lo", [P, H], F32R)
        ucat = lb("ucat", [P, KC, P + 1])

        xt = lb("xt", [P, KC, P])
        xs, sg = ([lb(f"{n}{b}", [P, DC, P]) for b in range(2)] for n in ("xs", "sg"))
        ssm, ssm2 = lb("ssm", [P, P]), lb("ssm2", [P, 2, 2, L])
        tr, sq3 = lb("tr", [P, 3, 64]), lb("sq3", [P, 3, 64])
        rms = lb("rms", [P, 4])
        tsn, c_col = lb("tsn", [P, RK]), [lb(f"c_col{b}", [P, NS]) for b in range(2)]
        b_nrm = lb("b_nrm", [P, 2, NS])
        b_hi, b_lo = lb("b_hi", [P, 2, NS]), lb("b_lo", [P, 2, NS])
        diag_hi, diag_lo = lb("diag_hi", [P, 2, NS, L], F32R), lb("diag_lo", [P, 2, NS, L], F32R)
        tst = lb("tst", [P, P])
        dt = [lb(f"dt{b}", [P, DC, P]) for b in range(2)]
        du = lb("du", [P, DC, P])
        du_t = lb("du_t", [P, 2, DC, P], F32R)
        decay = lb("decay", [P, DRING, GN, 2, L])
        state = lb("state", [P, RING, GN, P])
        acc = lb("acc", [P, DI])
        x1 = lb("x1", [P, H])
        bn, mv, rstd = lb("bn", [P, 6]), lb("mv", [P, 2]), lb("rstd", [P, 1])
        du_hl = state[:, 0:4, :, :].rearrange("p r g t -> p (r g t)").rearrange(
            "p (c b s l) -> p c b s l", c=DC, b=2, s=2)
        y = du

        c2, cs = lb("c2", [P, H]), lb("cs", [P, H], F32R)
        ctx1 = lb("ctx1", [P, KC, 65])
        km, nkm = lb("km", [P, KC]), lb("nkm", [P, KC])
        kdiag = lb("kdiag", [P, KC, P], F32R)
        ek, eq = lb("ek", [P, KC, H]), lb("eq", [P, KC, H])
        gt = lb("gt", [P, H])
        rz = lb("rz", [P, 4])
        mt = [[lb(f"mt{b}{j}", [P, KC, P]) for j in range(2)] for b in range(2)]
        s_hl = [lb(f"s_hl{j}", [P, H], F32R) for j in range(2)]
        s_tmp = lb("s_tmp", [P, H], F32R)
        qm = lb("qm", [P, KC, HEADS])
        qrow = lb("qrow", [P, H], F32R)
        rq, u2, rn = lb("rq", [P, 2, H]), lb("u2", [P, H]), lb("rn", [P, H])
        bn2, mv2, rstd2 = lb("bn2", [P, 6]), lb("mv2", [P, 2]), lb("rstd2", [P, 1])
        wq_raw, wk_raw = rn, u2
        wv_raw = ek[:, 0, 0:KC * 64].rearrange("p (c j) -> p c j", c=KC)
        wo_raw = ek[:, 1, :].rearrange("p (c j) -> p c j", c=KC)
        pick_raw = eq[:, 0, :].rearrange("p (c j) -> p c j", c=KC)
        ones_raw = eq[:, 1, 0:P]
        loop_mem.close()

        hid_mem = whole.enter_context(ExitStack())
        hid_hi = sb("hid_hi", [P, FC, TOK], F32R, hid_mem)
        hid_lo = sb("hid_lo", [P, FC, TOK], F32R, hid_mem)
        dw_raw = sb("dw_raw", [P, FC, H], I32, hid_mem)
        ds_sb = sb("ds_sb", [P, H], F32, hid_mem)
        up_mem = whole.enter_context(ExitStack())
        x2t_hi = sb("x2t_hi", [P, KC, TOK], F32R, up_mem)
        x2t_lo = sb("x2t_lo", [P, KC, TOK], F32R, up_mem)
        gu_raw = sb("gu_raw", [P, WR, 2, KC, P], I32, up_mem)
        gu = sb("gu", [P, WR, 2, KC, P], F32R, up_mem)
        gate = sb("gate", [P, 2, HALF], F32, up_mem)
        hid = sb("hid", [P, 2, HALF], F32, up_mem)
        x2_in = [gate[:, 0, :], gate[:, 1, :], hid[:, 0, :], hid[:, 1, :]]
        up_mem.close()
        down_mem = whole.enter_context(ExitStack())
        dw = sb("dw", [P, FC, H], F32R, down_mem)
        x2_res = sb("x2_res", [P, 2, H], F32, down_mem)
        r3 = sb("r3", [P, 2, H], F32, down_mem)
        y3 = sb("y3", [P, 2, H], F32, down_mem)
        bn3, mv3, rstd3 = sb("bn3", [P, 2, 6], F32, down_mem), sb("mv3", [P, 2, 2], F32, down_mem), sb("rstd3", [P, 2, 1], F32, down_mem)
        down_mem.close()

        par_in, win_in, wout_in = sem("par_in"), sem("win_in"), sem("wout_in")
        xt_in, xtok_in, ctx_in, ctx1_in = sem("xt_in"), sem("xtok_in"), sem("ctx_in"), sem("ctx1_in")
        const_step, const_done, setup_act, setup_vec, setup_pe = (
            sem("const_step"), sem("const_done"), sem("setup_act"), sem("setup_vec"), sem("setup_pe"))
        front_full, drive_full = sem("front_full"), sem("drive_full")
        turned_full, att_full = sem("turned_full"), sem("att_full")
        front_free = [sem("front_free0"), sem("front_free1")]
        att_free = [sem("att_free0"), sem("att_free1")]
        taps_done, conv_step, xs_done = sem("taps_done"), sem("conv_step"), sem("xs_done")
        sq3_done, rms_step = sem("sq3_done"), sem("rms_step")
        diag_done = sem("diag_done")
        log_step, dt_done, du_done, du_hi = sem("log_step"), sem("dt_done"), sem("du_done"), sem("du_hi")
        du_lo = sem("du_lo")
        decay_done, scan_done, mix_done = sem("decay_done"), sem("scan_done"), sem("mix_done")
        y_done, ln1_step, x1_done = sem("y_done"), sem("ln1_step"), sem("x1_done")
        cs_hi, cs_lo = sem("cs_hi"), sem("cs_lo")
        km_done, kdiag_done = sem("km_done"), sem("kdiag_done")
        rz_step = sem("rz_step")
        s_hi, s_lo, s_in = sem("s_hi"), sem("s_lo"), sem("s_in")
        rms_root, ln1_root, ln2_root, ln3_root = sem("rms_root"), sem("ln1_root"), sem("ln2_root"), sem("ln3_root")
        norm_step, rq_done = sem("norm_step"), sem("rq_done")
        eq_done = sem("eq_done")
        usq_done, ln2_step, x2_done, x2_out = sem("usq_done"), sem("ln2_step"), sem("x2_done"), sem("x2_out")
        x2_stored = sem("x2_stored")
        f_in = [sem(f"f_in{k}") for k in range(4)]
        f_full, f_hi, f_lo = sem("f_full"), sem("f_hi"), sem("f_lo")
        gu_in = [sem(f"gu_in{k}") for k in range(WR)]
        gu_done, gate_full, up_full, gate_done, hid_done = (
            sem("gu_done"), sem("gate_full"), sem("up_full"), sem("gate_done"), sem("hid_done"))
        hid_hi_done, hid_lo_done, dw_in, dw_done = sem("hid_hi_done"), sem("hid_lo_done"), sem("dw_in"), sem("dw_done")
        res_in = [sem("res_in0"), sem("res_in1")]
        down_full, ln3_step, y3_done = sem("down_full"), sem("ln3_step"), sem("y3_done")
        out_done = [sem("out_done0"), sem("out_done1")]

        block = whole.enter_context(nc.Block())
        N_PAR = 26

        @block.sync
        def _(sp):
            def load(dst, src, to=par_in):
                sp.dma_start(dst, src).then_inc(to, 16)

            for k in range(KC):
                load(win[:, k, :], w_in[k], win_in)
            load(cw[:, :, :], conv_w)
            load(cb[:, :], conv_b)
            load(bdt[:, :], b_dt)
            load(dsk[:, :], d_skip)
            load(neg_a[:, :, :], a_log)
            load(wx[:, :, :], w_x)
            load(wq_raw[0:64, :], wq)
            load(wq_raw[64:P, :], wq)
            load(wk_raw[0:64, :], wk)
            load(wk_raw[64:P, :], wk)
            load(wv_raw, wv)
            sp.wait_ge(const_done, 1)
            load(wdt[0:RK, :], w_dt)
            for c in range(KC):
                for j in range(2):
                    load(wo_raw[64 * j:64 * j + 64, c, 64 * j:64 * j + 64], wo[64 * j:64 * j + 64, c, :])
            load(bo_sb[0:64, :], bo)
            load(bo_sb[64:P, :], bo)
            load(g8[0:64, :], gain)
            load(g8[64:P, :], gain)
            load(gs_sb[:, :], gate_s)
            load(us_sb[:, :], up_s)
            load(wout[:, :, :], w_out, wout_in)

            def load_tokens(q):
                sp.wait_ge(xs_done, PRIMED + 2 * q)
                load(xt[:, :, :], x_t[q], xt_in)

            def load_residual(p):
                sp.wait_ge(x2_done, PRIMED + p)
                load(x1[:, :], x_tok[p], xtok_in)

            def load_context(i, j):
                sp.wait_ge(cs_lo, PRIMED + 2 * i + j)
                load(c2[0:64, :], ctx[2 * i + j], ctx_in)
                load(c2[64:P, :], ctx[2 * i + j], ctx_in)
                sp.wait_ge(rz_step, PRIMED + 4 * i + 2 * j)
                load(ctx1[:, :, 0:64], ctx_t[2 * i + j], ctx1_in)

            def move_parts(p):
                sp.wait_ge(s_lo, p + 1)
                load(s_hl[0][64:P, :].bitcast(F32), s_tmp[0:64, :].bitcast(F32), s_in)
                load(s_hl[1][0:64, :].bitcast(F32), s_tmp[64:P, :].bitcast(F32), s_in)

            def turn(i):
                if begins(i):
                    load_tokens(i + 1)
                if scans(i):
                    load_context(i, 0)
                if ends(i):
                    load_residual(i - 1)
                if scans(i):
                    load_context(i, 1)
                if ends(i):
                    move_parts(i - 1)

            turn(-1)
            turn(0)
            with sp.Fori(0, (PAIRS - 2) // 2) as r:
                turn(2 * r + 1)
                turn(2 * r + 2)
            turn(PAIRS - 1)
            turn(PAIRS)

            sp.wait_ge(x2_out, 16 * PAIRS)
            sp.wait_ge(att_full, PRIMED + place(att_uses, PAIRS, A_ALL)[1])
            for t in range(TC):
                if t >= 4:
                    sp.wait_ge(f_lo, t - 3)
                load(x2_in[t % 4], x2_dram[t], f_in[t % 4])
            for f in range(FC):
                if f == 0:
                    load(ds_sb[:, :], down_s.partition_broadcast(P), dw_in)
                if f >= WR:
                    sp.wait_ge(gu_done, f - WR + 1)
                load(gu_raw[:, f % WR, 0, :, :], gate_w[f], gu_in[f % WR])
                load(gu_raw[:, f % WR, 1, :, :], up_w[f], gu_in[f % WR])
                load(dw_raw[:, f, :], down_w[f], dw_in)
            for t in range(TC):
                if t < 2:
                    sp.wait_ge(up_full, HALVES * FC)
                    sp.wait_ge(hid_lo_done, HALVES * FC)
                else:
                    sp.wait_ge(ln3_step, 4 * (t - 2) + 2)
                load(x2_res[:, t % 2, :], x2_dram[t], res_in[t % 2])

        @block.gpsimd
        def _(pool):
            for counter in (xs_done, front_full, *front_free, cs_lo, rz_step, drive_full, scan_done, mix_done, diag_done, y_done,
                            turned_full, eq_done, x2_done, decay_done, kdiag_done, att_full, *att_free, x2_stored):
                pool.sem_inc(counter, PRIMED)
            pool.memset(ident[:, :], 0.0)
            pool.memset(eps_ln[:, :], LN_EPS)
            pool.memset(eps_rms[:, :], RMS_EPS)
            pool.memset(two_eyes[:, :], 0.0)
            pool.memset(pick_raw, 0.0)
            pool.memset(ones_raw, 1.0)
            pool.memset(ek[:, 1, :], 0.0)
            pool.memset(blocks[:, :], 0.0)
            pool.memset(wdt[:, :], 0.0).then_inc(const_step, 1)
            pool.wait_ge(const_step, 1)
            pool.affine_select(out=ident[:, :], in_=ident[:, :], compare_op=ALU.not_equal, fill=1.0, base=0,
                               pattern=[[-1, P]], channel_multiplier=1)
            pool.affine_select(out=pick_raw, in_=pick_raw, compare_op=ALU.not_equal, fill=-1.0, base=0,
                               pattern=[[-2, KC], [-1, 2], [0, 64]], channel_multiplier=1)
            pool.affine_select(out=two_eyes[:, :], in_=two_eyes[:, :], compare_op=ALU.not_equal, fill=1.0, base=0,
                               pattern=[[-1, L]], channel_multiplier=1).then_inc(const_step, 1)
            pool.wait_ge(const_step, 2)
            pool.affine_select(out=two_eyes[:, :], in_=two_eyes[:, :], compare_op=ALU.not_equal, fill=1.0, base=-L,
                               pattern=[[-1, L]], channel_multiplier=1)
            pool.memset(blocks[0:64, 0:64], 1.0)
            pool.memset(tst[:, :], 0.0)
            pool.memset(ssm[:, :], 0.0)
            pool.memset(ssm2[:, :, :, :], 0.0)
            pool.memset(decay[:, :, :, :, :].rearrange("p r n b l -> p (r n b l)"), 0.0)
            pool.memset(qrow[:, :].bitcast(F32), 0.0)
            for b in range(2):
                for j in range(2):
                    pool.memset(mt[b][j][:, :, :], 0.0)
            pool.memset(ctx1[:, :, 64:65], 1.0)
            pool.memset(ucat[:, :, :], 0.0).then_inc(const_step, 1)
            pool.wait_ge(const_step, 3)
            pool.memset(blocks[64:P, 64:P], 1.0)
            pool.memset(ucat[64:65, :, P:P + 1], 1.0).then_inc(const_done, 1)
            pool.wait_ge(const_done, 1)

            def diagonals(q):
                pool.wait_ge(rms_step, 6 * q + 6)
                pool.wait_ge(drive_full, PRIMED + SCANS * q)
                for g in range(NG):
                    for b in range(2):
                        for part, diag in ((b_hi, diag_hi), (b_lo, diag_lo)):
                            pool.tensor_tensor(
                                diag[:, b, g * GN:(g + 1) * GN, :],
                                two_eyes[:, :].unsqueeze(1).to_broadcast([P, GN, L]),
                                part[:, b, g * GN:(g + 1) * GN].unsqueeze(2).to_broadcast([P, GN, L]),
                                ALU.mult).then_inc(diag_done, 1)

            def maxima(i, j):
                pool.wait_ge(km_done, 2 * i + j + 1)
                pool.wait_ge(rz_step, PRIMED + 4 * i + 2 * j)
                pool.tensor_tensor(
                    kdiag[:, :, :], ident[:, :].unsqueeze(1).to_broadcast([P, KC, P]),
                    nkm[:, :].unsqueeze(2).to_broadcast([P, KC, P]), ALU.mult).then_inc(kdiag_done, 1)

            def store_x2(p):
                pool.wait_ge(x2_done, PRIMED + p + 1)
                pool.dma_start(x2_dram[p], u2[:, :]).then_inc(x2_out, 16)
                pool.wait_ge(x2_out, 16 * p + 16)
                pool.sem_inc(x2_stored, 1)

            def turn(i):
                if scans(i):
                    maxima(i, 0)
                    maxima(i, 1)
                if begins(i):
                    diagonals(i + 1)
                if ends(i):
                    store_x2(i - 1)

            turn(-1)
            turn(0)
            with pool.Fori(0, (PAIRS - 2) // 2) as r:
                turn(2 * r + 1)
                turn(2 * r + 2)
            turn(PAIRS - 1)
            turn(PAIRS)

            for f in range(FC):
                for h in range(HALVES):
                    n = f * HALVES + h
                    pool.wait_ge(hid_hi_done, n + 1)
                    pool.tensor_tensor(hid_lo[:, f, h * HALF:(h + 1) * HALF], hid[:, n % 2, :],
                                       hid_hi[:, f, h * HALF:(h + 1) * HALF].bitcast(F32),
                                       ALU.subtract).then_inc(hid_lo_done, 1)
            for t in range(TC):
                pool.wait_ge(y3_done, t + 1)
                pool.dma_start(out[t], y3[:, t % 2, :]).then_inc(out_done[t % 2], 16)
            for k in range(2):
                pool.wait_ge(out_done[k], 16 * TC // 2)

        @block.scalar
        def _(act):
            act.preload_act_table_set("natural_log_exp_and_others")
            act.wait_ge(par_in, 16 * N_PAR)
            act.wait_ge(const_done, 1)
            act.activation(neg_a[:, :, :], neg_a[:, :, :], ACT.Exp).then_inc(setup_act, 1)
            act.activation(wq_hi[:, :], wq_raw[:, :], ACT.Copy).then_inc(setup_act, 1)
            act.activation(wk_hi[:, :], wk_raw[:, :], ACT.Copy).then_inc(setup_act, 1)
            act.activation(pick[:, :, :], pick_raw, ACT.Copy).then_inc(setup_act, 1)
            act.activation(ones_r[:, :], ones_raw, ACT.Copy).then_inc(setup_act, 1)
            act.wait_ge(setup_pe, 1)
            act.activation(ucat[0:64, :, 0:P], att[0][0:64, :].rearrange("p (c j) -> p c j", c=KC),
                           ACT.Copy).then_inc(setup_act, 1)
            act.wait_ge(setup_vec, 1)

            def inverse_root(to, var, eps, step, before):
                act.activation(to, var, ACT.Ln, bias=eps).then_inc(step, 1)
                act.wait_ge(step, before + 1)
                act.activation(to, to, ACT.Exp, scale=-0.5).then_inc(step, 1)

            def front_filled(i, n):
                bank, before, _ = place(front_uses, i, n)
                act.wait_ge(front_full, PRIMED + before + 1)
                return front[bank], front_free[bank]

            def front_read(i, n):
                bank, _, own = place(front_uses, i, n)
                act.wait_ge(front_free[bank], PRIMED + own + 1)

            def att_filled(i, n):
                bank, before, _ = place(att_uses, i, n)
                act.wait_ge(att_full, PRIMED + before + 1)
                return att[bank], att_free[bank]

            def att_read(i, n):
                bank, _, own = place(att_uses, i, n)
                act.wait_ge(att_free[bank], PRIMED + own + 1)

            def last_tap(i, nxt, h):
                held, _ = front_filled(i, (F_CONV0, F_CONV1)[h])
                act.wait_ge(y_done, PRIMED + 2 * max(i, 0) if isinstance(i, int) else PRIMED + 2 * i)
                for c in range(4):
                    d = 4 * h + c
                    tap = act.activation(xs[nxt][:, d, :], held[:, c * P:(c + 1) * P], ACT.Identity,
                                         bias=cb[:, d:d + 1], scale=cw[:, d, TAPS - 1:TAPS])
                tap.then_inc(taps_done, 1)

            def silus(i, nxt):
                for h in range(2):
                    held, free = front_filled(i, F_GATE + h)
                    act.activation(sg[nxt][:, 4 * h:4 * h + 4, :], held[:, :].rearrange("p (c t) -> p c t", c=4),
                                   ACT.Silu).then_inc(free, 1)
                for h in range(2):
                    front_read(i, (F_CONV0, F_CONV1)[h])
                    act.activation(xs[nxt][:, 4 * h:4 * h + 4, :], xs[nxt][:, 4 * h:4 * h + 4, :],
                                   ACT.Silu).then_inc(xs_done, 1)
                act.preload_act_table_set("natural_log_exp_and_others")

            def ssm_by_channel(i):
                held, free = front_filled(i, F_SSM)
                act.activation(ssm[0:64, :], held[0:64, 0:P], ACT.Copy)
                act.activation(ssm2[0:64, :, :, :], held[0:64, 0:P].rearrange("k (b l) -> k b l", b=2).unsqueeze(2)
                               .to_broadcast([64, 2, 2, L]), ACT.Copy).then_inc(free, 1)

            def ssm_by_token(i):
                held, free = front_filled(i, F_TOKEN)
                act.activation(tr[:, :, :], held[:, 0:3 * P].rearrange("p (s k) -> p s k", s=3)[:, :, 0:64],
                               ACT.Copy).then_inc(free, 1)
                front_read(i, F_TOKEN)
                act.activation(sq3[:, :, :], tr[:, :, :], ACT.Square).then_inc(sq3_done, 1)

            def root_rms(i):
                act.wait_ge(rms_step, 6 * (i + 1) + 2)
                inverse_root(rms[:, :], rms[:, :], eps_rms[:, :], rms_root, 2 * (i + 1))

            def dt_input(i):
                held, free = front_filled(i, F_DT_IN)
                act.activation(tst[0:RK, :], held[0:RK, 0:P], ACT.Copy).then_inc(free, 1)

            def softplus_abs(i, nxt):
                front_read(i, F_DT)
                front_read(i, F_DT + 1)
                act.activation(du[:, :, :], dt[nxt][:, :, :], ACT.Abs).then_inc(log_step, 1)

            def softplus_exp(i):
                act.wait_ge(log_step, 3 * (i + 1) + 1)
                act.activation(du[:, :, :], du[:, :, :], ACT.Exp, scale=-1.0).then_inc(log_step, 1)

            def softplus_log(i):
                act.wait_ge(log_step, 3 * (i + 1) + 2)
                act.activation(du[:, :, :], du[:, :, :], ACT.Ln, bias=1.0).then_inc(log_step, 1)

            def du_high_part(i):
                act.wait_ge(du_done, i + 2)
                if scans(i):
                    act.wait_ge(turned_full, PRIMED + SCANS * i + SCANS - GN)
                act.activation(du_hl[:, :, :, 0, :].bitcast(F32R), du[:, :, :].rearrange("p c (b l) -> p c b l", b=2),
                               ACT.Copy).then_inc(du_hi, 1)

            def du_by_token(i, k):
                held, free = front_filled(i, F_DU + k)
                act.wait_ge(drive_full, PRIMED + SCANS * (i + 1))
                act.activation(du_t[:, :, 2 * k:2 * k + 2, :], held[:, :].rearrange("p (b c d) -> p b c d", b=2, c=2),
                               ACT.Copy).then_inc(free, 1)

            def decays(i, par, u):
                g, d = u // DC, u % DC
                if isinstance(i, int) and SCANS * i + u < DRING:
                    act.wait_ge(const_done, 1)
                else:
                    act.wait_ge(scan_done, PRIMED + SCANS * i + u - DRING + 1)
                if u == 0:
                    act.wait_ge(dt_done, i + 1)
                for n in range(GN):
                    ins = act.activation(
                        decay[:, u % DRING, n, :, 1:L],
                        dt[par][:, d, :].rearrange("p (b l) -> p b l", b=2)[:, :, 1:L],
                        ACT.Exp, scale=neg_a[:, d, g * GN + n:g * GN + n + 1])
                ins.then_inc(decay_done, 1)

            def split_context(i, j):
                act.wait_ge(ctx_in, 64 * i + 32 * j + 32)
                if j == 1:
                    act.wait_ge(att_full, PRIMED + place(att_uses, i, key_use(0, A_CTX))[1])
                act.activation(cs[:, :], c2[:, :], ACT.Copy).then_inc(cs_hi, 1)

            def exp_keys(i, j, c):
                held, free = att_filled(i, key_use(j, A_POS + c))
                act.activation(ek[:, c, :], held[:, :], ACT.Exp).then_inc(free, 1)

            def keys_times_context(i, j):
                held, free = att_filled(i, key_use(j, A_CTX))
                act.activation(gt[0:65, :], held[0:65, :], ACT.Copy).then_inc(free, 1)

            def root_ln1(i):
                p = i - 1
                act.wait_ge(ln1_step, 2 * p + 2)
                inverse_root(rstd[:, :], mv[:, 1:2], eps_ln[:, :], ln1_root, 2 * p)

            def split_x1(i):
                act.wait_ge(x1_done, i)
                act.activation(s_hl[0][0:64, :], x1[0:64, :], ACT.Copy)
                act.activation(s_tmp[64:P, :], x1[64:P, :], ACT.Copy).then_inc(s_hi, 1)

            def query_maxima(i, j):
                held, free = att_filled(i, query_use(j, A_QMAX))
                act.activation(qrow[0:HEADS, :], held[0:HEADS, :], ACT.Copy).then_inc(free, 1)

            def exp_queries(i, j, c):
                held, free = att_filled(i, query_use(j, A_QCH + c))
                act.activation(eq[:, c, :], held[:, :], ACT.Exp).then_inc(free, 1)

            def inverse_sums(i, j, c):
                held, free = att_filled(i, query_use(j, A_SUM + c))
                act.wait_ge(eq_done, PRIMED + 8 * (i - 1) + 4 * j + max(c - 1, 0))
                act.activation(rq[:, c % 2, :], held[:, :], ACT.Ln).then_inc(free, 1)
                att_read(i, query_use(j, A_SUM + c))
                act.activation(rq[:, c % 2, :], rq[:, c % 2, :], ACT.Exp, scale=-1.0).then_inc(rq_done, 1)

            def attention_out(i, j):
                held, free = att_filled(i, query_use(j, A_OUT))
                act.wait_ge(x2_stored, PRIMED + i - 1)
                act.activation(u2[64 * j:64 * j + 64, :], held[64 * j:64 * j + 64, :], ACT.Identity,
                               bias=bo_sb[64 * j:64 * j + 64, :]).then_inc(free, 1)

            def norm_of_out(i):
                att_read(i, query_use(1, A_OUT))
                act.activation(rn[:, :], u2[:, :], ACT.Square).then_inc(usq_done, 1)

            def inverse_norm(i):
                att_read(i, A_NORM)
                act.activation(rn[:, :], rn[:, :], ACT.Ln, scale=NORM_SCALE).then_inc(norm_step, 1)
                act.wait_ge(norm_step, 2 * (i - 1) + 1)
                act.activation(rn[:, :], rn[:, :], ACT.Exp, scale=-0.5).then_inc(norm_step, 1)

            def root_ln2(i):
                act.wait_ge(ln2_step, 4 * (i - 1) + 4)
                inverse_root(rstd2[:, :], mv2[:, 1:2], eps_ln[:, :], ln2_root, 2 * (i - 1))

            def beside(i, par, s):
                nxt = 1 - par
                if scans(i):
                    if s in (0, 6):
                        split_context(i, s // 6)
                    if s in (4, 5, 12, 13):
                        for c in range(2):
                            exp_keys(i, s // 12, 2 * (s % 4 == 1) + c)
                    if s in (7, 15):
                        keys_times_context(i, s // 15)
                if ends(i):
                    if s == 10:
                        root_ln1(i)
                    if s == 11:
                        split_x1(i)
                    for j, first in ((0, 17), (1, 26)):
                        if s == first + 2:
                            query_maxima(i, j)
                        if s in (first + 3, first + 4):
                            for c in range(2):
                                exp_queries(i, j, 2 * (s - first - 3) + c)
                        if s in (first + 5, first + 6):
                            for c in range(2):
                                inverse_sums(i, j, 2 * (s - first - 5) + c)
                        if s == first + 8:
                            attention_out(i, j)
                    if s == 34:
                        norm_of_out(i)
                if begins(i):
                    if s in (3, 12):
                        last_tap(i, nxt, s // 12)
                    if s == 20:
                        silus(i, nxt)
                    if s == 22:
                        ssm_by_channel(i)
                    if s == 23:
                        ssm_by_token(i)
                    if s == 24:
                        root_rms(i)
                    if s == 26:
                        dt_input(i)
                    if s == 28:
                        softplus_abs(i, nxt)
                    if s == 29:
                        softplus_exp(i)
                    if s == 30:
                        softplus_log(i)
                    if s == 32:
                        du_high_part(i)
                    if s in (33, 34):
                        for k in range(2):
                            du_by_token(i, 2 * (s - 33) + k)
                if ends(i) and s == 35:
                    inverse_norm(i)

            def turn(i, par):
                for s in range(STEPS):
                    beside(i, par, s)
                    if scans(i) and s + LEAD < SCANS:
                        decays(i, par, s + LEAD)
                    if begins(i) and s + LEAD >= STEPS:
                        decays(i + 1, 1 - par, s + LEAD - STEPS)
                if ends(i):
                    root_ln2(i)

            turn(-1, 1)
            turn(0, 0)
            with act.Fori(0, (PAIRS - 2) // 2) as r:
                turn(2 * r + 1, 1)
                turn(2 * r + 2, 0)
            turn(PAIRS - 1, 1)
            turn(PAIRS, 0)

            for t in range(TC):
                act.wait_ge(f_full, t + 1)
                act.activation(x2t_hi[:, :, t * P:(t + 1) * P],
                               front[t % 2][:, :].rearrange("p (c t) -> p c t", c=KC), ACT.Copy).then_inc(f_hi, 1)

            def convert(f):
                act.wait_ge(gu_in[f % WR], 32 * (f // WR) + 32)
                if f >= WR:
                    act.wait_ge(up_full, HALVES * (f - WR + 1))
                act.activation(gu[:, f % WR, :, :, :].rearrange("p s c k -> p (s c k)"),
                               gu_raw[:, f % WR, :, :, :].rearrange("p s c k -> p (s c k)"),
                               ACT.Copy).then_inc(gu_done, 1)

            convert(0)
            for f in range(FC):
                if f + 1 < FC:
                    convert(f + 1)
                for h in range(HALVES):
                    n = f * HALVES + h
                    act.wait_ge(gate_full, n + 1)
                    if n >= 2:
                        act.wait_ge(hid_done, n - 1)
                    act.activation(gate[:, n % 2, :], drive[n % 2][:, :], ACT.Silu,
                                   scale=gs_sb[:, f:f + 1]).then_inc(gate_done, 1)
                    act.wait_ge(hid_done, n + 1)
                    act.activation(hid_hi[:, f, h * HALF:(h + 1) * HALF], hid[:, n % 2, :],
                                   ACT.Copy).then_inc(hid_hi_done, 1)
            act.preload_act_table_set("natural_log_exp_and_others")
            for t in range(TC):
                act.wait_ge(ln3_step, 4 * t + 4)
                inverse_root(rstd3[:, t % 2, :], mv3[:, t % 2, 1:2], eps_ln[:, :], ln3_root, 2 * t)

        @block.vector
        def _(dve):
            dve.wait_ge(par_in, 16 * N_PAR)
            dve.wait_ge(setup_act, 3)
            dve.tensor_tensor(wq_lo[:, :], wq_raw[:, :], wq_hi[:, :].bitcast(F32), ALU.subtract)
            dve.tensor_tensor(wk_lo[:, :], wk_raw[:, :], wk_hi[:, :].bitcast(F32), ALU.subtract)
            dve.tensor_scalar(g8[:, :], g8[:, :], float(np.sqrt(DH) * np.sqrt(NORM_SCALE)), None, ALU.mult)
            dve.tensor_scalar(neg_a[:, :, :], neg_a[:, :, :], -1.0, None, ALU.mult).then_inc(setup_vec, 1)

            def front_filled(i, n):
                bank, before, _ = place(front_uses, i, n)
                dve.wait_ge(front_full, PRIMED + before + 1)
                return front[bank], front_free[bank]

            def front_read(i, n):
                bank, _, own = place(front_uses, i, n)
                dve.wait_ge(front_free[bank], PRIMED + own + 1)

            def att_filled(i, n):
                bank, before, _ = place(att_uses, i, n)
                dve.wait_ge(att_full, PRIMED + before + 1)
                return att[bank], att_free[bank]

            def att_read(i, n):
                bank, _, own = place(att_uses, i, n)
                dve.wait_ge(att_free[bank], PRIMED + own + 1)

            def convolve(i, nxt, h, s):
                bank, _, _ = place(front_uses, i, (F_CONV0, F_CONV1)[h])
                if s == 1:
                    dve.wait_ge(taps_done, 2 * (i + 1) + h + 1)
                else:
                    dve.wait_ge(conv_step, 4 * (i + 1) + 2 * h + s - 1)
                for c in range(4):
                    d = 4 * h + c
                    new = xs[nxt][:, d, :].rearrange("p (b l) -> p b l", b=2)[:, :, s:L]
                    src = front[bank][:, c * P:(c + 1) * P].rearrange("p (b l) -> p b l", b=2)[:, :, 0:L - s]
                    tap = dve.scalar_tensor_tensor(out=new, in0=src, scalar=cw[:, d, TAPS - 1 - s:TAPS - s],
                                                   in1=new, op0=ALU.mult, op1=ALU.add)
                tap.then_inc(conv_step if s < TAPS - 1 else front_free[bank], 1)

            def ssm_squares(i):
                q = i + 1
                dve.wait_ge(sq3_done, q + 1)
                dve.tensor_reduce(rms[:, 0:1], sq3[:, 0, 0:RK], AX_X, ALU.add)
                dve.tensor_reduce(rms[:, 1:2], sq3[:, 0, RK + NS:64], AX_X, ALU.add)
                dve.tensor_reduce(rms[:, 2:4], sq3[:, 1:3, RK:RK + NS], AX_X, ALU.add).then_inc(rms_step, 1)
                dve.wait_ge(rms_step, 6 * q + 1)
                dve.tensor_scalar(rms[:, 0:1], rms[:, 0:1], 1.0 / RK, None, ALU.mult)
                dve.tensor_scalar(rms[:, 1:4], rms[:, 1:4], 1.0 / NS, None, ALU.mult).then_inc(rms_step, 1)

            def ssm_norms(i, nxt):
                q = i + 1
                dve.wait_ge(rms_root, 2 * q + 2)
                dve.tensor_scalar(tsn[:, :], tr[:, 0, 0:RK], rms[:, 0:1], None, ALU.mult).then_inc(rms_step, 1)
                dve.tensor_scalar(c_col[nxt][:, :], tr[:, 0, RK + NS:64], rms[:, 1:2], None, ALU.mult)
                for b in range(2):
                    ins = dve.tensor_scalar(b_nrm[:, b, :], tr[:, 1 + b, RK:RK + NS], rms[:, 2 + b:3 + b], None, ALU.mult)
                ins.then_inc(rms_step, 1)
                dve.wait_ge(rms_step, 6 * q + 4)
                dve.wait_ge(diag_done, PRIMED + 16 * q)
                dve.tensor_copy(b_hi[:, :, :].bitcast(F32R), b_nrm[:, :, :]).then_inc(rms_step, 1)
                dve.wait_ge(rms_step, 6 * q + 5)
                dve.tensor_tensor(b_lo[:, :, :], b_nrm[:, :, :], b_hi[:, :, :], ALU.subtract).then_inc(rms_step, 1)

            def dt_before_softplus(i, nxt):
                for h in range(2):
                    held, free = front_filled(i, F_DT + h)
                    dve.tensor_tensor(dt[nxt][:, 4 * h:4 * h + 4, :], held[:, :].rearrange("p (c t) -> p c t", c=4),
                                      bdt[:, 4 * h:4 * h + 4].unsqueeze(2).to_broadcast([P, 4, P]),
                                      ALU.add).then_inc(free, 1)

            def dt_whole(i, nxt):
                dve.wait_ge(log_step, 3 * (i + 1) + 3)
                z = dt[nxt][:, :, :].rearrange("p c t -> p (c t)")
                dve.scalar_tensor_tensor(out=z, in0=z, scalar=0.0, in1=du[:, :, :].rearrange("p c t -> p (c t)"),
                                         op0=ALU.max, op1=ALU.add).then_inc(dt_done, 1)

            def dt_times_x(i, nxt):
                dve.wait_ge(dt_done, i + 2)
                dve.wait_ge(xs_done, PRIMED + 2 * (i + 1) + 2)
                dve.tensor_tensor(du[:, :, :], dt[nxt][:, :, :], xs[nxt][:, :, :], ALU.mult).then_inc(du_done, 1)

            def du_low_part(i):
                dve.wait_ge(du_hi, i + 2)
                dve.tensor_tensor(du_hl[:, :, :, 1, :], du[:, :, :].rearrange("p c (b l) -> p c b l", b=2),
                                  du_hl[:, :, :, 0, :], ALU.subtract).then_inc(du_lo, 1)

            def scan(i, u):
                dve.wait_ge(decay_done, PRIMED + SCANS * i + u + 1)
                dve.wait_ge(drive_full, PRIMED + SCANS * i + u + 1)
                dve.wait_ge(turned_full, PRIMED + SCANS * i + max(GN * (u // GC - 1), 0))
                dve.tensor_tensor_scan(
                    state[:, u % RING, :, :].rearrange("p n t -> p (n t)"),
                    decay[:, u % DRING, :, :, :].rearrange("p n b l -> p (n b l)"),
                    drive[u % 2][:, :], 0.0, ALU.mult, ALU.add).then_inc(scan_done, 1)

            def mix(i, par, v):
                item, c = v // GN, v % GN
                n, part = (item // NGC) * GN + c, item % NGC
                to = acc[:, part * 512:(part + 1) * 512]
                dve.wait_ge(turned_full, PRIMED + SCANS * i + v + 1)
                dve.wait_ge(mix_done, PRIMED + SCANS * i + v)
                if v == 0 and ends(i):
                    dve.wait_ge(front_full, PRIMED + place(front_uses, i, F_SUM + 1)[1] + 1)
                if n == 0:
                    ins = dve.tensor_scalar(to, turned[v % 2][:, :], c_col[par][:, n:n + 1], None, ALU.mult)
                else:
                    ins = dve.scalar_tensor_tensor(out=to, in0=turned[v % 2][:, :], scalar=c_col[par][:, n:n + 1],
                                                   in1=to, op0=ALU.mult, op1=ALU.add)
                ins.then_inc(mix_done, 1)

            def context_low_part(i, j):
                dve.wait_ge(cs_hi, 2 * i + j + 1)
                dve.tensor_tensor(cs[64:P, :], c2[64:P, :], cs[64:P, :].bitcast(F32), ALU.subtract).then_inc(cs_lo, 1)

            def key_maxima(i, j, c):
                held, free = att_filled(i, key_use(j, A_KEY + c))
                dve.tensor_reduce(km[:, c:c + 1], held[:, :], AX_X, ALU.max).then_inc(free, 1)
                if c == KC - 1:
                    att_read(i, key_use(j, A_KEY + c))
                    dve.wait_ge(kdiag_done, PRIMED + 2 * i + j)
                    dve.tensor_scalar(nkm[:, :], km[:, :], -1.0, None, ALU.mult).then_inc(km_done, 1)

            def context_matrix(i, par, j, k):
                held, free = att_filled(i, key_use(j, A_MAT + k))
                both = held[:, 0:2 * (P + 1)].rearrange("p (c x) -> p c x", c=2)
                dve.reciprocal(rz[:, 2 * k:2 * k + 2], both[:, :, P:P + 1].squeeze(2)).then_inc(rz_step, 1)
                dve.wait_ge(rz_step, PRIMED + 4 * i + 2 * j + k + 1)
                for r in (0, 64):
                    ins = dve.scalar_tensor_tensor(
                        out=mt[par][j][r:r + 64, 2 * k:2 * k + 2, 64 * j:64 * j + 64], in0=both[r:r + 64, :, r:r + 64],
                        scalar=DH ** -0.5, in1=rz[r:r + 64, 2 * k:2 * k + 2].unsqueeze(2).to_broadcast([64, 2, 64]),
                        op0=ALU.mult, op1=ALU.mult)
                ins.then_inc(free, 1)

            def gated_sum(i, prv, h):
                held, free = front_filled(i, F_SUM + h)
                for c in range(4):
                    d = 4 * h + c
                    ins = dve.scalar_tensor_tensor(out=y[:, d, :], in0=xs[prv][:, d, :], scalar=dsk[:, d:d + 1],
                                                   in1=held[:, c * P:(c + 1) * P], op0=ALU.mult, op1=ALU.add)
                ins.then_inc(free, 1)
                front_read(i, F_SUM + h)
                dve.tensor_tensor(y[:, 4 * h:4 * h + 4, :], y[:, 4 * h:4 * h + 4, :], sg[prv][:, 4 * h:4 * h + 4, :],
                                  ALU.mult).then_inc(y_done, 1)

            def residual_x1(i):
                held, free = front_filled(i, F_OUT)
                dve.wait_ge(xtok_in, 16 * i)
                dve.tensor_tensor(x1[:, :], held[:, :], x1[:, :], ALU.add).then_inc(free, 1)
                front_read(i, F_OUT)
                dve.bn_stats(bn[:, :], x1[:, :]).then_inc(ln1_step, 1)
                dve.drain()
                dve.bn_aggr(mv[:, :], bn[:, :]).then_inc(ln1_step, 1)

            def layernorm_x1(i):
                dve.wait_ge(ln1_root, 2 * (i - 1) + 2)
                dve.tensor_scalar(x1[:, :], x1[:, :], mv[:, 0:1], rstd[:, 0:1], ALU.subtract, ALU.mult).then_inc(x1_done, 1)

            def x1_low_part(i):
                dve.wait_ge(s_hi, i)
                dve.tensor_tensor(s_tmp[0:64, :], x1[0:64, :], s_hl[0][0:64, :].bitcast(F32), ALU.subtract)
                dve.tensor_tensor(s_hl[1][64:P, :], x1[64:P, :], s_tmp[64:P, :].bitcast(F32),
                                  ALU.subtract).then_inc(s_lo, 1)

            def query_maxima(i, j, c):
                held, free = att_filled(i, query_use(j, A_QPOS + c))
                dve.tensor_reduce(qm[:, c, :], held[:, :].rearrange("p (h d) -> p h d", h=HEADS),
                                  AX_X, ALU.max).then_inc(free, 1)

            def softmax_queries(i, j, c):
                dve.wait_ge(rq_done, 8 * (i - 1) + 4 * j + c + 1)
                dve.tensor_tensor(eq[:, c, :], eq[:, c, :], rq[:, c % 2, :], ALU.mult).then_inc(eq_done, 1)

            def bound_norm(i):
                held, free = att_filled(i, A_NORM)
                dve.tensor_scalar(rn[:, :], held[:, :], 1e-24, None, ALU.max).then_inc(free, 1)

            def residual_x2(i):
                p = i - 1
                dve.wait_ge(norm_step, 2 * p + 2)
                dve.scalar_tensor_tensor(out=u2[:, :], in0=u2[:, :], scalar=g8[:, 0:1], in1=rn[:, :],
                                         op0=ALU.mult, op1=ALU.mult).then_inc(ln2_step, 1)
                dve.wait_ge(ln2_step, 4 * p + 1)
                dve.tensor_tensor(u2[:, :], u2[:, :], x1[:, :], ALU.add).then_inc(ln2_step, 1)
                dve.wait_ge(ln2_step, 4 * p + 2)
                dve.bn_stats(bn2[:, :], u2[:, :]).then_inc(ln2_step, 1)
                dve.drain()
                dve.bn_aggr(mv2[:, :], bn2[:, :]).then_inc(ln2_step, 1)

            def layernorm_x2(i):
                dve.wait_ge(ln2_root, 2 * (i - 1) + 2)
                dve.tensor_scalar(u2[:, :], u2[:, :], mv2[:, 0:1], rstd2[:, 0:1], ALU.subtract, ALU.mult).then_inc(x2_done, 1)

            def beside(i, par, s):
                nxt = 1 - par
                if ends(i) and s in (0, 1):
                    gated_sum(i, nxt, s)
                if scans(i):
                    if s in (0, 6):
                        context_low_part(i, s // 6)
                    if s in (1, 2, 9, 10):
                        for c in range(2):
                            key_maxima(i, s // 9, 2 * (s in (2, 10)) + c)
                    if s in (8, 16):
                        for k in range(2):
                            context_matrix(i, par, s // 16, k)
                if ends(i):
                    if s == 9:
                        residual_x1(i)
                    if s == 10:
                        layernorm_x1(i)
                    if s == 11:
                        x1_low_part(i)
                    for j, first in ((0, 17), (1, 26)):
                        if s in (first, first + 1):
                            for c in range(2):
                                query_maxima(i, j, 2 * (s - first) + c)
                        if s in (first + 5, first + 6):
                            for c in range(2):
                                softmax_queries(i, j, 2 * (s - first - 5) + c)
                if begins(i):
                    if s in (3, 4, 5):
                        convolve(i, nxt, 0, s - 2)
                    if s in (12, 13, 14):
                        convolve(i, nxt, 1, s - 11)
                    if s == 23:
                        ssm_squares(i)
                    if s == 24:
                        ssm_norms(i, nxt)
                    if s == 27:
                        dt_before_softplus(i, nxt)
                    if s == 30:
                        dt_whole(i, nxt)
                    if s == 31:
                        dt_times_x(i, nxt)
                    if s == 32:
                        du_low_part(i)

            def turn(i, par):
                for s in range(STEPS):
                    if scans(i) and AHEAD <= s < SCANS:
                        scan(i, s)
                    if s > 0:
                        beside(i, par, s - 1)
                    if scans(i) and s >= GC:
                        mix(i, par, s - GC)
                if ends(i):
                    bound_norm(i)
                if begins(i):
                    scan(i + 1, 0)
                if ends(i):
                    residual_x2(i)
                if begins(i):
                    scan(i + 1, 1)
                if ends(i):
                    layernorm_x2(i)

            turn(-1, 1)
            turn(0, 0)
            with dve.Fori(0, (PAIRS - 2) // 2) as r:
                turn(2 * r + 1, 1)
                turn(2 * r + 2, 0)
            turn(PAIRS - 1, 1)
            turn(PAIRS, 0)

            for t in range(TC):
                dve.wait_ge(f_hi, t + 1)
                dve.tensor_tensor(x2t_lo[:, :, t * P:(t + 1) * P], front[t % 2][:, :].rearrange("p (c t) -> p c t", c=KC),
                                  x2t_hi[:, :, t * P:(t + 1) * P].bitcast(F32), ALU.subtract).then_inc(f_lo, 1)
            for n in range(FC * HALVES):
                f = n // HALVES
                dve.wait_ge(gate_done, n + 1)
                dve.wait_ge(up_full, n + 1)
                if n >= 2:
                    dve.wait_ge(hid_lo_done, n - 1)
                dve.scalar_tensor_tensor(out=hid[:, n % 2, :], in0=turned[n % 2][:, :], scalar=us_sb[:, f:f + 1],
                                         in1=gate[:, n % 2, :], op0=ALU.mult, op1=ALU.mult).then_inc(hid_done, 1)
            dve.wait_ge(dw_in, 16 * (FC + 1))
            for f in range(FC):
                dve.tensor_copy(dw[:, f, :], dw_raw[:, f, :]).then_inc(dw_done, 1)
            for t in range(TC):
                k = t % 2
                dve.wait_ge(down_full, t + 1)
                dve.tensor_tensor(r3[:, k, :], att[k][:, :], ds_sb[:, :], ALU.mult).then_inc(ln3_step, 1)
                dve.wait_ge(ln3_step, 4 * t + 1)
                dve.wait_ge(res_in[k], 16 * (t // 2 + 1))
                dve.tensor_tensor(r3[:, k, :], r3[:, k, :], x2_res[:, k, :], ALU.add).then_inc(ln3_step, 1)
                dve.wait_ge(ln3_step, 4 * t + 2)
                dve.bn_stats(bn3[:, k, :], r3[:, k, :]).then_inc(ln3_step, 1)
                dve.wait_ge(ln3_step, 4 * t + 3)
                dve.bn_aggr(mv3[:, k, :], bn3[:, k, :]).then_inc(ln3_step, 1)
                dve.wait_ge(ln3_root, 2 * t + 2)
                if t >= 2:
                    dve.wait_ge(out_done[k], 16 * (t // 2))
                dve.tensor_scalar(y3[:, k, :], r3[:, k, :], mv3[:, k, 0:1], rstd3[:, k, 0:1],
                                  ALU.subtract, ALU.mult).then_inc(y3_done, 1)

        @block.tensor
        def _(pe):
            pe.wait_ge(par_in, 16 * N_PAR)
            pe.wait_ge(const_done, 1)
            for c in range(KC):
                mm = pe.matmul(att[0][0:64, c * P:(c + 1) * P], wv_raw[:, c, :], wo_raw[:, c, :], start=True, stop=True)
            mm.then_inc(setup_pe, 1)
            pe.wait_ge(win_in, 16 * KC)
            pe.wait_ge(setup_act, 6)
            pe.wait_ge(setup_vec, 1)
            pe.wait_ge(wout_in, 16)

            def fill_front(i, n):
                bank, _, own = place(front_uses, i, n)
                pe.wait_ge(front_free[bank], PRIMED + own)
                return front[bank]

            def front_read(i, n):
                bank, _, own = place(front_uses, i, n)
                pe.wait_ge(front_free[bank], PRIMED + own + 1)

            def fill(i, n):
                bank, _, own = place(att_uses, i, n)
                pe.wait_ge(att_free[bank], PRIMED + own)
                return att[bank]

            def att_read(i, n):
                bank, _, own = place(att_uses, i, n)
                pe.wait_ge(att_free[bank], PRIMED + own + 1)

            def project(i, h, half):
                n = (F_CONV0, F_CONV1, F_GATE, F_GATE + 1)[h]
                if half == 0:
                    fill_front(i, n)
                    pe.wait_ge(xt_in, 16 * (i + 1) + 16)
                to = front[n % 2]
                for c in range(2 * half, 2 * half + 2):
                    for k in range(KC):
                        mm = pe.matmul(to[:, c * P:(c + 1) * P], win[:, k, (4 * h + c) * P:(4 * h + c + 1) * P],
                                       xt[:, k, :], start=(k == 0), stop=(k == KC - 1))
                if half == 1:
                    mm.then_inc(front_full, 1)

            def ssm_by_channel(i, nxt):
                to = fill_front(i, F_SSM)
                pe.wait_ge(xs_done, PRIMED + 2 * (i + 1) + 2)
                for d in range(DC):
                    mm = pe.matmul(to[0:64, 0:P], wx[:, d, :], xs[nxt][:, d, :], start=(d == 0), stop=(d == DC - 1))
                mm.then_inc(front_full, 1)

            def ssm_by_token(i):
                to = fill_front(i, F_TOKEN)
                front_read(i, F_SSM)
                pe.transpose(to[:, 0:P], ssm[:, :], ident[:, :])
                for b in range(2):
                    mm = pe.transpose(to[:, P * (b + 1):P * (b + 2)],
                                      ssm2[:, b, :, :].rearrange("k s l -> k (s l)"), ident[:, :])
                mm.then_inc(front_full, 1)

            def dt_input(i):
                to = fill_front(i, F_DT_IN)
                pe.wait_ge(rms_step, 6 * (i + 1) + 3)
                pe.transpose(to[0:RK, 0:P], tsn[:, :], ident[:, :]).then_inc(front_full, 1)

            def dt_projection(i):
                front_read(i, F_DT_IN)
                for h in range(2):
                    to = fill_front(i, F_DT + h)
                    for c in range(4):
                        d = 4 * h + c
                        mm = pe.matmul(to[:, c * P:(c + 1) * P], wdt[:, d * P:(d + 1) * P], tst[:, :], start=True, stop=True)
                    mm.then_inc(front_full, 1)

            def du_by_token(i, k):
                to = fill_front(i, F_DU + k)
                pe.wait_ge(du_lo, i + 2)
                for b in range(2):
                    for c in range(2):
                        mm = pe.transpose(to[:, (2 * b + c) * P:(2 * b + c + 1) * P],
                                          du_hl[:, 2 * k + c, b, :, :].rearrange("p s l -> p (s l)"), ident[:, :])
                mm.then_inc(front_full, 1)

            def drives(i, u):
                g, d = u // DC, u % DC
                if u == 0:
                    front_read(i - 1, F_DU + 2)
                    front_read(i - 1, F_DU + 3)
                pe.wait_ge(scan_done, PRIMED + SCANS * i + max(u - 1, 0))
                pe.wait_ge(diag_done, PRIMED + 16 * i + 4 * (g + 1))
                to = drive[u % 2][:, :].rearrange("p (n b l) -> p n b l", n=GN, b=2)
                for b in range(2):
                    pe.matmul(to[:, :, b, :], du_t[:, b, d, :], diag_hi[:, b, g * GN:(g + 1) * GN, :],
                              start=True, stop=False)
                    mm = pe.matmul(to[:, :, b, :], du_t[:, b, d, :], diag_lo[:, b, g * GN:(g + 1) * GN, :],
                                   start=False, stop=True)
                mm.then_inc(drive_full, 1)

            def states_by_token(i, v):
                item, c = v // GN, v % GN
                pe.wait_ge(scan_done, PRIMED + SCANS * i + GC * (item + 1))
                pe.wait_ge(mix_done, PRIMED + SCANS * i + max(v - 1, 0))
                for k in range(GC):
                    mm = pe.transpose(turned[v % 2][:, k * P:(k + 1) * P],
                                      state[:, (GC * item + k) % RING, c, :], ident[:, :])
                mm.then_inc(turned_full, 1)

            def keys_by_channel(i, j, c):
                to = fill(i, key_use(j, A_KEY + c))
                pe.wait_ge(cs_lo, PRIMED + 2 * i + j + 1)
                pe.matmul(to[:, :], wk_hi[:, c * P:(c + 1) * P], cs[:, :], start=True, stop=True).then_inc(att_full, 1)

            def keys_by_position(i, j, c):
                to = fill(i, key_use(j, A_POS + c))
                pe.matmul(to[:, :], cs[:, c * P:(c + 1) * P], wk_hi[:, :], start=True, stop=False)
                pe.matmul(to[:, :], cs[:, c * P:(c + 1) * P], wk_lo[:, :], start=False, stop=False)
                pe.wait_ge(kdiag_done, PRIMED + 2 * i + j + 1)
                pe.matmul(to[:, :], ones_r[:, :], kdiag[:, :, :].rearrange("p c k -> p (c k)"),
                          start=False, stop=True).then_inc(att_full, 1)

            def keys_times_context(i, j, c):
                n = key_use(j, A_CTX)
                if c == 0:
                    fill(i, n)
                    att_read(i, key_use(j, A_POS + 2))
                    att_read(i, key_use(j, A_POS + 3))
                    pe.wait_ge(ctx1_in, 32 * i + 16 * j + 16)
                mm = pe.matmul(att[n % 2][0:65, :], ctx1[:, c, :], ek[:, c, :], start=(c == 0), stop=(c == KC - 1))
                if c == KC - 1:
                    mm.then_inc(att_full, 1)

            def context_matrix(i, j, k):
                att_read(i, key_use(j, A_CTX))
                to = fill(i, key_use(j, A_MAT + k))
                for c in range(2):
                    h = 2 * k + c
                    mm = pe.matmul(to[:, c * (P + 1):(c + 1) * (P + 1)], gt[0:65, h * P:(h + 1) * P],
                                   ucat[0:65, h, :], start=True, stop=True)
                mm.then_inc(att_full, 1)

            def sums_by_channel(i):
                pe.wait_ge(mix_done, PRIMED + SCANS * i)
                for h in range(2):
                    to = fill_front(i, F_SUM + h)
                    for c in range(4):
                        d = 4 * h + c
                        mm = pe.transpose(to[:, c * P:(c + 1) * P], acc[:, d * P:(d + 1) * P], ident[:, :])
                    mm.then_inc(front_full, 1)

            def project_out(i, quarter):
                if quarter == 0:
                    fill_front(i, F_OUT)
                    pe.wait_ge(y_done, PRIMED + 2 * i)
                for d in range(2 * quarter, 2 * quarter + 2):
                    mm = pe.matmul(front[F_OUT % 2][:, :], y[:, d, :], wout[:, d, :], start=(d == 0), stop=(d == DC - 1))
                if quarter == 3:
                    mm.then_inc(front_full, 1)

            def queries_by_position(i, j, c):
                to = fill(i, query_use(j, A_QPOS + c))
                pe.wait_ge(s_in, 32 * i)
                pe.matmul(to[:, :], s_hl[j][:, c * P:(c + 1) * P], wq_hi[:, :],
                          start=True, stop=True).then_inc(att_full, 1)

            def query_maxima(i, j):
                to = fill(i, query_use(j, A_QMAX))
                att_read(i, query_use(j, A_QPOS + 3))
                for c in range(KC):
                    mm = pe.transpose(to[0:HEADS, c * P:(c + 1) * P], qm[:, c, :], ident[:, :])
                mm.then_inc(att_full, 1)

            def queries_by_channel(i, j, c):
                to = fill(i, query_use(j, A_QCH + c))
                pe.matmul(to[:, :], wq_hi[:, c * P:(c + 1) * P], s_hl[j][:, :], start=True, stop=False)
                pe.matmul(to[:, :], wq_lo[:, c * P:(c + 1) * P], s_hl[j][:, :], start=False, stop=False)
                att_read(i, query_use(j, A_QMAX))
                pe.matmul(to[:, :], pick[:, c, :], qrow[:, :], start=False, stop=True).then_inc(att_full, 1)

            def query_sums(i, j, c):
                to = fill(i, query_use(j, A_SUM + c))
                att_read(i, query_use(j, A_QCH + c))
                pe.matmul(to[:, :], blocks[:, :], eq[:, c, :], start=True, stop=True).then_inc(att_full, 1)

            def attention_out(i, prv, j, c):
                n = query_use(j, A_OUT)
                if c == 0:
                    fill(i, n)
                pe.wait_ge(eq_done, PRIMED + 8 * (i - 1) + 4 * j + c + 1)
                mm = pe.matmul(att[n % 2][:, :], mt[prv][j][:, c, :], eq[:, c, :], start=(c == 0), stop=(c == KC - 1))
                if c == KC - 1:
                    mm.then_inc(att_full, 1)

            def norm_of_out(i):
                to = fill(i, A_NORM)
                pe.wait_ge(usq_done, i)
                pe.matmul(to[:, :], blocks[:, :], rn[:, :], start=True, stop=True).then_inc(att_full, 1)

            def beside(i, par, s):
                nxt = 1 - par
                if ends(i):
                    if s == 0:
                        sums_by_channel(i)
                    if s in (3, 4, 8, 9):
                        project_out(i, (3, 4, 8, 9).index(s))
                if begins(i):
                    if s in (1, 2):
                        project(i, 0, s - 1)
                    if s in (10, 11):
                        project(i, 1, s - 10)
                    if 16 <= s < 20:
                        project(i, 2 + (s - 16) // 2, s % 2)
                if scans(i):
                    for j, first in ((0, 1), (1, 9)):
                        if s in (first, first + 1):
                            for c in range(2):
                                keys_by_channel(i, j, 2 * (s - first) + c)
                        if s in (first + 3, first + 4):
                            for c in range(2):
                                keys_by_position(i, j, 2 * (s - first - 3) + c)
                        if s in (first + 5, first + 6):
                            for c in range(2):
                                keys_times_context(i, j, 2 * (s - first - 5) + c)
                        if s == first + 7:
                            for k in range(2):
                                context_matrix(i, j, k)
                if begins(i):
                    if s == 22:
                        ssm_by_channel(i, nxt)
                    if s == 23:
                        ssm_by_token(i)
                    if s == 26:
                        dt_input(i)
                    if s == 27:
                        dt_projection(i)
                if ends(i):
                    for j, first in ((0, 17), (1, 26)):
                        if s in (first, first + 1):
                            for c in range(2):
                                queries_by_position(i, j, 2 * (s - first) + c)
                        if s == first + 2:
                            query_maxima(i, j)
                        if s in (first + 3, first + 4):
                            for c in range(2):
                                queries_by_channel(i, j, 2 * (s - first - 3) + c)
                        if s in (first + 5, first + 6):
                            for c in range(2):
                                query_sums(i, j, 2 * (s - first - 5) + c)
                        if s in (first + 7, first + 8):
                            for c in range(2):
                                attention_out(i, nxt, j, 2 * (s - first - 7) + c)
                if begins(i) and s in (33, 34):
                    for k in range(2):
                        du_by_token(i, 2 * (s - 33) + k)
                if ends(i) and s == 35:
                    norm_of_out(i)

            def turn(i, par):
                for s in range(STEPS):
                    if scans(i) and AHEAD <= s + 1 < SCANS:
                        drives(i, s + 1)
                    if begins(i) and s == STEPS - 1:
                        drives(i + 1, 0)
                    if scans(i) and s >= GC:
                        states_by_token(i, s - GC)
                    beside(i, par, s)
                if begins(i):
                    drives(i + 1, 1)

            turn(-1, 1)
            turn(0, 0)
            with pe.Fori(0, (PAIRS - 2) // 2) as r:
                turn(2 * r + 1, 1)
                turn(2 * r + 2, 0)
            turn(PAIRS - 1, 1)
            turn(PAIRS, 0)

            for t in range(TC):
                pe.wait_ge(f_in[t % 4], 16 * (t // 4 + 1))
                if t >= 2:
                    pe.wait_ge(f_lo, t - 1)
                for c in range(KC):
                    mm = pe.transpose(front[t % 2][:, c * P:(c + 1) * P], x2_in[t % 4][:, c * P:(c + 1) * P], ident[:, :])
                mm.then_inc(f_full, 1)
            pe.wait_ge(f_lo, TC)
            for f in range(FC):
                pe.wait_ge(gu_done, f + 1)
                for h in range(HALVES):
                    n = f * HALVES + h
                    for s, banks, free, full in ((0, drive, gate_done, gate_full), (1, turned, hid_done, up_full)):
                        if n >= 2:
                            pe.wait_ge(free, n - 1)
                        for k in range(KC):
                            for part in (x2t_hi, x2t_lo):
                                mm = pe.matmul(banks[n % 2][:, :], gu[:, f % WR, s, k, :],
                                               part[:, k, h * HALF:(h + 1) * HALF],
                                               start=(k == 0 and part is x2t_hi), stop=(k == KC - 1 and part is x2t_lo))
                        mm.then_inc(full, 1)
            pe.wait_ge(hid_hi_done, FC * HALVES)
            pe.wait_ge(hid_lo_done, FC * HALVES)
            for t in range(TC):
                if t >= 2:
                    pe.wait_ge(ln3_step, 4 * (t - 2) + 1)
                for f in range(FC):
                    if t == 0:
                        pe.wait_ge(dw_done, f + 1)
                    for part in (hid_hi, hid_lo):
                        mm = pe.matmul(att[t % 2][:, :], part[:, f, t * P:(t + 1) * P], dw[:, f, :],
                                       start=(f == 0 and part is hid_hi), stop=(f == FC - 1 and part is hid_lo))
                mm.then_inc(down_full, 1)


def lay_out(a):
    c = np.ascontiguousarray
    x, ctx = a["x"].reshape(TOK, H), a["ctx_4096"]

    def by_part(w):
        return c(w.reshape(-1, P, w.shape[1]).transpose(1, 0, 2))

    def col(v):
        return c(v.reshape(-1, P).T)

    def blocks_t(w):
        return c(w.reshape(FC, P, KC, P).transpose(0, 3, 2, 1))

    return {
        "x_tok": c(x.reshape(PAIRS, P, H)),
        "x_t": c(x.reshape(PAIRS, P, KC, P).transpose(0, 3, 2, 1)),
        "ctx": c(ctx),
        "ctx_t": c(ctx.reshape(B, L, KC, P).transpose(0, 3, 2, 1)),
        "w_in": c(a["L0_attn_W_in"].T.reshape(KC, P, 2 * DI)),
        "conv_w": by_part(a["L0_attn_conv_w"]),
        "conv_b": col(a["L0_attn_conv_b"]),
        "w_x": by_part(a["L0_attn_W_x"].T),
        "w_dt": c(a["L0_attn_W_dt"].T),
        "b_dt": col(a["L0_attn_b_dt"]),
        "a_log": by_part(a["L0_attn_A_log"]),
        "d_skip": col(a["L0_attn_D"]),
        "w_out": by_part(a["L0_attn_W_out"].T),
        "wq": c(a["L0_xattn_Wq"].T),
        "wk": c(a["L0_xattn_Wk"].T),
        "wv": by_part(a["L0_xattn_Wv"]),
        "wo": by_part(a["L0_xattn_Wo"].T),
        "bo": c(a["L0_xattn_bo"].reshape(64, 1)),
        "gain": c(a["L0_xattn_g"].reshape(64, 1)),
        "gate_w": blocks_t(a["L0_ffn_gate_t"]),
        "up_w": blocks_t(a["L0_ffn_up_t"]),
        "down_w": c(a["L0_ffn_down_t"].T.reshape(FC, P, H)),
        "gate_s": col(a["L0_ffn_gate_s"]),
        "up_s": col(a["L0_ffn_up_s"]),
        "down_s": c(a["L0_ffn_down_s"]),
    }


def kernel(**inputs):
    import concourse.bacc as bacc
    from concourse.bass_utils import run_bass_kernel_spmd

    arrays = lay_out({k: np.asarray(v) for k, v in inputs.items()})
    nc = bacc.Bacc("TRN2", target_bir_lowering=False, num_devices=1)
    args = [nc.dram_tensor(f"in_{k}", v.shape, mybir.dt.from_np(v.dtype), kind="ExternalInput").ap()
            for k, v in arrays.items()]
    out = nc.dram_tensor("out", (TC, P, H), F32, kind="ExternalOutput").ap()
    decoder_kernel(nc, *args, out)
    r = run_bass_kernel_spmd(nc, [{f"in_{k}": v for k, v in arrays.items()}], core_ids=[0])
    return r.results[0]["out"].reshape(B, L, H)
```

```python
from contextlib import ExitStack

import numpy as np

import concourse.bass as bass
from concourse import mybir

F32 = mybir.dt.float32
F32R = mybir.dt.float32r
I32 = mybir.dt.int32
ALU = mybir.AluOpType
ACT = mybir.ActivationFunctionType
AX_X = mybir.AxisListType.X

P = 128
B, L, H = 16, 64, 512
PAIRS = B // 2
KC = H // P
DI, NS, RK = 1024, 16, 32
DC = DI // P
TAPS = 4
HEADS, DH = 8, 64
GN = 4
NG = NS // GN
GC = 4
NGC = DC // GC
ITEMS = NG * NGC
SCANS = ITEMS * GC
STEPS = SCANS + GC
FF = 1792
FC = FF // P
HALF = 512
TOK = B * L
TC = TOK // P
HALVES = TOK // HALF
WR = 2
LN_EPS, RMS_EPS = 1e-5, 1e-6
NORM_SCALE = 2.0 ** 20

RING = 8
DRING = 4
LEAD = 3
AHEAD = 2
PRIMED = 1




def begins(i):
    return not isinstance(i, int) or i < PAIRS - 1


def scans(i):
    return not isinstance(i, int) or 0 <= i < PAIRS


def ends(i):
    return not isinstance(i, int) or i > 0


PROJECT = (1, 2, 3, 4, 7, 8, 9, 10)
OUT = (11, 11, 12, 13)
SSM, TOKEN, DT_IN, DT_PROJ, DU_TOKEN = 14, 15, 17, 19, (33, 33)
KEYS = ((2, 3), (11, 12))
POS = ((5, 6), (14, 15))
CTX = ((7, 8), (17, 17))
MAT = (9, 18)
QPOS = ((19, 19), (26, 26))
QMAX = (20, 28)
QCH = ((21, 22), (29, 30))
SUM = ((23, 24), (31, 32))
ATTN = ((25, 26), (33, 34))
SPLIT = (0, 7)
TAP, CONV = (3, 4), ((3, 4, 5), (5, 7, 8))
SILU, ABS, EXP, LOG, DU_HIGH = 11, 27, 27, 29, 31
RESIDUAL, X1, SPLIT_X1 = 13, 14, 16

X2_TURN = (14, 15, 15, 15, 20, 21, 21)
CONVERT = (15, 16)

FRONT_ORDER = [name for _, name in sorted(
    [((OUT[0], 2), "out"), ((STEPS, 0), "sum0"), ((STEPS, 1), "sum1")]
    + [((PROJECT[2 * h], 3 + h), ("conv0", "conv1", "gate0", "gate1")[h]) for h in range(4)]
    + [((SSM, 7), "ssm"), ((TOKEN, 8), "token"), ((DT_IN, 9), "dt_in"), ((DT_PROJ, 10), "dt0"), ((DT_PROJ, 11), "dt1")]
    + [((DU_TOKEN[k // 2], 12 + k), f"du{k}") for k in range(4)])]
A_KEY, A_POS, A_CTX, A_MAT, A_KEYS = 0, 4, 8, 9, 11
A_QPOS, A_QMAX, A_QCH, A_SUM, A_OUT, A_QUERIES = 0, 4, 5, 9, 13, 14
A_NORM = 2 * A_KEYS + 2 * A_QUERIES
A_ALL = A_NORM + 1


def key_use(j, n):
    return A_KEYS * j + n


def query_use(j, n):
    return 2 * A_KEYS + A_QUERIES * j + n


def front_uses(t):
    has = {"sum0": scans(t), "sum1": scans(t), "out": ends(t)}
    return [n for n, name in enumerate(FRONT_ORDER) if has.get(name, begins(t))]


def att_uses(t):
    return [n for n in range(A_ALL) if (ends(t) if n >= 2 * A_KEYS else scans(t))]


def place(uses, i, n):
    n = n if isinstance(n, int) else FRONT_ORDER.index(n)
    t, bank = (i if isinstance(i, int) else 1), n % 2
    before = [m for s in range(-1, t) for m in uses(s)] + [m for m in uses(t) if m < n]
    own = [m for m in before if m % 2 == bank]
    if isinstance(i, int):
        return bank, len(before), len(own)
    return bank, len(uses(1)) * (i - 1) + len(before), sum(m % 2 == bank for m in uses(1)) * (i - 1) + len(own)


def decoder_kernel(nc, x_tok, x_t, ctx, ctx_t, w_in, conv_w, conv_b, w_x, w_dt, b_dt, a_log, d_skip, w_out,
                   wq, wk, wv, wo, bo, gain, gate_w, up_w, down_w, gate_s, up_s, down_s, out):
    x2_dram = nc.dram_tensor("x2_scratch", [PAIRS, P, H], F32).ap()
    with ExitStack() as whole:
        def sem(name):
            return whole.enter_context(nc.semaphore(name))

        def sb(name, shape, dt=F32, scope=whole):
            return scope.enter_context(nc.sbuf_tensor(name, shape, dt))

        front = [whole.enter_context(nc.psum_tensor(f"front{i}", [P, 512], F32)) for i in range(2)]
        drive = [whole.enter_context(nc.psum_tensor(f"drive{i}", [P, 512], F32)) for i in range(2)]
        turned = [whole.enter_context(nc.psum_tensor(f"turned{i}", [P, 512], F32)) for i in range(2)]
        att = [whole.enter_context(nc.psum_tensor(f"att{i}", [P, 512], F32)) for i in range(2)]

        ident = sb("ident", [P, P])
        eps_ln, eps_rms = sb("eps_ln", [P, 1]), sb("eps_rms", [P, 1])
        gs_sb, us_sb = sb("gs_sb", [P, FC]), sb("us_sb", [P, FC])

        loop_mem = whole.enter_context(ExitStack())

        def lb(name, shape, dt=F32):
            return sb(name, shape, dt, loop_mem)

        win = lb("win", [P, KC, 2 * DI])
        wx = lb("wx", [P, DC, 64])
        wdt = lb("wdt", [P, DI])
        diag_hi, diag_lo = lb("diag_hi", [P, 2, NS, L], F32R), lb("diag_lo", [P, 2, NS, L], F32R)
        decay = lb("decay", [P, DRING, GN, 2, L])

        blocks = lb("blocks", [P, P])
        ones_r = lb("ones_r", [P, P], F32R)
        two_eyes = lb("two_eyes", [P, L])
        pick = lb("pick", [P, KC, P], F32R)
        cw, cb = lb("cw", [P, DC, TAPS]), lb("cb", [P, DC])
        bdt, dsk = lb("bdt", [P, DC]), lb("dsk", [P, DC])
        neg_a = lb("neg_a", [P, DC, NS])
        bo_sb, g8 = lb("bo_sb", [P, 1]), lb("g8", [P, 1])
        wout = lb("wout", [P, DC, H])
        wq_hi, wq_lo = lb("wq_hi", [P, H], F32R), lb("wq_lo", [P, H], F32R)
        wk_hi, wk_lo = lb("wk_hi", [P, H], F32R), lb("wk_lo", [P, H], F32R)
        ucat = lb("ucat", [P, KC, P + 1])

        xt = lb("xt", [P, KC, P])
        xs, sg = ([lb(f"{n}{b}", [P, DC, P]) for b in range(2)] for n in ("xs", "sg"))
        ssm, ssm2 = lb("ssm", [P, P]), lb("ssm2", [P, 2, 2, L])
        tr, sq3 = lb("tr", [P, 3, 64]), lb("sq3", [P, 3, 64])
        rms = lb("rms", [P, 4])
        tsn, c_col = lb("tsn", [P, RK]), [lb(f"c_col{b}", [P, NS]) for b in range(2)]
        b_nrm = lb("b_nrm", [P, 2, NS])
        b_hi, b_lo = lb("b_hi", [P, 2, NS]), lb("b_lo", [P, 2, NS])
        tst = lb("tst", [P, P])
        dt = [lb(f"dt{b}", [P, DC, P]) for b in range(2)]
        du = lb("du", [P, DC, P])
        du_t = lb("du_t", [P, 2, DC, P], F32R)
        state = lb("state", [P, RING, GN, P])
        acc = lb("acc", [P, DI])
        x1 = lb("x1", [P, H])
        bn, mv, rstd = lb("bn", [P, 6]), lb("mv", [P, 2]), lb("rstd", [P, 1])
        du_hl = state[:, 0:4, :, :].rearrange("p r g t -> p (r g t)").rearrange(
            "p (c b s l) -> p c b s l", c=DC, b=2, s=2)
        y = du

        c2, cs = lb("c2", [P, H]), lb("cs", [P, H], F32R)
        ctx1 = lb("ctx1", [P, KC, 65])
        km, nkm = lb("km", [P, KC]), lb("nkm", [P, KC])
        kdiag = lb("kdiag", [P, KC, P], F32R)
        ek, eq = lb("ek", [P, KC, H]), lb("eq", [P, KC, H])
        gt = lb("gt", [P, H])
        rz = lb("rz", [P, 4])
        mt = [[lb(f"mt{b}{j}", [P, KC, P]) for j in range(2)] for b in range(2)]
        s_hl = [lb(f"s_hl{j}", [P, H], F32R) for j in range(2)]
        s_tmp = lb("s_tmp", [P, H], F32R)
        qm = lb("qm", [P, KC, HEADS])
        qrow = lb("qrow", [P, H], F32R)
        rq, u2, rn = lb("rq", [P, 2, H]), lb("u2", [P, H]), lb("rn", [P, H])
        bn2, mv2, rstd2 = lb("bn2", [P, 6]), lb("mv2", [P, 2]), lb("rstd2", [P, 1])
        wq_raw, wk_raw = rn, u2
        wv_raw = ek[:, 0, 0:KC * 64].rearrange("p (c j) -> p c j", c=KC)
        wo_raw = ek[:, 1, :].rearrange("p (c j) -> p c j", c=KC)
        pick_raw = eq[:, 0, :].rearrange("p (c j) -> p c j", c=KC)
        ones_raw = eq[:, 1, 0:P]
        loop_mem.close()

        up_mem = whole.enter_context(ExitStack())
        x2t_hi = sb("x2t_hi", [P, KC, TOK], F32R, up_mem)
        x2t_lo = sb("x2t_lo", [P, KC, TOK], F32R, up_mem)
        gu_raw = sb("gu_raw", [P, WR, 2, KC, P], I32, up_mem)
        gu = sb("gu", [P, WR, 2, KC, P], F32R, up_mem)
        gate = sb("gate", [P, 2, HALF], F32, up_mem)
        hid = sb("hid", [P, 2, HALF], F32, up_mem)
        x2_in = [gate[:, 0, :], gate[:, 1, :], hid[:, 0, :], hid[:, 1, :]]
        up_mem.close()
        dw = sb("dw", [P, FC, H], F32R)
        x2_res = sb("x2_res", [P, 2, H])
        r3, y3 = sb("r3", [P, 2, H]), sb("y3", [P, 2, H])
        bn3, mv3, rstd3 = sb("bn3", [P, 2, 6]), sb("mv3", [P, 2, 2]), sb("rstd3", [P, 2, 1])
        up_words = 2 * KC * TOK + 2 * WR * 2 * KC * P + 4 * HALF
        sb("gap", [P, up_words - FC * H - 6 * H])
        hid_hi = sb("hid_hi", [P, FC, TOK], F32R)
        hid_lo = sb("hid_lo", [P, FC, TOK], F32R)
        dw_raw = sb("dw_raw", [P, FC, H], I32)
        ds_sb = sb("ds_sb", [P, H])

        par_in, wout_in, begin_in, wdt_in = sem("par_in"), sem("wout_in"), sem("begin_in"), sem("wdt_in")
        win_in = [sem(f"win_in{h}") for h in range(4)]
        xt_in, xtok_in, ctx_in, ctx1_in = sem("xt_in"), sem("xtok_in"), sem("ctx_in"), sem("ctx1_in")
        const_step, const_done, setup_act, setup_vec, setup_pe = (
            sem("const_step"), sem("const_done"), sem("setup_act"), sem("setup_vec"), sem("setup_pe"))
        front_full, drive_full = sem("front_full"), sem("drive_full")
        turned_full, att_full = sem("turned_full"), sem("att_full")
        front_free = [sem("front_free0"), sem("front_free1")]
        att_free = [sem("att_free0"), sem("att_free1")]
        taps_done, conv_step, xs_done = sem("taps_done"), sem("conv_step"), sem("xs_done")
        sq3_done, rms_step = sem("sq3_done"), sem("rms_step")
        diag_done = sem("diag_done")
        log_step, du_hi = sem("log_step"), sem("du_hi")
        dt_done, du_done, du_lo = sem("dt_done"), sem("du_done"), sem("du_lo")
        decay_done, scan_done, mix_done = sem("decay_done"), sem("scan_done"), sem("mix_done")
        y_done, ln1_step, x1_done = sem("y_done"), sem("ln1_step"), sem("x1_done")
        cs_hi, cs_lo = sem("cs_hi"), sem("cs_lo")
        km_done, kdiag_done = sem("km_done"), sem("kdiag_done")
        rz_step = sem("rz_step")
        s_hi, s_lo, s_in = sem("s_hi"), sem("s_lo"), sem("s_in")
        rms_root, ln1_root = sem("rms_root"), sem("ln1_root")
        ln2_root, ln3_root = sem("ln2_root"), sem("ln3_root")
        norm_step, rq_done = sem("norm_step"), sem("rq_done")
        eq_done = sem("eq_done")
        usq_done, ln2_step, x2_done = sem("usq_done"), sem("ln2_step"), sem("x2_done")
        x2_out, x2_stored = sem("x2_out"), sem("x2_stored")
        f_in = [sem(f"f_in{k}") for k in range(4)]
        f_full, f_hi, f_lo = sem("f_full"), sem("f_hi"), sem("f_lo")
        gu_in = [sem(f"gu_in{k}") for k in range(WR)]
        gu_done, gate_full, up_full, gate_done, hid_done = (
            sem("gu_done"), sem("gate_full"), sem("up_full"), sem("gate_done"), sem("hid_done"))
        hid_hi_done, hid_lo_done, dw_in, dw_done = sem("hid_hi_done"), sem("hid_lo_done"), sem("dw_in"), sem("dw_done")
        res_in = [sem("res_in0"), sem("res_in1")]
        down_full, ln3_step, y3_done = sem("down_full"), sem("ln3_step"), sem("y3_done")
        out_done = [sem("out_done0"), sem("out_done1")]

        def x2_bank(t):
            return front[0] if t == TC - 1 else drive[t % 2]

        block = whole.enter_context(nc.Block())
        N_PAR, N_BEGIN = 19, 6

        @block.sync
        def _(sp):
            def load(dst, src, to=par_in):
                sp.dma_start(dst, src).then_inc(to, 16)

            load(neg_a[:, :, :], a_log, begin_in)
            load(cw[:, :, :], conv_w, begin_in)
            load(cb[:, :], conv_b, begin_in)
            load(xt[:, :, :], x_t[0], xt_in)
            load(bdt[:, :], b_dt, begin_in)
            load(dsk[:, :], d_skip, begin_in)
            load(wx[:, :, :], w_x, begin_in)
            for h in range(4):
                load(win[:, :, 512 * h:512 * h + 512], w_in[h], win_in[h])
            load(wq_raw[0:64, :], wq)
            load(wq_raw[64:P, :], wq)
            load(wk_raw[0:64, :], wk)
            load(wk_raw[64:P, :], wk)
            load(wv_raw, wv)
            sp.wait_ge(const_done, 1)
            for c in range(KC):
                for j in range(2):
                    load(wo_raw[64 * j:64 * j + 64, c, 64 * j:64 * j + 64], wo[64 * j:64 * j + 64, c, :])
            load(bo_sb[0:64, :], bo)
            load(bo_sb[64:P, :], bo)
            load(g8[0:64, :], gain)
            load(g8[64:P, :], gain)
            load(gs_sb[:, :], gate_s)
            load(us_sb[:, :], up_s)
            load(wout[:, :, :], w_out, wout_in)

            def load_tokens(q):
                sp.wait_ge(xs_done, PRIMED + 2 * q)
                load(xt[:, :, :], x_t[q], xt_in)

            def load_residual(p):
                sp.wait_ge(x2_done, PRIMED + p)
                load(x1[:, :], x_tok[p], xtok_in)

            def load_context(i, j):
                sp.wait_ge(cs_lo, PRIMED + 2 * i + j)
                load(c2[0:64, :], ctx[2 * i + j], ctx_in)
                load(c2[64:P, :], ctx[2 * i + j], ctx_in)
                sp.wait_ge(rz_step, PRIMED + 4 * i + 2 * j)
                load(ctx1[:, :, 0:64], ctx_t[2 * i + j], ctx1_in)

            def load_gate_and_up(f):
                if f >= WR:
                    sp.wait_ge(gu_done, f - WR + 1)
                load(gu_raw[:, f % WR, 0, :, :], gate_w[f], gu_in[f % WR])
                load(gu_raw[:, f % WR, 1, :, :], up_w[f], gu_in[f % WR])

            def start_ffn():
                sp.wait_ge(scan_done, PRIMED + SCANS * PAIRS)
                sp.wait_ge(x2_out, 16 * (PAIRS - 1))
                for t in range(4):
                    load(x2_in[t], x2_dram[t], f_in[t])
                load_gate_and_up(0)
                load_gate_and_up(1)

            def go_on_with_ffn():
                for t in range(4, TC - 1):
                    sp.wait_ge(f_lo, t - 3)
                    load(x2_in[t % 4], x2_dram[t], f_in[t % 4])

            def move_parts(p):
                sp.wait_ge(s_lo, p + 1)
                load(s_hl[0][64:P, :].bitcast(F32), s_tmp[0:64, :].bitcast(F32), s_in)
                load(s_hl[1][0:64, :].bitcast(F32), s_tmp[64:P, :].bitcast(F32), s_in)

            def turn(i):
                if begins(i):
                    load_tokens(i + 1)
                if scans(i):
                    load_context(i, 0)
                if ends(i):
                    load_residual(i - 1)
                if scans(i):
                    load_context(i, 1)
                if isinstance(i, int) and i == PAIRS:
                    start_ffn()
                if ends(i):
                    move_parts(i - 1)
                if isinstance(i, int) and i == PAIRS:
                    go_on_with_ffn()

            turn(0)
            with sp.Fori(0, (PAIRS - 2) // 2) as r:
                turn(2 * r + 1)
                turn(2 * r + 2)
            turn(PAIRS - 1)
            turn(PAIRS)

            sp.wait_ge(x2_out, 16 * PAIRS)
            sp.wait_ge(att_full, PRIMED + place(att_uses, PAIRS, A_ALL)[1])
            sp.wait_ge(f_full, TC)
            load(ds_sb[:, :], down_s.partition_broadcast(P), dw_in)
            for f in range(FC):
                if f >= WR:
                    load_gate_and_up(f)
                load(dw_raw[:, f, :], down_w[f], dw_in)
            for t in range(TC):
                if t < 2:
                    sp.wait_ge(up_full, HALVES * FC)
                    sp.wait_ge(hid_lo_done, HALVES * FC)
                else:
                    sp.wait_ge(ln3_step, 4 * (t - 2) + 2)
                load(x2_res[:, t % 2, :], x2_dram[t], res_in[t % 2])

        @block.gpsimd
        def _(pool):
            for counter in (xs_done, front_full, *front_free, cs_lo, rz_step, drive_full, scan_done, mix_done,
                            diag_done, y_done, turned_full, eq_done, x2_done, decay_done, kdiag_done, att_full,
                            *att_free, x2_stored):
                pool.sem_inc(counter, PRIMED)
            pool.memset(ident[:, :], 0.0)
            pool.memset(eps_ln[:, :], LN_EPS)
            pool.memset(eps_rms[:, :], RMS_EPS)
            pool.memset(two_eyes[:, :], 0.0)
            pool.memset(pick_raw, 0.0)
            pool.memset(ones_raw, 1.0)
            pool.memset(ek[:, 1, :], 0.0)
            pool.memset(blocks[:, :], 0.0)
            pool.memset(wdt[:, :], 0.0).then_inc(const_step, 1)
            pool.wait_ge(const_step, 1)
            pool.affine_select(out=ident[:, :], in_=ident[:, :], compare_op=ALU.not_equal, fill=1.0, base=0,
                               pattern=[[-1, P]], channel_multiplier=1)
            pool.affine_select(out=pick_raw, in_=pick_raw, compare_op=ALU.not_equal, fill=-1.0, base=0,
                               pattern=[[-2, KC], [-1, 2], [0, 64]], channel_multiplier=1)
            pool.affine_select(out=two_eyes[:, :], in_=two_eyes[:, :], compare_op=ALU.not_equal, fill=1.0, base=0,
                               pattern=[[-1, L]], channel_multiplier=1).then_inc(const_step, 1)
            pool.wait_ge(const_step, 2)
            pool.affine_select(out=two_eyes[:, :], in_=two_eyes[:, :], compare_op=ALU.not_equal, fill=1.0, base=-L,
                               pattern=[[-1, L]], channel_multiplier=1)
            pool.memset(blocks[0:64, 0:64], 1.0)
            pool.memset(tst[:, :], 0.0)
            pool.memset(ssm[:, :], 0.0)
            pool.memset(ssm2[:, :, :, :], 0.0)
            pool.memset(decay[:, :, :, :, :].rearrange("p r n b l -> p (r n b l)"), 0.0)
            pool.memset(qrow[:, :].bitcast(F32), 0.0)
            for b in range(2):
                for j in range(2):
                    pool.memset(mt[b][j][:, :, :], 0.0)
            pool.memset(ctx1[:, :, 64:65], 1.0)
            pool.memset(ucat[:, :, :], 0.0).then_inc(const_step, 1)
            pool.wait_ge(const_step, 3)
            pool.memset(blocks[64:P, 64:P], 1.0)
            pool.memset(ucat[64:65, :, P:P + 1], 1.0).then_inc(const_done, 1)
            pool.wait_ge(const_done, 1)

            def diagonals(q):
                pool.wait_ge(rms_step, 6 * q + 6)
                pool.wait_ge(drive_full, PRIMED + SCANS * q)
                for g in range(NG):
                    for b in range(2):
                        for part, diag in ((b_hi, diag_hi), (b_lo, diag_lo)):
                            pool.tensor_tensor(
                                diag[:, b, g * GN:(g + 1) * GN, :],
                                two_eyes[:, :].unsqueeze(1).to_broadcast([P, GN, L]),
                                part[:, b, g * GN:(g + 1) * GN].unsqueeze(2).to_broadcast([P, GN, L]),
                                ALU.mult).then_inc(diag_done, 1)

            def maxima(i, j):
                pool.wait_ge(km_done, 2 * i + j + 1)
                pool.wait_ge(rz_step, PRIMED + 4 * i + 2 * j)
                pool.tensor_tensor(
                    kdiag[:, :, :], ident[:, :].unsqueeze(1).to_broadcast([P, KC, P]),
                    nkm[:, :].unsqueeze(2).to_broadcast([P, KC, P]), ALU.mult).then_inc(kdiag_done, 1)

            def store_x2(p):
                pool.wait_ge(x2_done, PRIMED + p + 1)
                pool.dma_start(x2_dram[p], u2[:, :]).then_inc(x2_out, 16)
                pool.wait_ge(x2_out, 16 * p + 16)
                pool.sem_inc(x2_stored, 1)

            def turn(i):
                if scans(i):
                    maxima(i, 0)
                    maxima(i, 1)
                if begins(i):
                    diagonals(i + 1)
                if ends(i):
                    store_x2(i - 1)

            turn(-1)
            turn(0)
            with pool.Fori(0, (PAIRS - 2) // 2) as r:
                turn(2 * r + 1)
                turn(2 * r + 2)
            turn(PAIRS - 1)
            turn(PAIRS)

            for f in range(FC):
                for h in range(HALVES):
                    n = f * HALVES + h
                    pool.wait_ge(hid_hi_done, n + 1)
                    pool.tensor_tensor(hid_lo[:, f, h * HALF:(h + 1) * HALF], hid[:, n % 2, :],
                                       hid_hi[:, f, h * HALF:(h + 1) * HALF].bitcast(F32),
                                       ALU.subtract).then_inc(hid_lo_done, 1)
            for t in range(TC):
                pool.wait_ge(y3_done, t + 1)
                pool.dma_start(out[t], y3[:, t % 2, :]).then_inc(out_done[t % 2], 16)
            for k in range(2):
                pool.wait_ge(out_done[k], 16 * TC // 2)

        @block.scalar
        def _(act):
            act.preload_act_table_set("natural_log_exp_and_others")
            act.wait_ge(begin_in, 16 * N_BEGIN)
            act.activation(neg_a[:, :, :], neg_a[:, :, :], ACT.Exp).then_inc(setup_act, 1)
            act.wait_ge(const_done, 1)
            act.dma_start(wdt[0:RK, :], w_dt).then_inc(wdt_in, 16)
            act.wait_ge(setup_vec, 1)

            def inverse_root(to, var, eps, step, before):
                act.activation(to, var, ACT.Ln, bias=eps).then_inc(step, 1)
                act.wait_ge(step, before + 1)
                act.activation(to, to, ACT.Exp, scale=-0.5).then_inc(step, 1)

            def front_filled(i, n):
                bank, before, _ = place(front_uses, i, n)
                act.wait_ge(front_full, PRIMED + before + 1)
                return front[bank], front_free[bank]

            def front_read(i, n):
                bank, _, own = place(front_uses, i, n)
                act.wait_ge(front_free[bank], PRIMED + own + 1)

            def att_filled(i, n):
                bank, before, _ = place(att_uses, i, n)
                act.wait_ge(att_full, PRIMED + before + 1)
                return att[bank], att_free[bank]

            def att_read(i, n):
                bank, _, own = place(att_uses, i, n)
                act.wait_ge(att_free[bank], PRIMED + own + 1)

            def last_tap(i, nxt, h):
                held, _ = front_filled(i, f"conv{h}")
                act.wait_ge(y_done, PRIMED + 2 * (max(i, 0) if isinstance(i, int) else i))
                for c in range(4):
                    d = 4 * h + c
                    tap = act.activation(xs[nxt][:, d, :], held[:, c * P:(c + 1) * P], ACT.Identity,
                                         bias=cb[:, d:d + 1], scale=cw[:, d, TAPS - 1:TAPS])
                tap.then_inc(taps_done, 1)

            def silus(i, nxt):
                for h in range(2):
                    held, free = front_filled(i, f"gate{h}")
                    act.activation(sg[nxt][:, 4 * h:4 * h + 4, :], held[:, :].rearrange("p (c t) -> p c t", c=4),
                                   ACT.Silu).then_inc(free, 1)
                for h in range(2):
                    front_read(i, f"conv{h}")
                    act.activation(xs[nxt][:, 4 * h:4 * h + 4, :], xs[nxt][:, 4 * h:4 * h + 4, :],
                                   ACT.Silu).then_inc(xs_done, 1)
                act.preload_act_table_set("natural_log_exp_and_others")

            def ssm_by_channel(i):
                held, free = front_filled(i, "ssm")
                act.activation(ssm[0:64, :], held[0:64, 0:P], ACT.Copy)
                act.activation(ssm2[0:64, :, :, :], held[0:64, 0:P].rearrange("k (b l) -> k b l", b=2).unsqueeze(2)
                               .to_broadcast([64, 2, 2, L]), ACT.Copy).then_inc(free, 1)

            def ssm_by_token(i):
                held, free = front_filled(i, "token")
                act.activation(tr[:, :, :], held[:, 0:3 * P].rearrange("p (s k) -> p s k", s=3)[:, :, 0:64],
                               ACT.Copy).then_inc(free, 1)
                front_read(i, "token")
                act.activation(sq3[:, :, :], tr[:, :, :], ACT.Square).then_inc(sq3_done, 1)

            def root_rms(i):
                act.wait_ge(rms_step, 6 * (i + 1) + 2)
                inverse_root(rms[:, :], rms[:, :], eps_rms[:, :], rms_root, 2 * (i + 1))

            def dt_input(i):
                held, free = front_filled(i, "dt_in")
                act.activation(tst[0:RK, :], held[0:RK, 0:P], ACT.Copy).then_inc(free, 1)

            def softplus_abs(i, nxt):
                front_read(i, "dt0")
                front_read(i, "dt1")
                act.activation(du[:, :, :], dt[nxt][:, :, :], ACT.Abs).then_inc(log_step, 1)

            def softplus_exp(i):
                act.wait_ge(log_step, 3 * (i + 1) + 1)
                act.activation(du[:, :, :], du[:, :, :], ACT.Exp, scale=-1.0).then_inc(log_step, 1)

            def softplus_log(i):
                act.wait_ge(log_step, 3 * (i + 1) + 2)
                act.activation(du[:, :, :], du[:, :, :], ACT.Ln, bias=1.0).then_inc(log_step, 1)

            def du_high_part(i):
                act.wait_ge(du_done, i + 2)
                if scans(i):
                    act.wait_ge(turned_full, PRIMED + SCANS * i + SCANS - GN)
                act.activation(du_hl[:, :, :, 0, :].bitcast(F32R), du[:, :, :].rearrange("p c (b l) -> p c b l", b=2),
                               ACT.Copy).then_inc(du_hi, 1)

            def du_by_token(i, k):
                held, free = front_filled(i, f"du{k}")
                act.wait_ge(drive_full, PRIMED + SCANS * (i + 1))
                act.activation(du_t[:, :, 2 * k:2 * k + 2, :], held[:, :].rearrange("p (b c d) -> p b c d", b=2, c=2),
                               ACT.Copy).then_inc(free, 1)

            def decays(i, par, u):
                g, d = u // DC, u % DC
                if isinstance(i, int) and SCANS * i + u < DRING:
                    act.wait_ge(const_done, 1)
                else:
                    act.wait_ge(scan_done, PRIMED + SCANS * i + u - DRING + 1)
                if u == 0:
                    act.wait_ge(dt_done, i + 1)
                for n in range(GN):
                    ins = act.activation(
                        decay[:, u % DRING, n, :, 1:L],
                        dt[par][:, d, :].rearrange("p (b l) -> p b l", b=2)[:, :, 1:L],
                        ACT.Exp, scale=neg_a[:, d, g * GN + n:g * GN + n + 1])
                ins.then_inc(decay_done, 1)

            def split_context(i, j):
                act.wait_ge(ctx_in, 64 * i + 32 * j + 32)
                if j == 1:
                    act.wait_ge(att_full, PRIMED + place(att_uses, i, key_use(0, A_CTX))[1])
                act.activation(cs[:, :], c2[:, :], ACT.Copy).then_inc(cs_hi, 1)

            def exp_keys(i, j, c):
                held, free = att_filled(i, key_use(j, A_POS + c))
                act.activation(ek[:, c, :], held[:, :], ACT.Exp).then_inc(free, 1)

            def keys_times_context(i, j):
                held, free = att_filled(i, key_use(j, A_CTX))
                act.activation(gt[0:65, :], held[0:65, :], ACT.Copy).then_inc(free, 1)

            def root_ln1(i):
                p = i - 1
                act.wait_ge(ln1_step, 2 * p + 2)
                inverse_root(rstd[:, :], mv[:, 1:2], eps_ln[:, :], ln1_root, 2 * p)

            def split_x1(i):
                act.wait_ge(x1_done, i)
                act.activation(s_hl[0][0:64, :], x1[0:64, :], ACT.Copy)
                act.activation(s_tmp[64:P, :], x1[64:P, :], ACT.Copy).then_inc(s_hi, 1)

            def query_maxima(i, j):
                held, free = att_filled(i, query_use(j, A_QMAX))
                act.activation(qrow[0:HEADS, :], held[0:HEADS, :], ACT.Copy).then_inc(free, 1)

            def exp_queries(i, j, c):
                held, free = att_filled(i, query_use(j, A_QCH + c))
                act.activation(eq[:, c, :], held[:, :], ACT.Exp).then_inc(free, 1)

            def inverse_sums(i, j, c):
                held, free = att_filled(i, query_use(j, A_SUM + c))
                act.wait_ge(eq_done, PRIMED + 8 * (i - 1) + 4 * j + max(c - 1, 0))
                act.activation(rq[:, c % 2, :], held[:, :], ACT.Ln).then_inc(free, 1)
                att_read(i, query_use(j, A_SUM + c))
                act.activation(rq[:, c % 2, :], rq[:, c % 2, :], ACT.Exp, scale=-1.0).then_inc(rq_done, 1)

            def attention_out(i, j):
                held, free = att_filled(i, query_use(j, A_OUT))
                act.wait_ge(x2_stored, PRIMED + i - 1)
                act.activation(u2[64 * j:64 * j + 64, :], held[64 * j:64 * j + 64, :], ACT.Identity,
                               bias=bo_sb[64 * j:64 * j + 64, :]).then_inc(free, 1)

            def norm_of_out(i):
                att_read(i, query_use(1, A_OUT))
                act.activation(rn[:, :], u2[:, :], ACT.Square).then_inc(usq_done, 1)

            def inverse_norm(i):
                att_read(i, A_NORM)
                act.activation(rn[:, :], rn[:, :], ACT.Ln, scale=NORM_SCALE).then_inc(norm_step, 1)
                act.wait_ge(norm_step, 2 * (i - 1) + 1)
                act.activation(rn[:, :], rn[:, :], ACT.Exp, scale=-0.5).then_inc(norm_step, 1)

            def root_ln2(i):
                act.wait_ge(ln2_step, 4 * (i - 1) + 4)
                inverse_root(rstd2[:, :], mv2[:, 1:2], eps_ln[:, :], ln2_root, 2 * (i - 1))

            def beside(i, par, s):
                nxt = 1 - par
                for j in range(2):
                    if scans(i):
                        if s == SPLIT[j]:
                            split_context(i, j)
                        for h in range(2):
                            if s == POS[j][h]:
                                exp_keys(i, j, 2 * h)
                                exp_keys(i, j, 2 * h + 1)
                        if s == CTX[j][1]:
                            keys_times_context(i, j)
                if ends(i):
                    if s == X1:
                        root_ln1(i)
                    if s == SPLIT_X1:
                        split_x1(i)
                    for j in range(2):
                        if s == QMAX[j]:
                            query_maxima(i, j)
                        for h in range(2):
                            if s == QCH[j][h]:
                                exp_queries(i, j, 2 * h)
                                exp_queries(i, j, 2 * h + 1)
                            if s == SUM[j][h]:
                                inverse_sums(i, j, 2 * h)
                                inverse_sums(i, j, 2 * h + 1)
                        if s == ATTN[j][1]:
                            attention_out(i, j)
                    if s == ATTN[1][1]:
                        norm_of_out(i)
                if begins(i):
                    for h in range(2):
                        if s == TAP[h]:
                            last_tap(i, nxt, h)
                    if s == SILU:
                        silus(i, nxt)
                    if s == SSM:
                        ssm_by_channel(i)
                    if s == TOKEN:
                        ssm_by_token(i)
                    if s == TOKEN + 1:
                        root_rms(i)
                    if s == DT_IN:
                        dt_input(i)
                    if s == ABS:
                        softplus_abs(i, nxt)
                    if s == EXP:
                        softplus_exp(i)
                    if s == LOG:
                        softplus_log(i)
                    if s == DU_HIGH:
                        du_high_part(i)
                    for h in range(2):
                        if s == DU_TOKEN[h]:
                            du_by_token(i, 2 * h)
                            du_by_token(i, 2 * h + 1)
                if ends(i) and s == STEPS - 1:
                    inverse_norm(i)

            def x2_high_part(t):
                act.wait_ge(f_full, t + 1)
                act.activation(x2t_hi[:, :, t * P:(t + 1) * P], x2_bank(t)[:, :].rearrange("p (c t) -> p c t", c=KC),
                               ACT.Copy).then_inc(f_hi, 1)

            def convert(f):
                act.wait_ge(gu_in[f % WR], 32 * (f // WR) + 32)
                if f >= WR:
                    act.wait_ge(up_full, HALVES * (f - WR + 1))
                act.activation(gu[:, f % WR, :, :, :].rearrange("p s c k -> p (s c k)"),
                               gu_raw[:, f % WR, :, :, :].rearrange("p s c k -> p (s c k)"),
                               ACT.Copy).then_inc(gu_done, 1)

            def turn(i, par):
                for s in range(STEPS):
                    if isinstance(i, int) and i == PAIRS:
                        for t in range(TC - 1):
                            if s == X2_TURN[t]:
                                x2_high_part(t)
                        if s in CONVERT:
                            convert(CONVERT.index(s))
                    beside(i, par, s)
                    if scans(i) and s + LEAD < SCANS:
                        decays(i, par, s + LEAD)
                    if begins(i) and s + LEAD >= STEPS:
                        decays(i + 1, 1 - par, s + LEAD - STEPS)
                if ends(i):
                    root_ln2(i)

            turn(-1, 1)
            act.wait_ge(par_in, 16 * N_PAR)
            act.activation(wq_hi[:, :], wq_raw[:, :], ACT.Copy).then_inc(setup_act, 1)
            act.activation(wk_hi[:, :], wk_raw[:, :], ACT.Copy).then_inc(setup_act, 1)
            act.activation(pick[:, :, :], pick_raw, ACT.Copy).then_inc(setup_act, 1)
            act.activation(ones_r[:, :], ones_raw, ACT.Copy).then_inc(setup_act, 1)
            act.wait_ge(setup_pe, 1)
            act.activation(ucat[0:64, :, 0:P], att[0][0:64, :].rearrange("p (c j) -> p c j", c=KC),
                           ACT.Copy).then_inc(setup_act, 1)
            turn(0, 0)
            with act.Fori(0, (PAIRS - 2) // 2) as r:
                turn(2 * r + 1, 1)
                turn(2 * r + 2, 0)
            turn(PAIRS - 1, 1)
            turn(PAIRS, 0)

            x2_high_part(TC - 1)
            for f in range(FC):
                if WR <= f + 1 < FC:
                    convert(f + 1)
                for h in range(HALVES):
                    n = f * HALVES + h
                    act.wait_ge(gate_full, n + 1)
                    if n >= 2:
                        act.wait_ge(hid_done, n - 1)
                    act.activation(gate[:, n % 2, :], drive[n % 2][:, :], ACT.Silu,
                                   scale=gs_sb[:, f:f + 1]).then_inc(gate_done, 1)
                    act.wait_ge(hid_done, n + 1)
                    if n == 0:
                        act.wait_ge(x2_stored, PRIMED + PAIRS)
                    act.activation(hid_hi[:, f, h * HALF:(h + 1) * HALF], hid[:, n % 2, :],
                                   ACT.Copy).then_inc(hid_hi_done, 1)
            act.preload_act_table_set("natural_log_exp_and_others")
            for t in range(TC):
                act.wait_ge(ln3_step, 4 * t + 4)
                inverse_root(rstd3[:, t % 2, :], mv3[:, t % 2, 1:2], eps_ln[:, :], ln3_root, 2 * t)

        @block.vector
        def _(dve):
            dve.wait_ge(begin_in, 16 * N_BEGIN)
            dve.wait_ge(setup_act, 1)
            dve.tensor_scalar(neg_a[:, :, :], neg_a[:, :, :], -1.0, None, ALU.mult).then_inc(setup_vec, 1)

            def front_filled(i, n):
                bank, before, _ = place(front_uses, i, n)
                dve.wait_ge(front_full, PRIMED + before + 1)
                return front[bank], front_free[bank]

            def front_read(i, n):
                bank, _, own = place(front_uses, i, n)
                dve.wait_ge(front_free[bank], PRIMED + own + 1)

            def att_filled(i, n):
                bank, before, _ = place(att_uses, i, n)
                dve.wait_ge(att_full, PRIMED + before + 1)
                return att[bank], att_free[bank]

            def att_read(i, n):
                bank, _, own = place(att_uses, i, n)
                dve.wait_ge(att_free[bank], PRIMED + own + 1)

            def convolve(i, nxt, h, s):
                bank, _, _ = place(front_uses, i, f"conv{h}")
                if s == 1:
                    dve.wait_ge(taps_done, 2 * (i + 1) + h + 1)
                else:
                    dve.wait_ge(conv_step, 4 * (i + 1) + 2 * h + s - 1)
                for c in range(4):
                    d = 4 * h + c
                    new = xs[nxt][:, d, :].rearrange("p (b l) -> p b l", b=2)[:, :, s:L]
                    src = front[bank][:, c * P:(c + 1) * P].rearrange("p (b l) -> p b l", b=2)[:, :, 0:L - s]
                    tap = dve.scalar_tensor_tensor(out=new, in0=src, scalar=cw[:, d, TAPS - 1 - s:TAPS - s],
                                                   in1=new, op0=ALU.mult, op1=ALU.add)
                tap.then_inc(conv_step if s < TAPS - 1 else front_free[bank], 1)

            def ssm_squares(i):
                q = i + 1
                dve.wait_ge(sq3_done, q + 1)
                dve.tensor_reduce(rms[:, 0:1], sq3[:, 0, 0:RK], AX_X, ALU.add)
                dve.tensor_reduce(rms[:, 1:2], sq3[:, 0, RK + NS:64], AX_X, ALU.add)
                dve.tensor_reduce(rms[:, 2:4], sq3[:, 1:3, RK:RK + NS], AX_X, ALU.add).then_inc(rms_step, 1)
                dve.wait_ge(rms_step, 6 * q + 1)
                dve.tensor_scalar(rms[:, 0:1], rms[:, 0:1], 1.0 / RK, None, ALU.mult)
                dve.tensor_scalar(rms[:, 1:4], rms[:, 1:4], 1.0 / NS, None, ALU.mult).then_inc(rms_step, 1)

            def ssm_norms(i, nxt):
                q = i + 1
                dve.wait_ge(rms_root, 2 * q + 2)
                dve.tensor_scalar(tsn[:, :], tr[:, 0, 0:RK], rms[:, 0:1], None, ALU.mult).then_inc(rms_step, 1)
                dve.tensor_scalar(c_col[nxt][:, :], tr[:, 0, RK + NS:64], rms[:, 1:2], None, ALU.mult)
                for b in range(2):
                    ins = dve.tensor_scalar(b_nrm[:, b, :], tr[:, 1 + b, RK:RK + NS], rms[:, 2 + b:3 + b], None,
                                            ALU.mult)
                ins.then_inc(rms_step, 1)
                dve.wait_ge(rms_step, 6 * q + 4)
                dve.wait_ge(diag_done, PRIMED + 16 * q)
                dve.tensor_copy(b_hi[:, :, :].bitcast(F32R), b_nrm[:, :, :]).then_inc(rms_step, 1)
                dve.wait_ge(rms_step, 6 * q + 5)
                dve.tensor_tensor(b_lo[:, :, :], b_nrm[:, :, :], b_hi[:, :, :], ALU.subtract).then_inc(rms_step, 1)

            def dt_before_softplus(i, nxt):
                for h in range(2):
                    held, free = front_filled(i, f"dt{h}")
                    dve.tensor_tensor(dt[nxt][:, 4 * h:4 * h + 4, :], held[:, :].rearrange("p (c t) -> p c t", c=4),
                                      bdt[:, 4 * h:4 * h + 4].unsqueeze(2).to_broadcast([P, 4, P]),
                                      ALU.add).then_inc(free, 1)

            def dt_whole(i, nxt):
                dve.wait_ge(log_step, 3 * (i + 1) + 3)
                z = dt[nxt][:, :, :].rearrange("p c t -> p (c t)")
                dve.scalar_tensor_tensor(out=z, in0=z, scalar=0.0, in1=du[:, :, :].rearrange("p c t -> p (c t)"),
                                         op0=ALU.max, op1=ALU.add).then_inc(dt_done, 1)

            def dt_times_x(i, nxt):
                dve.wait_ge(dt_done, i + 2)
                dve.wait_ge(xs_done, PRIMED + 2 * (i + 1) + 2)
                dve.tensor_tensor(du[:, :, :], dt[nxt][:, :, :], xs[nxt][:, :, :], ALU.mult).then_inc(du_done, 1)

            def du_low_part(i):
                dve.wait_ge(du_hi, i + 2)
                dve.tensor_tensor(du_hl[:, :, :, 1, :], du[:, :, :].rearrange("p c (b l) -> p c b l", b=2),
                                  du_hl[:, :, :, 0, :], ALU.subtract).then_inc(du_lo, 1)

            def scan(i, u):
                dve.wait_ge(decay_done, PRIMED + SCANS * i + u + 1)
                dve.wait_ge(drive_full, PRIMED + SCANS * i + u + 1)
                dve.wait_ge(turned_full, PRIMED + SCANS * i + max(GN * (u // GC - 1), 0))
                dve.tensor_tensor_scan(
                    state[:, u % RING, :, :].rearrange("p n t -> p (n t)"),
                    decay[:, u % DRING, :, :, :].rearrange("p n b l -> p (n b l)"),
                    drive[u % 2][:, :], 0.0, ALU.mult, ALU.add).then_inc(scan_done, 1)

            def mix(i, par, v):
                item, c = v // GN, v % GN
                n, part = (item // NGC) * GN + c, item % NGC
                to = acc[:, part * 512:(part + 1) * 512]
                dve.wait_ge(turned_full, PRIMED + SCANS * i + v + 1)
                dve.wait_ge(mix_done, PRIMED + SCANS * i + v)
                if v == 0 and ends(i):
                    dve.wait_ge(front_full, PRIMED + place(front_uses, i - 1, "sum1")[1] + 1)
                if n == 0:
                    ins = dve.tensor_scalar(to, turned[v % 2][:, :], c_col[par][:, n:n + 1], None, ALU.mult)
                else:
                    ins = dve.scalar_tensor_tensor(out=to, in0=turned[v % 2][:, :], scalar=c_col[par][:, n:n + 1],
                                                   in1=to, op0=ALU.mult, op1=ALU.add)
                ins.then_inc(mix_done, 1)

            def context_low_part(i, j):
                dve.wait_ge(cs_hi, 2 * i + j + 1)
                dve.tensor_tensor(cs[64:P, :], c2[64:P, :], cs[64:P, :].bitcast(F32), ALU.subtract).then_inc(cs_lo, 1)

            def key_maxima(i, j, c):
                held, free = att_filled(i, key_use(j, A_KEY + c))
                dve.tensor_reduce(km[:, c:c + 1], held[:, :], AX_X, ALU.max).then_inc(free, 1)
                if c == KC - 1:
                    att_read(i, key_use(j, A_KEY + c))
                    dve.wait_ge(kdiag_done, PRIMED + 2 * i + j)
                    dve.tensor_scalar(nkm[:, :], km[:, :], -1.0, None, ALU.mult).then_inc(km_done, 1)

            def context_matrix(i, par, j, k):
                held, free = att_filled(i, key_use(j, A_MAT + k))
                both = held[:, 0:2 * (P + 1)].rearrange("p (c x) -> p c x", c=2)
                dve.reciprocal(rz[:, 2 * k:2 * k + 2], both[:, :, P:P + 1].squeeze(2)).then_inc(rz_step, 1)
                dve.wait_ge(rz_step, PRIMED + 4 * i + 2 * j + k + 1)
                for r in (0, 64):
                    ins = dve.scalar_tensor_tensor(
                        out=mt[par][j][r:r + 64, 2 * k:2 * k + 2, 64 * j:64 * j + 64], in0=both[r:r + 64, :, r:r + 64],
                        scalar=DH ** -0.5, in1=rz[r:r + 64, 2 * k:2 * k + 2].unsqueeze(2).to_broadcast([64, 2, 64]),
                        op0=ALU.mult, op1=ALU.mult)
                ins.then_inc(free, 1)

            def gated_sum(i, par, h):
                held, free = front_filled(i, f"sum{h}")
                for c in range(4):
                    d = 4 * h + c
                    ins = dve.scalar_tensor_tensor(out=y[:, d, :], in0=xs[par][:, d, :], scalar=dsk[:, d:d + 1],
                                                   in1=held[:, c * P:(c + 1) * P], op0=ALU.mult, op1=ALU.add)
                ins.then_inc(free, 1)
                front_read(i, f"sum{h}")
                dve.tensor_tensor(y[:, 4 * h:4 * h + 4, :], y[:, 4 * h:4 * h + 4, :], sg[par][:, 4 * h:4 * h + 4, :],
                                  ALU.mult).then_inc(y_done, 1)

            def residual_x1(i):
                held, free = front_filled(i, "out")
                dve.wait_ge(xtok_in, 16 * i)
                dve.tensor_tensor(x1[:, :], held[:, :], x1[:, :], ALU.add).then_inc(free, 1)
                front_read(i, "out")
                dve.bn_stats(bn[:, :], x1[:, :]).then_inc(ln1_step, 1)
                dve.drain()
                dve.bn_aggr(mv[:, :], bn[:, :]).then_inc(ln1_step, 1)

            def layernorm_x1(i):
                dve.wait_ge(ln1_root, 2 * (i - 1) + 2)
                dve.tensor_scalar(x1[:, :], x1[:, :], mv[:, 0:1], rstd[:, 0:1],
                                  ALU.subtract, ALU.mult).then_inc(x1_done, 1)

            def x1_low_part(i):
                dve.wait_ge(s_hi, i)
                dve.tensor_tensor(s_tmp[0:64, :], x1[0:64, :], s_hl[0][0:64, :].bitcast(F32), ALU.subtract)
                dve.tensor_tensor(s_hl[1][64:P, :], x1[64:P, :], s_tmp[64:P, :].bitcast(F32),
                                  ALU.subtract).then_inc(s_lo, 1)

            def query_maxima(i, j, c):
                held, free = att_filled(i, query_use(j, A_QPOS + c))
                dve.tensor_reduce(qm[:, c, :], held[:, :].rearrange("p (h d) -> p h d", h=HEADS),
                                  AX_X, ALU.max).then_inc(free, 1)

            def softmax_queries(i, j, c):
                dve.wait_ge(rq_done, 8 * (i - 1) + 4 * j + c + 1)
                dve.tensor_tensor(eq[:, c, :], eq[:, c, :], rq[:, c % 2, :], ALU.mult).then_inc(eq_done, 1)

            def bound_norm(i):
                held, free = att_filled(i, A_NORM)
                dve.tensor_scalar(rn[:, :], held[:, :], 1e-24, None, ALU.max).then_inc(free, 1)

            def residual_x2(i):
                p = i - 1
                dve.wait_ge(norm_step, 2 * p + 2)
                dve.scalar_tensor_tensor(out=u2[:, :], in0=u2[:, :], scalar=g8[:, 0:1], in1=rn[:, :],
                                         op0=ALU.mult, op1=ALU.mult).then_inc(ln2_step, 1)
                dve.wait_ge(ln2_step, 4 * p + 1)
                dve.tensor_tensor(u2[:, :], u2[:, :], x1[:, :], ALU.add).then_inc(ln2_step, 1)
                dve.wait_ge(ln2_step, 4 * p + 2)
                dve.bn_stats(bn2[:, :], u2[:, :]).then_inc(ln2_step, 1)
                dve.drain()
                dve.bn_aggr(mv2[:, :], bn2[:, :]).then_inc(ln2_step, 1)

            def layernorm_x2(i):
                dve.wait_ge(ln2_root, 2 * (i - 1) + 2)
                dve.tensor_scalar(u2[:, :], u2[:, :], mv2[:, 0:1], rstd2[:, 0:1],
                                  ALU.subtract, ALU.mult).then_inc(x2_done, 1)

            def beside(i, par, s):
                nxt = 1 - par
                if begins(i):
                    for h in range(2):
                        for b in range(1, TAPS):
                            if s == CONV[h][b - 1]:
                                convolve(i, nxt, h, b)
                if scans(i):
                    for j in range(2):
                        if s == SPLIT[j]:
                            context_low_part(i, j)
                        for h in range(2):
                            if s == KEYS[j][h]:
                                key_maxima(i, j, 2 * h)
                                key_maxima(i, j, 2 * h + 1)
                        if s == MAT[j]:
                            context_matrix(i, par, j, 0)
                            context_matrix(i, par, j, 1)
                if ends(i):
                    if s == RESIDUAL:
                        residual_x1(i)
                    if s == X1:
                        layernorm_x1(i)
                    if s == SPLIT_X1:
                        x1_low_part(i)
                    for j in range(2):
                        for h in range(2):
                            if s == QPOS[j][h]:
                                query_maxima(i, j, 2 * h)
                                query_maxima(i, j, 2 * h + 1)
                            if s == SUM[j][h]:
                                softmax_queries(i, j, 2 * h)
                                softmax_queries(i, j, 2 * h + 1)
                if begins(i):
                    if s == TOKEN:
                        ssm_squares(i)
                    if s == TOKEN + 1:
                        ssm_norms(i, nxt)
                    if s == DT_PROJ:
                        dt_before_softplus(i, nxt)
                    if s == LOG:
                        dt_whole(i, nxt)
                    if s == LOG + 1:
                        dt_times_x(i, nxt)
                    if s == DU_HIGH:
                        du_low_part(i)

            def x2_low_part(t):
                dve.wait_ge(f_hi, t + 1)
                dve.tensor_tensor(x2t_lo[:, :, t * P:(t + 1) * P], x2_bank(t)[:, :].rearrange("p (c t) -> p c t", c=KC),
                                  x2t_hi[:, :, t * P:(t + 1) * P].bitcast(F32), ALU.subtract).then_inc(f_lo, 1)

            def turn(i, par):
                for s in range(STEPS):
                    if isinstance(i, int) and i == PAIRS:
                        for t in range(TC - 1):
                            if s == X2_TURN[t] + 1:
                                x2_low_part(t)
                    if scans(i) and AHEAD <= s < SCANS:
                        scan(i, s)
                    if s > 0:
                        beside(i, par, s - 1)
                    if scans(i) and s >= GC:
                        mix(i, par, s - GC)
                if ends(i):
                    bound_norm(i)
                if begins(i):
                    scan(i + 1, 0)
                if scans(i):
                    gated_sum(i, par, 0)
                if ends(i):
                    residual_x2(i)
                if begins(i):
                    scan(i + 1, 1)
                if scans(i):
                    gated_sum(i, par, 1)
                if ends(i):
                    layernorm_x2(i)

            turn(-1, 1)
            dve.wait_ge(par_in, 16 * N_PAR)
            dve.wait_ge(setup_act, 3)
            dve.tensor_tensor(wq_lo[:, :], wq_raw[:, :], wq_hi[:, :].bitcast(F32), ALU.subtract)
            dve.tensor_tensor(wk_lo[:, :], wk_raw[:, :], wk_hi[:, :].bitcast(F32), ALU.subtract)
            dve.tensor_scalar(g8[:, :], g8[:, :], float(np.sqrt(DH) * np.sqrt(NORM_SCALE)), None,
                              ALU.mult).then_inc(setup_vec, 1)
            turn(0, 0)
            with dve.Fori(0, (PAIRS - 2) // 2) as r:
                turn(2 * r + 1, 1)
                turn(2 * r + 2, 0)
            turn(PAIRS - 1, 1)
            turn(PAIRS, 0)

            x2_low_part(TC - 1)
            for n in range(FC * HALVES):
                f = n // HALVES
                dve.wait_ge(gate_done, n + 1)
                dve.wait_ge(up_full, n + 1)
                if n >= 2:
                    dve.wait_ge(hid_lo_done, n - 1)
                dve.scalar_tensor_tensor(out=hid[:, n % 2, :], in0=turned[n % 2][:, :], scalar=us_sb[:, f:f + 1],
                                         in1=gate[:, n % 2, :], op0=ALU.mult, op1=ALU.mult).then_inc(hid_done, 1)
            dve.wait_ge(dw_in, 16 * (FC + 1))
            for f in range(FC):
                dve.tensor_copy(dw[:, f, :], dw_raw[:, f, :]).then_inc(dw_done, 1)
            for t in range(TC):
                k = t % 2
                dve.wait_ge(down_full, t + 1)
                dve.tensor_tensor(r3[:, k, :], att[k][:, :], ds_sb[:, :], ALU.mult).then_inc(ln3_step, 1)
                dve.wait_ge(ln3_step, 4 * t + 1)
                dve.wait_ge(res_in[k], 16 * (t // 2 + 1))
                dve.tensor_tensor(r3[:, k, :], r3[:, k, :], x2_res[:, k, :], ALU.add).then_inc(ln3_step, 1)
                dve.wait_ge(ln3_step, 4 * t + 2)
                dve.bn_stats(bn3[:, k, :], r3[:, k, :]).then_inc(ln3_step, 1)
                dve.wait_ge(ln3_step, 4 * t + 3)
                dve.bn_aggr(mv3[:, k, :], bn3[:, k, :]).then_inc(ln3_step, 1)
                dve.wait_ge(ln3_root, 2 * t + 2)
                if t >= 2:
                    dve.wait_ge(out_done[k], 16 * (t // 2))
                dve.tensor_scalar(y3[:, k, :], r3[:, k, :], mv3[:, k, 0:1], rstd3[:, k, 0:1],
                                  ALU.subtract, ALU.mult).then_inc(y3_done, 1)

        @block.tensor
        def _(pe):
            def fill_front(i, n):
                bank, _, own = place(front_uses, i, n)
                pe.wait_ge(front_free[bank], PRIMED + own)
                return front[bank]

            def front_read(i, n):
                bank, _, own = place(front_uses, i, n)
                pe.wait_ge(front_free[bank], PRIMED + own + 1)

            def fill(i, n):
                bank, _, own = place(att_uses, i, n)
                pe.wait_ge(att_free[bank], PRIMED + own)
                return att[bank]

            def att_read(i, n):
                bank, _, own = place(att_uses, i, n)
                pe.wait_ge(att_free[bank], PRIMED + own + 1)

            def project(i, h, half):
                name = ("conv0", "conv1", "gate0", "gate1")[h]
                if half == 0:
                    fill_front(i, name)
                    pe.wait_ge(xt_in, 16 * (i + 1) + 16)
                if isinstance(i, int) and i == -1:
                    pe.wait_ge(win_in[h], 16)
                to = front[place(front_uses, i, name)[0]]
                for c in range(2 * half, 2 * half + 2):
                    for k in range(KC):
                        mm = pe.matmul(to[:, c * P:(c + 1) * P], win[:, k, (4 * h + c) * P:(4 * h + c + 1) * P],
                                       xt[:, k, :], start=(k == 0), stop=(k == KC - 1))
                if half == 1:
                    mm.then_inc(front_full, 1)

            def ssm_by_channel(i, nxt):
                to = fill_front(i, "ssm")
                pe.wait_ge(xs_done, PRIMED + 2 * (i + 1) + 2)
                if isinstance(i, int) and i == -1:
                    pe.wait_ge(begin_in, 16 * N_BEGIN)
                    pe.wait_ge(const_done, 1)
                for d in range(DC):
                    mm = pe.matmul(to[0:64, 0:P], wx[:, d, :], xs[nxt][:, d, :], start=(d == 0), stop=(d == DC - 1))
                mm.then_inc(front_full, 1)

            def ssm_by_token(i):
                to = fill_front(i, "token")
                front_read(i, "ssm")
                pe.transpose(to[:, 0:P], ssm[:, :], ident[:, :])
                for b in range(2):
                    mm = pe.transpose(to[:, P * (b + 1):P * (b + 2)],
                                      ssm2[:, b, :, :].rearrange("k s l -> k (s l)"), ident[:, :])
                mm.then_inc(front_full, 1)

            def dt_input(i):
                to = fill_front(i, "dt_in")
                pe.wait_ge(rms_step, 6 * (i + 1) + 3)
                pe.transpose(to[0:RK, 0:P], tsn[:, :], ident[:, :]).then_inc(front_full, 1)

            def dt_projection(i):
                front_read(i, "dt_in")
                if isinstance(i, int) and i == -1:
                    pe.wait_ge(wdt_in, 16)
                for h in range(2):
                    to = fill_front(i, f"dt{h}")
                    for c in range(4):
                        d = 4 * h + c
                        mm = pe.matmul(to[:, c * P:(c + 1) * P], wdt[:, d * P:(d + 1) * P], tst[:, :],
                                       start=True, stop=True)
                    mm.then_inc(front_full, 1)

            def du_by_token(i, k):
                to = fill_front(i, f"du{k}")
                pe.wait_ge(du_lo, i + 2)
                for b in range(2):
                    for c in range(2):
                        mm = pe.transpose(to[:, (2 * b + c) * P:(2 * b + c + 1) * P],
                                          du_hl[:, 2 * k + c, b, :, :].rearrange("p s l -> p (s l)"), ident[:, :])
                mm.then_inc(front_full, 1)

            def drives(i, u):
                g, d = u // DC, u % DC
                if u == 0:
                    front_read(i - 1, "du2")
                    front_read(i - 1, "du3")
                pe.wait_ge(scan_done, PRIMED + SCANS * i + max(u - 1, 0))
                pe.wait_ge(diag_done, PRIMED + 16 * i + 4 * (g + 1))
                to = drive[u % 2][:, :].rearrange("p (n b l) -> p n b l", n=GN, b=2)
                for b in range(2):
                    pe.matmul(to[:, :, b, :], du_t[:, b, d, :], diag_hi[:, b, g * GN:(g + 1) * GN, :],
                              start=True, stop=False)
                    mm = pe.matmul(to[:, :, b, :], du_t[:, b, d, :], diag_lo[:, b, g * GN:(g + 1) * GN, :],
                                   start=False, stop=True)
                mm.then_inc(drive_full, 1)

            def states_by_token(i, v):
                item, c = v // GN, v % GN
                pe.wait_ge(scan_done, PRIMED + SCANS * i + GC * (item + 1))
                pe.wait_ge(mix_done, PRIMED + SCANS * i + max(v - 1, 0))
                for k in range(GC):
                    mm = pe.transpose(turned[v % 2][:, k * P:(k + 1) * P],
                                      state[:, (GC * item + k) % RING, c, :], ident[:, :])
                mm.then_inc(turned_full, 1)

            def keys_by_channel(i, j, c):
                to = fill(i, key_use(j, A_KEY + c))
                pe.wait_ge(cs_lo, PRIMED + 2 * i + j + 1)
                pe.matmul(to[:, :], wk_hi[:, c * P:(c + 1) * P], cs[:, :], start=True, stop=True).then_inc(att_full, 1)

            def keys_by_position(i, j, c):
                to = fill(i, key_use(j, A_POS + c))
                pe.matmul(to[:, :], cs[:, c * P:(c + 1) * P], wk_hi[:, :], start=True, stop=False)
                pe.matmul(to[:, :], cs[:, c * P:(c + 1) * P], wk_lo[:, :], start=False, stop=False)
                pe.wait_ge(kdiag_done, PRIMED + 2 * i + j + 1)
                pe.matmul(to[:, :], ones_r[:, :], kdiag[:, :, :].rearrange("p c k -> p (c k)"),
                          start=False, stop=True).then_inc(att_full, 1)

            def keys_times_context(i, j, c):
                n = key_use(j, A_CTX)
                if c == 0:
                    fill(i, n)
                    att_read(i, key_use(j, A_POS + 2))
                    att_read(i, key_use(j, A_POS + 3))
                    pe.wait_ge(ctx1_in, 32 * i + 16 * j + 16)
                mm = pe.matmul(att[n % 2][0:65, :], ctx1[:, c, :], ek[:, c, :], start=(c == 0), stop=(c == KC - 1))
                if c == KC - 1:
                    mm.then_inc(att_full, 1)

            def context_matrix(i, j, k):
                att_read(i, key_use(j, A_CTX))
                to = fill(i, key_use(j, A_MAT + k))
                for c in range(2):
                    h = 2 * k + c
                    mm = pe.matmul(to[:, c * (P + 1):(c + 1) * (P + 1)], gt[0:65, h * P:(h + 1) * P],
                                   ucat[0:65, h, :], start=True, stop=True)
                mm.then_inc(att_full, 1)

            def sums_by_channel(i):
                pe.wait_ge(mix_done, PRIMED + SCANS * (i + 1))
                for h in range(2):
                    to = fill_front(i, f"sum{h}")
                    for c in range(4):
                        d = 4 * h + c
                        mm = pe.transpose(to[:, c * P:(c + 1) * P], acc[:, d * P:(d + 1) * P], ident[:, :])
                    mm.then_inc(front_full, 1)

            def project_out(i, quarter):
                to = front[place(front_uses, i, "out")[0]]
                if quarter == 0:
                    fill_front(i, "out")
                    pe.wait_ge(y_done, PRIMED + 2 * i)
                for d in range(2 * quarter, 2 * quarter + 2):
                    mm = pe.matmul(to[:, :], y[:, d, :], wout[:, d, :], start=(d == 0), stop=(d == DC - 1))
                if quarter == 3:
                    mm.then_inc(front_full, 1)

            def queries_by_position(i, j, c):
                to = fill(i, query_use(j, A_QPOS + c))
                pe.wait_ge(s_in, 32 * i)
                pe.matmul(to[:, :], s_hl[j][:, c * P:(c + 1) * P], wq_hi[:, :],
                          start=True, stop=True).then_inc(att_full, 1)

            def query_maxima(i, j):
                to = fill(i, query_use(j, A_QMAX))
                att_read(i, query_use(j, A_QPOS + 3))
                for c in range(KC):
                    mm = pe.transpose(to[0:HEADS, c * P:(c + 1) * P], qm[:, c, :], ident[:, :])
                mm.then_inc(att_full, 1)

            def queries_by_channel(i, j, c):
                to = fill(i, query_use(j, A_QCH + c))
                pe.matmul(to[:, :], wq_hi[:, c * P:(c + 1) * P], s_hl[j][:, :], start=True, stop=False)
                pe.matmul(to[:, :], wq_lo[:, c * P:(c + 1) * P], s_hl[j][:, :], start=False, stop=False)
                att_read(i, query_use(j, A_QMAX))
                pe.matmul(to[:, :], pick[:, c, :], qrow[:, :], start=False, stop=True).then_inc(att_full, 1)

            def query_sums(i, j, c):
                to = fill(i, query_use(j, A_SUM + c))
                att_read(i, query_use(j, A_QCH + c))
                pe.matmul(to[:, :], blocks[:, :], eq[:, c, :], start=True, stop=True).then_inc(att_full, 1)

            def attention_out(i, prv, j, c):
                n = query_use(j, A_OUT)
                if c == 0:
                    fill(i, n)
                pe.wait_ge(eq_done, PRIMED + 8 * (i - 1) + 4 * j + c + 1)
                mm = pe.matmul(att[n % 2][:, :], mt[prv][j][:, c, :], eq[:, c, :], start=(c == 0), stop=(c == KC - 1))
                if c == KC - 1:
                    mm.then_inc(att_full, 1)

            def norm_of_out(i):
                to = fill(i, A_NORM)
                pe.wait_ge(usq_done, i)
                pe.matmul(to[:, :], blocks[:, :], rn[:, :], start=True, stop=True).then_inc(att_full, 1)

            def beside(i, par, s):
                nxt = 1 - par
                if ends(i):
                    for q in range(4):
                        if s == OUT[q]:
                            project_out(i, q)
                if begins(i):
                    for h in range(4):
                        for half in range(2):
                            if s == PROJECT[2 * h + half]:
                                project(i, h, half)
                if scans(i):
                    for j in range(2):
                        for h in range(2):
                            if s == KEYS[j][h]:
                                keys_by_channel(i, j, 2 * h)
                                keys_by_channel(i, j, 2 * h + 1)
                            if s == POS[j][h]:
                                keys_by_position(i, j, 2 * h)
                                keys_by_position(i, j, 2 * h + 1)
                            if s == CTX[j][h]:
                                keys_times_context(i, j, 2 * h)
                                keys_times_context(i, j, 2 * h + 1)
                        if s == MAT[j]:
                            context_matrix(i, j, 0)
                            context_matrix(i, j, 1)
                if begins(i):
                    if s == SSM:
                        ssm_by_channel(i, nxt)
                    if s == TOKEN:
                        ssm_by_token(i)
                    if s == DT_IN:
                        dt_input(i)
                    if s == DT_PROJ:
                        dt_projection(i)
                if ends(i):
                    for j in range(2):
                        for h in range(2):
                            if s == QPOS[j][h]:
                                queries_by_position(i, j, 2 * h)
                                queries_by_position(i, j, 2 * h + 1)
                        if s == QMAX[j]:
                            query_maxima(i, j)
                        for h in range(2):
                            if s == QCH[j][h]:
                                queries_by_channel(i, j, 2 * h)
                                queries_by_channel(i, j, 2 * h + 1)
                            if s == SUM[j][h]:
                                query_sums(i, j, 2 * h)
                                query_sums(i, j, 2 * h + 1)
                            if s == ATTN[j][h]:
                                attention_out(i, nxt, j, 2 * h)
                                attention_out(i, nxt, j, 2 * h + 1)
                if begins(i):
                    for h in range(2):
                        if s == DU_TOKEN[h]:
                            du_by_token(i, 2 * h)
                            du_by_token(i, 2 * h + 1)
                if ends(i) and s == STEPS - 1:
                    norm_of_out(i)
                if scans(i) and s == STEPS - 1:
                    sums_by_channel(i)

            def x2_by_channel(t, source):
                if t == TC - 1:
                    pe.wait_ge(x2_done, PRIMED + PAIRS)
                else:
                    pe.wait_ge(f_in[t % 4], 16 * (t // 4 + 1))
                if t >= 2:
                    pe.wait_ge(f_lo, t - 1)
                for c in range(KC):
                    mm = pe.transpose(x2_bank(t)[:, c * P:(c + 1) * P], source[:, c * P:(c + 1) * P], ident[:, :])
                mm.then_inc(f_full, 1)

            def turn(i, par):
                for s in range(STEPS):
                    if isinstance(i, int) and i == PAIRS:
                        for t in range(TC - 1):
                            if s == X2_TURN[t]:
                                x2_by_channel(t, x2_in[t % 4])
                    if scans(i) and AHEAD <= s + 1 < SCANS:
                        drives(i, s + 1)
                    if begins(i) and s == STEPS - 1:
                        drives(i + 1, 0)
                    if scans(i) and s >= GC:
                        states_by_token(i, s - GC)
                    beside(i, par, s)
                if begins(i):
                    drives(i + 1, 1)

            turn(-1, 1)
            pe.wait_ge(par_in, 16 * N_PAR)
            for c in range(KC):
                mm = pe.matmul(att[0][0:64, c * P:(c + 1) * P], wv_raw[:, c, :], wo_raw[:, c, :], start=True, stop=True)
            mm.then_inc(setup_pe, 1)
            pe.wait_ge(setup_act, 6)
            pe.wait_ge(setup_vec, 2)
            pe.wait_ge(wout_in, 16)
            turn(0, 0)
            with pe.Fori(0, (PAIRS - 2) // 2) as r:
                turn(2 * r + 1, 1)
                turn(2 * r + 2, 0)
            turn(PAIRS - 1, 1)
            turn(PAIRS, 0)

            pe.wait_ge(f_lo, TC - 1)
            for f in range(FC):
                pe.wait_ge(gu_done, f + 1)
                for h in range(HALVES):
                    n = f * HALVES + h
                    if n == 1:
                        x2_by_channel(TC - 1, u2)
                        pe.wait_ge(f_lo, TC)
                    for s, banks, free, full in ((0, drive, gate_done, gate_full), (1, turned, hid_done, up_full)):
                        if n >= 2:
                            pe.wait_ge(free, n - 1)
                        for k in range(KC):
                            for part in (x2t_hi, x2t_lo):
                                mm = pe.matmul(banks[n % 2][:, :], gu[:, f % WR, s, k, :],
                                               part[:, k, h * HALF:(h + 1) * HALF],
                                               start=(k == 0 and part is x2t_hi), stop=(k == KC - 1 and part is x2t_lo))
                        mm.then_inc(full, 1)
            for t in range(TC):
                if t in (0, TC // HALVES):
                    pe.wait_ge(hid_hi_done, HALVES * (FC - 1) + t * HALVES // TC + 1)
                    pe.wait_ge(hid_lo_done, HALVES * (FC - 1) + t * HALVES // TC + 1)
                if t >= 2:
                    pe.wait_ge(ln3_step, 4 * (t - 2) + 1)
                for f in range(FC):
                    if t == 0:
                        pe.wait_ge(dw_done, f + 1)
                    for part in (hid_hi, hid_lo):
                        mm = pe.matmul(att[t % 2][:, :], part[:, f, t * P:(t + 1) * P], dw[:, f, :],
                                       start=(f == 0 and part is hid_hi), stop=(f == FC - 1 and part is hid_lo))
                mm.then_inc(down_full, 1)


def lay_out(a):
    c = np.ascontiguousarray
    x, ctx = a["x"].reshape(TOK, H), a["ctx_4096"]

    def by_part(w):
        return c(w.reshape(-1, P, w.shape[1]).transpose(1, 0, 2))

    def col(v):
        return c(v.reshape(-1, P).T)

    def blocks_t(w):
        return c(w.reshape(FC, P, KC, P).transpose(0, 3, 2, 1))

    return {
        "x_tok": c(x.reshape(PAIRS, P, H)),
        "x_t": c(x.reshape(PAIRS, P, KC, P).transpose(0, 3, 2, 1)),
        "ctx": c(ctx),
        "ctx_t": c(ctx.reshape(B, L, KC, P).transpose(0, 3, 2, 1)),
        "w_in": c(a["L0_attn_W_in"].reshape(4, 512, KC, P).transpose(0, 3, 2, 1)),
        "conv_w": by_part(a["L0_attn_conv_w"]),
        "conv_b": col(a["L0_attn_conv_b"]),
        "w_x": by_part(a["L0_attn_W_x"].T),
        "w_dt": c(a["L0_attn_W_dt"].T),
        "b_dt": col(a["L0_attn_b_dt"]),
        "a_log": by_part(a["L0_attn_A_log"]),
        "d_skip": col(a["L0_attn_D"]),
        "w_out": by_part(a["L0_attn_W_out"].T),
        "wq": c(a["L0_xattn_Wq"].T),
        "wk": c(a["L0_xattn_Wk"].T),
        "wv": by_part(a["L0_xattn_Wv"]),
        "wo": by_part(a["L0_xattn_Wo"].T),
        "bo": c(a["L0_xattn_bo"].reshape(64, 1)),
        "gain": c(a["L0_xattn_g"].reshape(64, 1)),
        "gate_w": blocks_t(a["L0_ffn_gate_t"]),
        "up_w": blocks_t(a["L0_ffn_up_t"]),
        "down_w": c(a["L0_ffn_down_t"].T.reshape(FC, P, H)),
        "gate_s": col(a["L0_ffn_gate_s"]),
        "up_s": col(a["L0_ffn_up_s"]),
        "down_s": c(a["L0_ffn_down_s"]),
    }


def kernel(**inputs):
    import concourse.bacc as bacc
    from concourse.bass_utils import run_bass_kernel_spmd

    arrays = lay_out({k: np.asarray(v) for k, v in inputs.items()})
    nc = bacc.Bacc("TRN2", target_bir_lowering=False, num_devices=1)
    args = [nc.dram_tensor(f"in_{k}", v.shape, mybir.dt.from_np(v.dtype), kind="ExternalInput").ap()
            for k, v in arrays.items()]
    out = nc.dram_tensor("out", (TC, P, H), F32, kind="ExternalOutput").ap()
    decoder_kernel(nc, *args, out)
    r = run_bass_kernel_spmd(nc, [{f"in_{k}": v for k, v in arrays.items()}], core_ids=[0])
    return r.results[0]["out"].reshape(B, L, H)
```
